# Optimizing a Trainium2 kernel written in Bass

```python
import numpy as np
import jax
import jax.numpy as jnp

def _softmax(x, axis=-1):
    return jax.nn.softmax(x, axis=axis)

def _gelu(x):
    return jax.nn.gelu(x, approximate=True)

def _silu(x):
    return jax.nn.silu(x)

def _sigmoid(x):
    return jax.nn.sigmoid(x)

def _layernorm(x, axis=-1, eps=1e-05):
    m = jnp.mean(x, axis=axis, keepdims=True)
    v = jnp.var(x, axis=axis, keepdims=True)
    return (x - m) / jnp.sqrt(v + eps)

def _scatter_add(tgt, idx, src, axis=0):
    return tgt.at[idx].add(src)

def _segment_sum(src, seg, n):
    return jax.ops.segment_sum(src, seg, n)
kernel_name = 'mk_hybrid_d1_jaxref_r4_d1583c'

def setup_inputs(seed: int=0):
    np.random.seed(seed)
    _w = jnp.asarray

    def _L0_attn_a_setup():
        import jax, jax.numpy as jnp
        import numpy as np
        EMBED = 256
        HEADS = 16
        HD = EMBED // HEADS
        M = 32
        R = 2
        EPS = 1e-06
        C_CONST = 2.0 + EPS
        CHUNK = 128

        def _features(x, omega, quad_nodes, quad_weights):
            B, H, T, D = x.shape
            xn = x / jnp.maximum(jnp.linalg.norm(x, axis=-1, keepdims=True), 1e-12)
            proj = jnp.einsum('bhtd,rhdm->rbhtm', xn, omega)
            s = quad_nodes[:, None, None, None, None]
            sqrt_2s = jnp.sqrt(2.0 * jnp.maximum(s, 0.0))
            arg = jnp.clip(proj * sqrt_2s - s, -20.0, 20.0)
            feat = jnp.exp(arg) / np.sqrt(M).astype(np.float32)
            feat = feat * jnp.sqrt(jnp.maximum(quad_weights, 0.0))[:, None, None, None, None]
            return jnp.transpose(feat, (1, 2, 3, 0, 4)).reshape(B, H, T, R * M)
        key = jax.random.key(seed)
        ks = jax.random.split(key, 4)
        B, T = (2, 512)
        x = jax.random.normal(ks[0], (B, T, EMBED), jnp.float32)
        Wqkv = jax.random.normal(ks[1], (EMBED, 3 * EMBED), jnp.float32) * 0.02
        bqkv = jnp.zeros((3 * EMBED,), jnp.float32)
        Wout = jax.random.normal(ks[2], (EMBED, EMBED), jnp.float32) * 0.02
        bout = jnp.zeros((EMBED,), jnp.float32)
        omega = jax.random.normal(ks[3], (R, HEADS, HD, M), jnp.float32)
        nodes, weights = np.polynomial.laguerre.laggauss(R)
        quad_nodes = jnp.asarray(nodes / C_CONST, jnp.float32)
        quad_weights = jnp.asarray(weights * (C_CONST / 4.0), jnp.float32)
        return {'x': x, 'Wqkv': Wqkv, 'bqkv': bqkv, 'Wout': Wout, 'bout': bout, 'omega': omega, 'quad_nodes': quad_nodes, 'quad_weights': quad_weights}
    _L0_attn_a_in = _L0_attn_a_setup()

    def _L0_attn_b_setup():
        import jax, jax.numpy as jnp
        import numpy as np
        D_MODEL = 256
        N_HEADS = 16
        D_HEAD = D_MODEL // N_HEADS

        def _rmsnorm(x, w):
            xf = x.astype(jnp.float32)
            rms = jnp.mean(xf * xf, axis=-1, keepdims=True)
            return (xf / jnp.sqrt(rms + 1e-06) * w.astype(jnp.float32)).astype(x.dtype)
        key = jax.random.key(seed)
        ks = jax.random.split(key, 7)
        x = jax.random.normal(ks[0], (1, 1024, D_MODEL), dtype=jnp.float32)
        Wqkv = jax.random.normal(ks[1], (3 * D_MODEL, D_MODEL), dtype=jnp.float32) * (1.0 / np.sqrt(D_MODEL))
        bqkv = jax.random.normal(ks[2], (3 * D_MODEL,), dtype=jnp.float32) * 0.01
        Wo = jax.random.normal(ks[3], (D_MODEL, D_MODEL), dtype=jnp.float32) * (1.0 / np.sqrt(D_MODEL))
        bo = jax.random.normal(ks[4], (D_MODEL,), dtype=jnp.float32) * 0.01
        wq = jnp.ones((D_HEAD,), dtype=jnp.float32)
        wk = jnp.ones((D_HEAD,), dtype=jnp.float32)
        return {'x': x, 'Wqkv': Wqkv, 'bqkv': bqkv, 'Wo': Wo, 'bo': bo, 'wq': wq, 'wk': wk}
    _L0_attn_b_in = _L0_attn_b_setup()

    def _L0_ffn_setup():
        import jax, jax.numpy as jnp
        import numpy as np
        B, S, D, E = (4, 1024, 256, 8)
        key = jax.random.key(seed)
        ks = jax.random.split(key, 6)
        scale = 1.0 / np.sqrt(D)
        return {'tokens': jax.random.normal(ks[0], (B, S, D), dtype=jnp.float32), 'gate_w': jax.random.normal(ks[1], (D, E), dtype=jnp.float32) * scale, 'w0': jax.random.normal(ks[2], (D, D), dtype=jnp.float32) * scale, 'b0': jax.random.normal(ks[3], (D,), dtype=jnp.float32) * 0.01, 'w1': jax.random.normal(ks[4], (D, D), dtype=jnp.float32) * scale, 'b1': jax.random.normal(ks[5], (D,), dtype=jnp.float32) * 0.01}
    _L0_ffn_in = _L0_ffn_setup()
    _d = {'L0_attn_a_x': _L0_attn_a_in['x'], 'L0_attn_a_Wqkv': _L0_attn_a_in['Wqkv'], 'L0_attn_a_bqkv': _L0_attn_a_in['bqkv'], 'L0_attn_a_Wout': _L0_attn_a_in['Wout'], 'L0_attn_a_bout': _L0_attn_a_in['bout'], 'L0_attn_a_omega': _L0_attn_a_in['omega'], 'L0_attn_a_quad_nodes': _L0_attn_a_in['quad_nodes'], 'L0_attn_a_quad_weights': _L0_attn_a_in['quad_weights'], 'L0_attn_b_Wqkv': _L0_attn_b_in['Wqkv'], 'L0_attn_b_bqkv': _L0_attn_b_in['bqkv'], 'L0_attn_b_Wo': _L0_attn_b_in['Wo'], 'L0_attn_b_bo': _L0_attn_b_in['bo'], 'L0_attn_b_wq': _L0_attn_b_in['wq'], 'L0_attn_b_wk': _L0_attn_b_in['wk'], 'L0_ffn_gate_w': _L0_ffn_in['gate_w'], 'L0_ffn_w0': _L0_ffn_in['w0'], 'L0_ffn_b0': _L0_ffn_in['b0'], 'L0_ffn_w1': _L0_ffn_in['w1'], 'L0_ffn_b1': _L0_ffn_in['b1']}
    _x0 = _d['L0_attn_a_x']
    _d['L0_attn_a_x'] = jax.random.normal(jax.random.fold_in(jax.random.key(seed), 1), (2, 2048, 256), dtype=_x0.dtype)
    del _x0
    return _d

def reference(L0_attn_a_x, L0_attn_a_Wqkv, L0_attn_a_bqkv, L0_attn_a_Wout, L0_attn_a_bout, L0_attn_a_omega, L0_attn_a_quad_nodes, L0_attn_a_quad_weights, L0_attn_b_Wqkv, L0_attn_b_bqkv, L0_attn_b_Wo, L0_attn_b_bo, L0_attn_b_wq, L0_attn_b_wk, L0_ffn_gate_w, L0_ffn_w0, L0_ffn_b0, L0_ffn_w1, L0_ffn_b1):

    def _L0_attn_a_ref(x, Wqkv, bqkv, Wout, bout, omega, quad_nodes, quad_weights):
        import jax, jax.numpy as jnp
        import numpy as np
        EMBED = 256
        HEADS = 16
        HD = EMBED // HEADS
        M = 32
        R = 2
        EPS = 1e-06
        C_CONST = 2.0 + EPS
        CHUNK = 128

        def _features(x, omega, quad_nodes, quad_weights):
            B, H, T, D = x.shape
            xn = x / jnp.maximum(jnp.linalg.norm(x, axis=-1, keepdims=True), 1e-12)
            proj = jnp.einsum('bhtd,rhdm->rbhtm', xn, omega)
            s = quad_nodes[:, None, None, None, None]
            sqrt_2s = jnp.sqrt(2.0 * jnp.maximum(s, 0.0))
            arg = jnp.clip(proj * sqrt_2s - s, -20.0, 20.0)
            feat = jnp.exp(arg) / np.sqrt(M).astype(np.float32)
            feat = feat * jnp.sqrt(jnp.maximum(quad_weights, 0.0))[:, None, None, None, None]
            return jnp.transpose(feat, (1, 2, 3, 0, 4)).reshape(B, H, T, R * M)
        B, T, C = x.shape
        qkv = x @ Wqkv + bqkv
        q, k, v = jnp.split(qkv, 3, axis=-1)
        resh = lambda t: t.reshape(B, T, HEADS, HD).transpose(0, 2, 1, 3)
        q, k, v = (resh(q), resh(k), resh(v))
        qf = _features(q, omega, quad_nodes, quad_weights)
        kf = _features(k, omega, quad_nodes, quad_weights)
        Fd = R * M
        nc = T // CHUNK
        to_chunks = lambda t, last: t.reshape(B, HEADS, nc, CHUNK, last).transpose(2, 0, 1, 3, 4)
        qc = to_chunks(qf, Fd)
        kc = to_chunks(kf, Fd)
        vc = to_chunks(v, HD)

        def step(carry, inp):
            kv_state, k_state = carry
            q_ch, k_ch, v_ch = inp
            kv_prod = jnp.einsum('bhtf,bhtd->bhtfd', k_ch, v_ch)
            kv_cur = jnp.cumsum(kv_prod, axis=2) + kv_state[:, :, None]
            k_cur = jnp.cumsum(k_ch, axis=2) + k_state[:, :, None]
            ctx = jnp.einsum('bhtf,bhtfd->bhtd', q_ch, kv_cur)
            den = jnp.maximum(jnp.einsum('bhtf,bhtf->bht', q_ch, k_cur), 1e-06)
            out_ch = ctx / den[..., None]
            return ((kv_cur[:, :, -1], k_cur[:, :, -1]), out_ch)
        init = (jnp.zeros((B, HEADS, Fd, HD), jnp.float32), jnp.zeros((B, HEADS, Fd), jnp.float32))
        _, outs = jax.lax.scan(step, init, (qc, kc, vc))
        out = outs.transpose(1, 2, 0, 3, 4).reshape(B, HEADS, T, HD)
        out = out.transpose(0, 2, 1, 3).reshape(B, T, C)
        return out @ Wout + bout

    def _L0_attn_b_ref(x, Wqkv, bqkv, Wo, bo, wq, wk):
        import jax, jax.numpy as jnp
        import numpy as np
        D_MODEL = 256
        N_HEADS = 16
        D_HEAD = D_MODEL // N_HEADS

        def _rmsnorm(x, w):
            xf = x.astype(jnp.float32)
            rms = jnp.mean(xf * xf, axis=-1, keepdims=True)
            return (xf / jnp.sqrt(rms + 1e-06) * w.astype(jnp.float32)).astype(x.dtype)
        b, s, d = x.shape
        qkv = x @ Wqkv.T + bqkv
        q, k, v = jnp.split(qkv, 3, axis=-1)
        q = q.reshape(b, s, N_HEADS, D_HEAD)
        k = k.reshape(b, s, N_HEADS, D_HEAD)
        v = v.reshape(b, s, N_HEADS, D_HEAD)
        q = _rmsnorm(q, wq)
        k = _rmsnorm(k, wk)
        qf = q.astype(jnp.float32)
        kf = k.astype(jnp.float32)
        vf = v.astype(jnp.float32)
        attn = jnp.einsum('bqhd,bkhd->bhqk', qf, kf)
        attn = jax.nn.softmax(attn, axis=-1)
        z = jnp.einsum('bhqk,bkhd->bqhd', attn, vf).astype(x.dtype)
        z = z.reshape(b, s, d)
        return z @ Wo.T + bo

    def _L0_ffn_ref(tokens, gate_w, w0, b0, w1, b1):
        import jax, jax.numpy as jnp
        import numpy as np
        B, S, D, E = (4, 1024, 256, 8)
        b, s, d = tokens.shape
        logits = jnp.einsum('bsd,de->bse', tokens, gate_w)
        weights = jax.nn.softmax(logits, axis=-1)
        topk_w, topk_idx = jax.lax.top_k(weights, 2)
        x = tokens.reshape(b * s, d)
        fw = topk_w.reshape(b * s, 2)
        fidx = topk_idx.reshape(b * s, 2)
        e0 = jax.nn.silu(x @ w0.T + b0)
        e1 = jax.nn.silu(x @ w1.T + b1)
        m0 = (fidx[:, 0:1] == 0).astype(x.dtype)
        m1 = (fidx[:, 1:2] == 1).astype(x.dtype)
        out = e0 * fw[:, 0:1] * m0 + e1 * fw[:, 1:2] * m1
        return out.reshape(b, s, d)
    x = L0_attn_a_x
    x = x + _L0_attn_a_ref(_layernorm(x, axis=-1), L0_attn_a_Wqkv, L0_attn_a_bqkv, L0_attn_a_Wout, L0_attn_a_bout, L0_attn_a_omega, L0_attn_a_quad_nodes, L0_attn_a_quad_weights)
    x = x + _L0_ffn_ref(_layernorm(x, axis=-1), L0_ffn_gate_w, L0_ffn_w0, L0_ffn_b0, L0_ffn_w1, L0_ffn_b1)
    x = x + _L0_attn_b_ref(_layernorm(x, axis=-1), L0_attn_b_Wqkv, L0_attn_b_bqkv, L0_attn_b_Wo, L0_attn_b_bo, L0_attn_b_wq, L0_attn_b_wk)
    x = x + _L0_ffn_ref(_layernorm(x, axis=-1), L0_ffn_gate_w, L0_ffn_w0, L0_ffn_b0, L0_ffn_w1, L0_ffn_b1)
    return x

_drawn_inputs = setup_inputs


def setup_inputs(seed=0):
    import zlib

    import numpy as np

    out = dict(_drawn_inputs(seed))
    spreads = {'L0_attn_a_bqkv': (0.0, 0.1),
     'L0_attn_a_bout': (0.0, 0.1),
     'L0_attn_b_wq': (1.0, 0.2),
     'L0_attn_b_wk': (1.0, 0.2)}
    factors = {'L0_attn_a_Wqkv': 3.039,
     'L0_attn_a_omega': 5.045,
     'L0_attn_a_quad_nodes': 3.028,
     'L0_attn_a_quad_weights': 10.633,
     'L0_attn_b_bqkv': 3.213,
     'L0_attn_b_bo': 4.679,
     'L0_ffn_b0': 25.962,
     'L0_ffn_b1': 40.587}
    for name, (base, spread) in spreads.items():
        noise = np.random.default_rng([zlib.crc32(name.encode()), seed]).standard_normal(out[name].shape)
        drawn = base * np.exp(spread * noise) if base else spread * noise
        out[name] = jnp.asarray(drawn.astype(out[name].dtype))
    for name, factor in factors.items():
        out[name] = (out[name] * factor).astype(out[name].dtype)
    return out
```

```python
from contextlib import ExitStack

import numpy as np

import concourse.bass as bass
from concourse import mybir

F32 = mybir.dt.float32
BF16 = mybir.dt.bfloat16
I32 = mybir.dt.int32
ALU = mybir.AluOpType
ACT = mybir.ActivationFunctionType
AX = mybir.AxisListType

P = 128
B, T, D = 2, 2048, 256
H = 16
HD = D // H
M, R = 32, 2
FD = R * M
NPAIR = H // 2
NT = B * T // P
TB = T // P
GT = 4
NG = NT // GT
C = D // P
V1 = HD + 1
E = 8
LN_EPS = 1e-5
RMS_EPS = 1e-6
NORM_FLOOR = 1e-12
CLIP = 20.0
DEN_FLOOR = 1e-6
SAFE_SCORE = 60.0
PARTS = 3
HROWS = PARTS * HD
SROWS = 2 * HROWS
KROWS = SROWS + 1
KT = T // P


def after(eng, sem, count):
    if isinstance(count, int) and count <= 0:
        return
    eng.wait_ge(sem, count)


def live(i, n):
    return not isinstance(i, int) or 0 <= i < n


def pipelined(eng, n, lead, tail, body):
    for i in range(lead):
        body(i, i % 2)
    turns = (n - lead) // 2
    with eng.Fori(0, turns) as q:
        for u in range(2):
            body(2 * q + (lead + u), (lead + u) % 2)
    for i in range(lead + 2 * turns, n + tail):
        body(i, i % 2)


class Phase:

    def __init__(self, nc, tag):
        self.nc, self.tag, self.ctx = nc, tag, ExitStack()

    def __enter__(self):
        self.ctx.__enter__()
        return self

    def __exit__(self, *e):
        return self.ctx.__exit__(*e)

    def sb(self, name, shape, dt=F32):
        return self.ctx.enter_context(self.nc.sbuf_tensor(f"{self.tag}_{name}", shape, dt))

    def ps(self, name, shape, dt=F32):
        return self.ctx.enter_context(self.nc.psum_tensor(f"{self.tag}_{name}", shape, dt))

    def sem(self, name):
        return self.ctx.enter_context(self.nc.semaphore(f"{self.tag}_{name}"))


def setup(nc, w, d):
    with Phase(nc, "setup") as ph:
        loaded = ph.sem("loaded")
        zeroed = ph.sem("zeroed")
        diagonal = ph.sem("diagonal")
        mrow_out = ph.sem("mrow_out")
        derived = ph.sem("derived")
        rooted = ph.sem("rooted")
        omega_in = ph.sem("omega_in")
        zrow = ph.sb("zrow", [32, T], BF16)
        roots = ph.sb("roots", [P, R])
        nodes = ph.sb("nodes", [P, R])
        half = ph.sb("half", [P, R])
        wrow = ph.sb("wrow", [1, 3, HD])
        top = ph.sb("top", [1, 1])

        def row(src, n=P):
            return src.unsqueeze(0).broadcast_to([n] + list(src.shape))

        loads = [
            (w.wa[:, :, :], d["L0_attn_a_Wqkv"].rearrange("(c p) n -> p c n", p=P)),
            (w.wb[:, :, :], d["attn_b_WqkvT"].rearrange("(c p) n -> p c n", p=P)),
            (w.woa[:, :, :], d["L0_attn_a_Wout"].rearrange("(c p) n -> p c n", p=P)),
            (w.wob[:, :, :], d["attn_b_WoT"].rearrange("(c p) n -> p c n", p=P)),
            (w.wf[:, :, 0:D], d["ffn_w0T"].rearrange("(c p) n -> p c n", p=P)),
            (w.wf[:, :, D:2 * D], d["ffn_w1T"].rearrange("(c p) n -> p c n", p=P)),
            (w.wf[:, :, 2 * D:2 * D + E], d["L0_ffn_gate_w"].rearrange("(c p) n -> p c n", p=P)),
            (w.ba[:, :], row(d["L0_attn_a_bqkv"])),
            (w.bb[:, :], row(d["L0_attn_b_bqkv"])),
            (w.boa[:, :], row(d["L0_attn_a_bout"])),
            (w.bob[:, :], row(d["L0_attn_b_bo"])),
            (w.bf[:, 0:D], row(d["L0_ffn_b0"])),
            (w.bf[:, D:2 * D], row(d["L0_ffn_b1"])),
            (w.wqk[:, 0, :], row(d["L0_attn_b_wq"])),
            (w.wqk[:, 1, :], row(d["L0_attn_b_wk"])),
            (wrow[0:1, 0, :], row(d["L0_attn_b_wq"], 1)),
            (wrow[0:1, 1, :], row(d["L0_attn_b_wk"], 1)),
            (nodes[:, :], row(d["L0_attn_a_quad_nodes"])),
        ]
        for q in range(P // M):
            r = q % R
            part = slice(M * q, M * q + M)
            loads.append((w.fnode[part, 0:1], row(d["L0_attn_a_quad_nodes"][r:r + 1], M)))
            loads.append((w.fweight[part, 0:1], row(d["L0_attn_a_quad_weights"][r:r + 1], M)))

        with nc.Block() as block:
            @block.sync
            def _(sp):
                for dst, src in loads:
                    sp.dma_start(dst, src).then_inc(loaded, 16)
                sp.wait_ge(zeroed, 2)
                for h in range(H):
                    c, hh = divmod(h, H // C)
                    sp.dma_start(
                        w.omega[HD * hh:HD * hh + HD, c, FD * hh:FD * hh + FD].rearrange("d (r m) -> d r m", r=R),
                        d["L0_attn_a_omega"][:, h].rearrange("r d m -> d r m"),
                    ).then_inc(omega_in, 16)
                sp.dma_start(d["mrow"], zrow[:, :]).then_inc(mrow_out, 16)
                sp.wait_ge(mrow_out, 16)

            @block.gpsimd
            def _(pool):
                pool.memset(w.omega[:, :, :], 0.0).then_inc(zeroed, 1)
                pool.memset(zrow[:, :], 0.0).then_inc(zeroed, 1)
                pool.memset(w.ident[:, :], 0.0).then_inc(zeroed, 1)
                pool.memset(w.mask[:, :], 1.0).then_inc(zeroed, 1)
                pool.memset(w.minushalf[:, :], -0.5).then_inc(zeroed, 1)
                pool.memset(half[:, :], 0.5).then_inc(zeroed, 1)
                pool.memset(w.keep[:, :], 1.0).then_inc(zeroed, 1)
                pool.memset(w.lneps[:, :], LN_EPS).then_inc(zeroed, 1)
                pool.memset(w.rmseps[:, :], HD * RMS_EPS).then_inc(zeroed, 1)
                pool.memset(w.one[:, :], 1.0).then_inc(zeroed, 1)
                pool.wait_ge(zeroed, 10)
                pool.memset(w.keep[:, TB - 1:TB], 0.0)
                pool.affine_select(out=w.ident[:, :], in_=w.ident[:, :], compare_op=ALU.not_equal, fill=1.0,
                                   base=0, pattern=[[-1, P]], channel_multiplier=1).then_inc(diagonal, 1)
                pool.affine_select(out=w.mask[:, :], in_=w.mask[:, :], compare_op=ALU.is_ge, fill=0.0,
                                   base=0, pattern=[[1, P]], channel_multiplier=-1)
                pool.wait_ge(derived, 1)
                pool.tensor_tensor(roots[:, :], nodes[:, :], half[:, :], ALU.pow).then_inc(rooted, 1)

            @block.vector
            def _(dve):
                dve.wait_ge(loaded, 16 * len(loads))
                dve.tensor_scalar(nodes[:, :], nodes[:, :], 0.0, 2.0, ALU.max, ALU.mult).then_inc(derived, 1)
                dve.tensor_scalar(w.flo[:, :], w.fnode[:, :], -CLIP, None, ALU.add)
                dve.tensor_scalar(w.fhi[:, :], w.fnode[:, :], CLIP, None, ALU.add)
                dve.tensor_scalar(w.fneg[:, :], w.fnode[:, :], -1.0, None, ALU.mult)
                dve.tensor_scalar(w.fscale[:, :], w.fweight[:, :], 0.0, 1.0 / M, ALU.max, ALU.mult)
                dve.tensor_scalar(w.wqk[:, :, :], w.wqk[:, :, :], float(HD) ** 0.5, None, ALU.mult)
                dve.wait_ge(diagonal, 1)
                dve.tensor_copy(w.identb[:, :], w.ident[:, :])
                dve.tensor_tensor(wrow[:, 2, :], wrow[:, 0, :], wrow[:, 1, :], ALU.mult).then_inc(derived, 1)
                dve.wait_ge(derived, 2)
                dve.tensor_reduce(top[:, :], wrow[:, 2, :], AX.X, ALU.max, apply_absolute_value=True).then_inc(derived, 1)
                dve.wait_ge(derived, 3)
                dve.tensor_scalar(w.flag[:, :], top[:, :], SAFE_SCORE / HD, None, ALU.is_gt)
                dve.wait_ge(rooted, 1)
                dve.wait_ge(omega_in, 16 * H)
                om = w.omega[:, :, :].rearrange("p c (h r m) -> p (c h) r m", r=R, m=M)
                for r in range(R):
                    dve.tensor_scalar(om[:, :, r, :], om[:, :, r, :], roots[:, r:r + 1], None, ALU.mult)


def attention_a(nc, w, d):
    with Phase(nc, "la") as ph:
        x_in = [ph.sem("x_in0"), ph.sem("x_in1")]
        (cleared, bn_done, mv_ready, var_ready, rstd_ready, h_ready, ht_ps, ht_ready, qkv_ps, qkv_read, sq_ready,
         ss_ready, ssm_ready, rn_ready, qn_ready, qkt_ps, qkt_ready, pq_ps, argq_ready, qf_ready, pk_ps, argk_ready,
         kexp_ready, kf_ready, kt_ps, kt_ready, at_ps, at_ready, ctx_ps, st_ps, st_ready, s_ps, s_ready, ct_ready,
         ctok_ps, den_ready, rden_ready, ctx_ready, vb_ready) = [ph.sem(s) for s in (
             "cleared bn_done mv_ready var_ready rstd_ready h_ready ht_ps ht_ready qkv_ps qkv_read sq_ready "
             "ss_ready ssm_ready rn_ready qn_ready qkt_ps qkt_ready pq_ps argq_ready qf_ready pk_ps argk_ready "
             "kexp_ready kf_ready kt_ps kt_ready at_ps at_ready ctx_ps st_ps st_ready s_ps s_ready ct_ready "
             "ctok_ps den_ready rden_ready ctx_ready vb_ready").split()]

        st6 = ph.sb("st6", [P, 2, 6])
        mv = ph.sb("mv", [P, 2, 2])
        var = ph.sb("var", [P, 2, 1])
        rstd = ph.sb("rstd", [P, 2, 1])
        hn = ph.sb("hn", [P, 2, D])
        ht = ph.sb("ht", [P, 2, C, P])
        qk = ph.sb("qk", [P, 2, 2 * D])
        vs = ph.sb("vs", [P, 2, D])
        vb = ph.sb("vb", [P, 2, H, V1])
        sq = ph.sb("sq", [P, 2 * D])
        ss = ph.sb("ss", [P, 2, 2 * H])
        ssm = ph.sb("ssm", [P, 2, 2 * H])
        rn = ph.sb("rn", [P, 2, 2 * H])
        qn = ph.sb("qn", [P, 2, 2 * D])
        qkt = ph.sb("qkt", [P, 2, 2 * C, P])
        argq = ph.sb("argq", [P, NPAIR, P])
        argk = ph.sb("argk", [P, NPAIR, P])
        kexp = ph.sb("kexp", [P, NPAIR, P])
        qf = ph.sb("qf", [P, 2, NPAIR, 2, P])
        kf = ph.sb("kf", [P, 2, NPAIR, P])
        kt = ph.sb("kt", [P, 2, NPAIR, P])
        at = ph.sb("at", [P, 2, NPAIR, 2, P])
        stt = ph.sb("stt", [P, 4, P])
        state = ph.sb("state", [P, H, V1])
        ct = ph.sb("ct", [P, 4, P])
        den = ph.sb("den", [P, 2, H])
        rden = ph.sb("rden", [P, 2, H])

        b0 = ph.ps("b0", [P, 4, P])
        b1 = ph.ps("b1", [P, 2 * D])
        b2 = ph.ps("b2", [P, 2 * D])
        b34 = ph.ps("b34", [P, NPAIR, P])
        b5 = ph.ps("b5", [P, 4, P])
        b6 = ph.ps("b6", [P, 4, P])
        b7 = ph.ps("b7", [P, 4, P])
        b56 = [b5, b6]

        xs = d["L0_attn_a_x"].rearrange("b (t p) d -> (b t) p d", p=P)
        mix = w.mix[:, :, :, :, :]

        def slots(bank):
            return bank[:, :, :].rearrange("p g (j s) -> p g j s", j=4)

        with nc.Block() as block:
            @block.sync
            def _(sp):
                def body(n, par):
                    if not isinstance(n, int):
                        sp.wait_ge(x_in[par], 16)
                    after(sp, x_in[par], 16 * ((n - par) // 2) if isinstance(n, int) else 8 * (n - par))
                    sp.dma_start(w.x[:, n, :], xs[n]).then_inc(x_in[par], 16)
                pipelined(sp, NT, 4, 0, body)

            @block.gpsimd
            def _(pool):
                pool.memset(vb[:, :, :, :], 1.0).then_inc(cleared, 1)
                pool.memset(qf[:, :, :, :, :], 0.0).then_inc(cleared, 1)
                pool.memset(state[:, :, :], 0.0).then_inc(cleared, 1)
                pool.wait_ge(cleared, 3)

                def body(n, par):
                    i, j = n - 1, n - 2
                    if live(j, NT):
                        after(pool, qkv_read, j + 1)
                        after(pool, ctx_ps, j - 1)
                        pool.tensor_tensor(vb[:, par, :, 0:HD], vs[:, par, :].rearrange("p (h e) -> p h e", h=H),
                                           w.one[:, 0:1].unsqueeze(2).broadcast_to([P, H, HD]), ALU.mult).then_inc(vb_ready, 1)
                    if live(i, NT):
                        after(pool, qkv_read, i + 1)
                        after(pool, ss_ready, i)
                        pool.tensor_tensor(sq[:, :], qk[:, 1 - par, :], qk[:, 1 - par, :], ALU.mult).then_inc(sq_ready, 1)
                        after(pool, ssm_ready, i + 1)
                        after(pool, qn_ready, i - 1)
                        pool.tensor_tensor(rn[:, 1 - par, :], ssm[:, 1 - par, :], w.minushalf[:, 0:2 * H], ALU.pow).then_inc(rn_ready, 1)
                    if live(n, NT):
                        after(pool, mv_ready, n + 1)
                        after(pool, rstd_ready, n - 1)
                        pool.tensor_tensor(var[:, par, :], mv[:, par, 1:2], w.lneps[:, 0:1], ALU.add).then_inc(var_ready, 1)
                        after(pool, var_ready, n + 1)
                        after(pool, h_ready, n - 1)
                        pool.tensor_tensor(rstd[:, par, :], var[:, par, :], w.minushalf[:, 0:1], ALU.pow).then_inc(rstd_ready, 1)
                pipelined(pool, NT, 5, 3, body)

            @block.vector
            def _(dve):
                dve.memset(b7[:, :, :], 0.0).then_inc(cleared, 1)

                def body(n, par):
                    i, j, k = n - 1, n - 2, n - 3
                    if live(j, NT):
                        after(dve, pq_ps, j + 1)
                        after(dve, qf_ready, j)
                        dve.tensor_scalar(argq[:, :, :], b34[:, :, :], w.flo[:, 0:1], w.fhi[:, 0:1],
                                          ALU.max, ALU.min).then_inc(argq_ready, 1)
                    if live(i, NT):
                        after(dve, qkv_ps, i + 1)
                        after(dve, sq_ready, i - 1)
                        dve.tensor_tensor(qk[:, 1 - par, :], b1[:, :], w.ba[:, 0:2 * D], ALU.add)
                        after(dve, vb_ready, i - 1)
                        dve.tensor_tensor(vs[:, 1 - par, :], b2[:, 0:D], w.ba[:, 2 * D:3 * D], ALU.add).then_inc(qkv_read, 1)
                    if live(j, NT):
                        after(dve, pk_ps, j + 1)
                        after(dve, kexp_ready, j)
                        dve.tensor_scalar(argk[:, :, :], b34[:, :, :], w.flo[:, 0:1], w.fhi[:, 0:1],
                                          ALU.max, ALU.min).then_inc(argk_ready, 1)
                    if live(i, NT):
                        after(dve, sq_ready, i + 1)
                        after(dve, ssm_ready, i - 1)
                        dve.tensor_reduce(ss[:, 1 - par, :], sq[:, :].rearrange("p (g e) -> p g e", e=HD),
                                          AX.X, ALU.add).then_inc(ss_ready, 1)
                        after(dve, ss_ready, i + 1)
                        dve.tensor_scalar(ssm[:, 1 - par, :], ss[:, 1 - par, :], NORM_FLOOR ** 2, None,
                                          ALU.max).then_inc(ssm_ready, 1)
                    if live(k, NT):
                        for r in range(4):
                            after(dve, at_ps, 4 * k + r + 1)
                            if r == 0:
                                after(dve, ctx_ps, k - 1)
                            dve.tensor_tensor(
                                at[:, 1 - par, 2 * r:2 * r + 2, :, :].rearrange("p g e t -> p (g e) t"),
                                b56[r % 2][:, :, :], w.mask[:, :].unsqueeze(1).broadcast_to([P, 4, P]),
                                ALU.mult).then_inc(at_ready, 1)
                            if r == 1 and live(j, NT):
                                after(dve, kexp_ready, j + 1)
                                after(dve, kt_ps, j - 1)
                                dve.tensor_scalar(kf[:, par, :, :], kexp[:, :, :], w.fscale[:, 0:1], None,
                                                  ALU.mult).then_inc(kf_ready, 1)
                    elif live(j, NT):
                        after(dve, kexp_ready, j + 1)
                        dve.tensor_scalar(kf[:, par, :, :], kexp[:, :, :], w.fscale[:, 0:1], None,
                                          ALU.mult).then_inc(kf_ready, 1)
                    if live(n, NT):
                        count = 16 * ((n - par) // 2 + 1) if isinstance(n, int) else 8 * (n - par) + 16
                        dve.wait_ge(x_in[par], count)
                        after(dve, mv_ready, n - 1)
                        dve.bn_stats(st6[:, par, :], w.x[:, n, :]).then_inc(bn_done, 1)
                        dve.wait_ge(bn_done, n + 1)
                        after(dve, rstd_ready, n - 1)
                    if live(i, NT):
                        after(dve, rn_ready, i + 1)
                        after(dve, qkt_ps, i - 1)
                        dve.tensor_tensor(
                            qn[:, 1 - par, :].rearrange("p (g e) -> p g e", e=HD),
                            qk[:, 1 - par, :].rearrange("p (g e) -> p g e", e=HD),
                            rn[:, 1 - par, :].unsqueeze(2).broadcast_to([P, 2 * H, HD]),
                            ALU.mult).then_inc(qn_ready, 1)
                    if live(n, NT):
                        dve.bn_aggr(mv[:, par, :], st6[:, par, :]).then_inc(mv_ready, 1)
                    if live(k, NT):
                        after(dve, s_ps, k + 1)
                        after(dve, ctx_ps, k + 1)
                        after(dve, s_ready, k)
                        dve.scalar_tensor_tensor(
                            out=state[:, :, :], in0=state[:, :, :], scalar=w.keep[:, bass.ds(k, 1)],
                            in1=b6[:, :, :].rearrange("p g (j s) -> p (g j) s", j=4)[:, :, 0:V1],
                            op0=ALU.mult, op1=ALU.add).then_inc(s_ready, 1)
                    if live(n, NT):
                        after(dve, rstd_ready, n + 1)
                        after(dve, ht_ps, n - 1)
                        dve.tensor_scalar(hn[:, par, :], w.x[:, n, :], mv[:, par, 0:1], rstd[:, par, :],
                                          ALU.subtract, ALU.mult).then_inc(h_ready, 1)
                    if live(k, NT):
                        after(dve, ctok_ps, k + 1)
                        tok = slots(b7)
                        kp = 1 - par
                        dve.tensor_scalar(den[:, kp, :].rearrange("p (g j) -> p g j", j=4), tok[:, :, :, HD],
                                          DEN_FLOOR, None, ALU.max).then_inc(den_ready, 1)
                        dve.wait_ge(den_ready, k + 1)
                        dve.reciprocal(rden[:, kp, :], den[:, kp, :]).then_inc(rden_ready, 1)
                        dve.wait_ge(rden_ready, k + 1)
                        out = mix[:, k // TB, :, k % TB, :].rearrange("p (g j) e -> p g j e", j=4)
                        dve.tensor_tensor(
                            out, tok[:, :, :, 0:HD],
                            rden[:, kp, :].rearrange("p (g j) -> p g j", j=4).unsqueeze(3).broadcast_to([P, 4, 4, HD]),
                            ALU.mult).then_inc(ctx_ready, 1)
                pipelined(dve, NT, 5, 3, body)

            @block.scalar
            def _(act):
                act.wait_ge(cleared, 4)

                def body(n, par):
                    i, j, k = n - 1, n - 2, n - 3
                    if live(i, NT):
                        after(act, ht_ps, i + 1)
                        after(act, qkv_ps, i - 1)
                        act.activation(ht[:, 1 - par, :, :], b0[:, 0:C, :], ACT.Copy).then_inc(ht_ready, 1)
                    if live(j, NT):
                        after(act, argq_ready, j + 1)
                        after(act, ctx_ps, j - 1)
                        act.activation(qf[0:FD, par, :, 0, :], argq[0:FD, :, :], ACT.Exp, bias=w.fneg[0:FD, 0:1])
                        act.activation(qf[FD:P, par, :, 1, :], argq[FD:P, :, :], ACT.Exp,
                                       bias=w.fneg[FD:P, 0:1]).then_inc(qf_ready, 1)
                        after(act, argk_ready, j + 1)
                        after(act, kf_ready, j)
                        act.activation(kexp[:, :, :], argk[:, :, :], ACT.Exp, bias=w.fneg[:, 0:1]).then_inc(kexp_ready, 1)
                    if live(k, NT):
                        after(act, st_ps, k + 1)
                        after(act, s_ps, k)
                        act.activation(stt[:, :, :], b5[:, :, :], ACT.Copy, scale=w.keep[:, bass.ds(k, 1)]).then_inc(st_ready, 1)
                        after(act, ctx_ps, k + 1)
                        after(act, ctok_ps, k)
                        act.activation(ct[:, :, :], b7[:, :, :], ACT.Copy).then_inc(ct_ready, 1)
                    if live(j, NT):
                        after(act, kt_ps, j + 1)
                        after(act, st_ps, j - 1)
                        act.activation(kt[:, par, :, :], b34[:, :, :], ACT.Copy).then_inc(kt_ready, 1)
                    if live(i, NT):
                        after(act, qkt_ps, i + 1)
                        after(act, pk_ps, i - 1)
                        act.activation(qkt[:, 1 - par, :, :], b0[:, :, :], ACT.Copy).then_inc(qkt_ready, 1)
                pipelined(act, NT, 5, 3, body)

            @block.tensor
            def _(pe):
                def project(half, par):
                    for g in range(NPAIR):
                        c, gg = divmod(g, NPAIR // C)
                        mm = pe.matmul(b34[:, g, :], w.omega[:, c, P * gg:P * gg + P], qkt[:, par, half + c, :],
                                       start=True, stop=True)
                    return mm

                def body(n, par):
                    i, j, k = n - 1, n - 2, n - 3
                    ip, jp, kp = 1 - par, par, 1 - par
                    if live(i, NT):
                        after(pe, h_ready, i + 1)
                        after(pe, qkt_ready, i)
                        for c in range(C):
                            mm = pe.transpose(b0[:, c, :], hn[:, ip, P * c:P * c + P], w.ident[:, :])
                        mm.then_inc(ht_ps, 1)
                    if live(j, NT):
                        after(pe, qkt_ready, j + 1)
                        after(pe, kt_ready, j)
                        project(0, jp).then_inc(pq_ps, 1)
                    if live(i, NT):
                        after(pe, ht_ready, i + 1)
                        after(pe, qkv_read, i)
                        for bank, lo, hi in ((b1, 0, 2 * D), (b2, 2 * D, 3 * D)):
                            for c in range(C):
                                mm = pe.matmul(bank[:, 0:hi - lo], ht[:, ip, c, :], w.wa[:, c, lo:hi],
                                               start=(c == 0), stop=(c == C - 1))
                        mm.then_inc(qkv_ps, 1)
                    if live(j, NT):
                        after(pe, argq_ready, j + 1)
                        project(C, jp).then_inc(pk_ps, 1)
                    if live(k, NT):
                        after(pe, kf_ready, k + 1)
                        after(pe, qf_ready, k + 1)
                        for r in range(4):
                            if r < 2:
                                after(pe, st_ready if r == 0 else s_ready, k)
                            else:
                                after(pe, at_ready, 4 * k + r - 1)
                            for g in (2 * r, 2 * r + 1):
                                mm = pe.matmul(b56[r % 2][:, 2 * (g % 2):2 * (g % 2) + 2, :], kf[:, kp, g, :],
                                               qf[:, kp, g, :, :], start=True, stop=True)
                            mm.then_inc(at_ps, 1)
                        after(pe, kt_ready, k + 1)
                        after(pe, vb_ready, k + 1)
                        after(pe, at_ready, 4 * k + 3)
                        for h in range(H):
                            q, s = divmod(h, 4)
                            mm = pe.matmul(b5[32 * s:32 * s + V1, q, :], vb[:, kp, h, :], kt[:, kp, h // 2, :],
                                           start=True, stop=True)
                        mm.then_inc(st_ps, 1)
                        after(pe, at_ready, 4 * k + 4)
                        after(pe, s_ready, k)
                        after(pe, ctx_ready, k)
                        if isinstance(k, int) and k == 0:
                            pe.wait_ge(cleared, 4)
                        for q in range(4):
                            for s in range(4):
                                h = 4 * q + s
                                pe.matmul(b7[32 * s:32 * s + V1, q, :], state[:, h, :], qf[:, kp, h // 2, h % 2, :],
                                          start=True, stop=False)
                            for s in range(4):
                                h = 4 * q + s
                                mm = pe.matmul(b7[32 * s:32 * s + V1, q, :], vb[:, kp, h, :],
                                               at[:, kp, h // 2, h % 2, :], start=False, stop=True)
                        mm.then_inc(ctx_ps, 1)
                    if live(j, NT):
                        after(pe, kf_ready, j + 1)
                        after(pe, argk_ready, j + 1)
                        for g in range(NPAIR):
                            mm = pe.transpose(b34[:, g, :], kf[:, jp, g, :], w.ident[:, :])
                        mm.then_inc(kt_ps, 1)
                    if live(k, NT):
                        after(pe, st_ready, k + 1)
                        for q in range(4):
                            mm = pe.transpose(b6[:, q, :], stt[:, q, :], w.ident[:, :])
                        mm.then_inc(s_ps, 1)
                        after(pe, ct_ready, k + 1)
                        for q in range(4):
                            mm = pe.transpose(b7[:, q, :], ct[:, q, :], w.ident[:, :])
                        mm.then_inc(ctok_ps, 1)
                    if live(i, NT):
                        after(pe, qn_ready, i + 1)
                        after(pe, ht_ready, i + 1)
                        for c in range(2 * C):
                            mm = pe.transpose(b0[:, c, :], qn[:, ip, P * c:P * c + P], w.ident[:, :])
                        mm.then_inc(qkt_ps, 1)
                pipelined(pe, NT, 5, 3, body)


def project_and_ffn(nc, w, d, tag, wo, bo, out):
    with Phase(nc, tag) as ph:
        (staged, xb_ready, ctx_ps, ct_ready, proj_ps, x1_ready, bn_done, mv_ready, var_ready, rstd_ready, h_ready,
         ht_ps, ht_ready, z_ps, z_read, th_ready, gate_read, top_ready, diff_ready, exp_ready, sum_ready, rsum_ready,
         above_ready, count_ready, tie_ready, rank_ready, pick_ready, gates_ready, u_ready, half_done, x2_ready, stored
         ) = [ph.sem(s) for s in (
             "staged xb_ready ctx_ps ct_ready proj_ps x1_ready bn_done mv_ready var_ready rstd_ready h_ready "
             "ht_ps ht_ready z_ps z_read th_ready gate_read top_ready diff_ready exp_ready sum_ready rsum_ready "
             "above_ready count_ready tie_ready rank_ready pick_ready gates_ready u_ready half_done x2_ready stored").split()]
        cs = ph.sb("cs", [P, 2, GT, D])
        ct = ph.sb("ct", [P, 2, C, GT, P])
        st6 = ph.sb("st6", [P, GT, 6])
        mv = ph.sb("mv", [P, 2, GT, 2])
        var = ph.sb("var", [P, GT])
        rstd = ph.sb("rstd", [P, 2, GT])
        hn = ph.sb("hn", [P, 2, GT, D])
        ht = ph.sb("ht", [P, 2, C, GT, P])
        z = ph.sb("z", [P, GT, 2 * D])
        th = ph.sb("th", [P, GT, 2 * D])
        lg = ph.sb("lg", [P, GT, E])
        top = ph.sb("top", [P, GT])
        diff = ph.sb("diff", [P, GT, E])
        ex = ph.sb("ex", [P, GT, E])
        total = ph.sb("total", [P, GT])
        half_r = ph.sb("half_r", [P, GT])
        above = ph.sb("above", [P, GT, E])
        rank = ph.sb("rank", [P, GT])
        tie = ph.sb("tie", [P, GT])
        pick = ph.sb("pick", [P, 2, GT])
        gates = ph.sb("gates", [P, 2, GT])

        b0 = ph.ps("b0", [P, GT, P])
        b1 = ph.ps("b1", [P, GT, P])
        b2 = ph.ps("b2", [P, GT, P])
        b3 = ph.ps("b3", [P, GT, P])
        bz = [ph.ps(f"bz{t}", [P, 2 * D]) for t in range(GT)]
        lps = b1[:, 0, 0:GT * E].rearrange("p (t e) -> p t e", t=GT)
        proj = [b2[:, :, :].rearrange("p (t c) k -> p t (c k)", c=C), b3[:, :, :].rearrange("p (t c) k -> p t (c k)", c=C)]

        def xg(g, t0=0, n=GT):
            return w.x[:, bass.ds(g * GT + t0, n), :]

        with nc.Block() as block:
            @block.gpsimd
            def _(pool):
                def body(n, par):
                    if live(n, NG):
                        pool.tensor_tensor(xg(n), xg(n), bo[:, :].unsqueeze(1).broadcast_to([P, GT, D]),
                                           ALU.add).then_inc(xb_ready, 1)
                        after(pool, mv_ready, n + 1)
                        pool.tensor_tensor(var[:, :], mv[:, par, :, 1], w.lneps[:, :], ALU.add).then_inc(var_ready, 1)
                        after(pool, var_ready, n + 1)
                        pool.tensor_tensor(rstd[:, par, :], var[:, :], w.minushalf[:, 0:GT], ALU.pow).then_inc(rstd_ready, 1)
                pipelined(pool, NG, 3, 1, body)

            @block.vector
            def _(dve):
                def stage(n, par):
                    after(dve, ctx_ps, 2 * (n - 1))
                    dve.tensor_copy(cs[:, par, :, :].rearrange("p t (h e) -> p h t e", h=H),
                                    w.mix[:, n // (NG // B), :, bass.ds((n % (NG // B)) * GT, GT), :]).then_inc(staged, 1)

                def body(n, par):
                    y, yp = n - 1, 1 - par
                    if live(n, NG):
                        stage(n, par)
                    if live(y, NG):
                        for t in range(GT):
                            after(dve, z_ps, GT * y + t + 1)
                            if t == 0:
                                after(dve, x2_ready, y)
                            dve.tensor_tensor(z[:, t, :], bz[t][:, :], w.bf[:, :], ALU.add).then_inc(z_read, 1)
                        dve.tensor_copy(lg[:, :, :], lps).then_inc(gate_read, 1)
                        dve.wait_ge(gate_read, y + 1)
                        dve.tensor_reduce(top[:, :], lg[:, :, :], AX.X, ALU.max).then_inc(top_ready, 1)
                        dve.tensor_tensor(above[:, :, :], lg[:, :, :], lg[:, :, 1:2].broadcast_to([P, GT, E]),
                                          ALU.is_gt).then_inc(above_ready, 1)
                        dve.tensor_tensor(tie[:, :], lg[:, :, 0], lg[:, :, 1], ALU.is_equal).then_inc(tie_ready, 1)
                        dve.wait_ge(top_ready, y + 1)
                        after(dve, exp_ready, y)
                        dve.tensor_tensor(diff[:, :, :], lg[:, :, :], top[:, :].unsqueeze(2).broadcast_to([P, GT, E]),
                                          ALU.subtract).then_inc(diff_ready, 1)
                        dve.wait_ge(above_ready, y + 1)
                        dve.tensor_reduce(rank[:, :], above[:, :, :], AX.X, ALU.add).then_inc(count_ready, 1)
                        dve.tensor_tensor(pick[:, 0, :], lg[:, :, 0], top[:, :], ALU.is_equal)
                        dve.wait_ge(count_ready, y + 1)
                        dve.wait_ge(tie_ready, y + 1)
                        dve.tensor_tensor(rank[:, :], rank[:, :], tie[:, :], ALU.add).then_inc(rank_ready, 1)
                        dve.wait_ge(exp_ready, y + 1)
                        dve.tensor_reduce(total[:, :], ex[:, :, :], AX.X, ALU.add).then_inc(sum_ready, 1)
                        dve.wait_ge(rank_ready, y + 1)
                        dve.scalar_tensor_tensor(out=pick[:, 1, :], in0=rank[:, :], scalar=1.0, in1=ex[:, :, 1],
                                                 op0=ALU.is_equal, op1=ALU.mult).then_inc(pick_ready, 1)
                        dve.wait_ge(sum_ready, y + 1)
                        dve.reciprocal(half_r[:, :], total[:, :]).then_inc(rsum_ready, 1)
                        dve.wait_ge(rsum_ready, y + 1)
                        dve.wait_ge(pick_ready, y + 1)
                        for e in range(2):
                            last = dve.scalar_tensor_tensor(out=gates[:, e, :], in0=pick[:, e, :], scalar=0.5,
                                                            in1=half_r[:, :], op0=ALU.mult, op1=ALU.mult)
                        last.then_inc(gates_ready, 1)
                    if live(n, NG):
                        after(dve, proj_ps, 2 * n + 2)
                        after(dve, xb_ready, n + 1)
                        for hf in range(2):
                            last = dve.tensor_tensor(xg(n, 2 * hf, 2), proj[hf], xg(n, 2 * hf, 2), ALU.add)
                        last.then_inc(x1_ready, 1)
                        dve.wait_ge(x1_ready, n + 1)
                    if live(y, NG):
                        after(dve, th_ready, y + 1)
                        dve.scalar_tensor_tensor(out=z[:, :, :], in0=th[:, :, :], scalar=1.0, in1=z[:, :, :],
                                                 op0=ALU.add, op1=ALU.mult).then_inc(u_ready, 1)
                    if live(n, NG):
                        for t in range(GT):
                            last = dve.bn_stats(st6[:, t, :], w.x[:, n * GT + t, :])
                        last.then_inc(bn_done, 1)
                        dve.wait_ge(bn_done, n + 1)

                    def add_expert(e):
                        for t in range(GT):
                            xt = w.x[:, y * GT + t, :]
                            last = dve.scalar_tensor_tensor(out=xt, in0=z[:, t, D * e:D * e + D],
                                                            scalar=gates[:, e, t:t + 1], in1=xt,
                                                            op0=ALU.mult, op1=ALU.add)
                        last.then_inc(x2_ready if e else half_done, 1)

                    if live(y, NG):
                        dve.wait_ge(u_ready, y + 1)
                        dve.wait_ge(gates_ready, y + 1)
                        dve.wait_ge(h_ready, y + 1)
                        add_expert(0)
                    if live(n, NG):
                        for t in range(GT):
                            last = dve.bn_aggr(mv[:, par, t, :], st6[:, t, :])
                        last.then_inc(mv_ready, 1)
                    if live(y, NG):
                        dve.wait_ge(half_done, y + 1)
                        add_expert(1)
                    if live(n, NG):
                        dve.wait_ge(rstd_ready, n + 1)
                        after(dve, ht_ps, 2 * (n - 1))
                        for t in range(GT):
                            last = dve.tensor_scalar(hn[:, par, t, :], w.x[:, n * GT + t, :], mv[:, par, t, 0:1],
                                                     rstd[:, par, t:t + 1], ALU.subtract, ALU.mult)
                        last.then_inc(h_ready, 1)
                pipelined(dve, NG, 3, 1, body)

            @block.scalar
            def _(act):
                def body(n, par):
                    y, yp = n - 1, 1 - par
                    if live(y, NG):
                        for c, bank in enumerate((b0, b1)):
                            after(act, ht_ps, 2 * y + c + 1)
                            if c == 0:
                                after(act, z_ps, GT * (y - 1))
                            act.activation(ht[:, yp, c, :, :], bank[:, :, :], ACT.Copy).then_inc(ht_ready, 1)
                    if live(n, NG):
                        for c, bank in enumerate((b2, b3)):
                            after(act, ctx_ps, 2 * n + c + 1)
                            if c == 0:
                                after(act, proj_ps, 2 * (n - 1))
                            act.activation(ct[:, par, c, :, :], bank[:, :, :], ACT.Copy).then_inc(ct_ready, 1)
                    if live(y, NG):
                        after(act, z_read, GT * y + GT)
                        after(act, u_ready, y)
                        act.activation(th[:, :, :], z[:, :, :], ACT.Tanh, scale=0.5).then_inc(th_ready, 1)
                        after(act, diff_ready, y + 1)
                        after(act, pick_ready, y)
                        act.activation(ex[:, :, :], diff[:, :, :], ACT.Exp).then_inc(exp_ready, 1)
                pipelined(act, NG, 3, 1, body)

            @block.tensor
            def _(pe):
                def body(n, par):
                    y, yp = n - 1, 1 - par
                    if live(y, NG):
                        after(pe, h_ready, y + 1)
                        for c, bank in enumerate((b0, b1)):
                            if c == 0:
                                after(pe, ht_ready, 2 * y - 1)
                            else:
                                after(pe, gate_read, y)
                            for t in range(GT):
                                mm = pe.transpose(bank[:, t, :], hn[:, yp, t, P * c:P * c + P], w.ident[:, :])
                            mm.then_inc(ht_ps, 1)
                    if live(n, NG):
                        after(pe, staged, n + 1)
                        after(pe, x1_ready, n)
                        for c, bank in enumerate((b2, b3)):
                            for t in range(GT):
                                mm = pe.transpose(bank[:, t, :], cs[:, par, t, P * c:P * c + P], w.ident[:, :])
                            mm.then_inc(ctx_ps, 1)
                    if live(y, NG):
                        after(pe, ht_ready, 2 * y + 2)
                        for t in range(GT):
                            after(pe, z_read, GT * (y - 1) + t + 1)
                            for c in range(C):
                                pe.matmul(lps[:, t, :], ht[:, yp, c, t, :], w.wf[:, c, 2 * D:2 * D + E],
                                          start=(c == 0), stop=(c == C - 1))
                            for c in range(C):
                                mm = pe.matmul(bz[t][:, :], ht[:, yp, c, t, :], w.wf[:, c, 0:2 * D],
                                               start=(c == 0), stop=(c == C - 1))
                            mm.then_inc(z_ps, 1)
                    if live(n, NG):
                        after(pe, ct_ready, 2 * n + 2)
                        for hf in range(2):
                            for t in range(2):
                                for c in range(C):
                                    mm = pe.matmul(proj[hf][:, t, :], ct[:, par, c, 2 * hf + t, :], wo[:, c, :],
                                                   start=(c == 0), stop=(c == C - 1))
                            mm.then_inc(proj_ps, 1)
                pipelined(pe, NG, 3, 1, body)

            @block.sync
            def _(sp):
                if out is None:
                    return
                rows = out.rearrange("b (g t p) d -> (b g) p t d", p=P, t=GT)

                def body(n, par):
                    sp.wait_ge(x2_ready, 1)
                    after(sp, x2_ready, n + 1)
                    sp.dma_start(rows[n], xg(n)).then_inc(stored, 16)
                pipelined(sp, NG, 2, 0, body)
                sp.wait_ge(stored, 16 * NG)


def prepare_b(nc, w, d):
    with Phase(nc, "pb") as ph:
        (bn_done, mv_ready, var_ready, rstd_ready, h_ready, ht_ps, ht_ready, qk_ps, qk_read, v_ps, v_read, sq_ready,
         ss_ready, ms_ready, rn_ready, qn_ready, qw_ready, part1, rest1, part2, part3, pt_ps, pt_ready, stored
         ) = [ph.sem(s) for s in (
             "bn_done mv_ready var_ready rstd_ready h_ready ht_ps ht_ready qk_ps qk_read v_ps v_read sq_ready "
             "ss_ready ms_ready rn_ready qn_ready qw_ready part1 rest1 part2 part3 pt_ps pt_ready stored").split()]
        st6 = ph.sb("st6", [P, GT, 6])
        mv = ph.sb("mv", [P, GT, 2])
        var = ph.sb("var", [P, GT])
        rstd = ph.sb("rstd", [P, GT])
        hn = ph.sb("hn", [P, GT, D])
        ht = ph.sb("ht", [P, C, GT, P])
        qk = ph.sb("qk", [P, 2, GT, 2 * D])
        sq = ph.sb("sq", [P, GT, 2 * D])
        ss = ph.sb("ss", [P, GT * 2 * H])
        ms = ph.sb("ms", [P, GT * 2 * H])
        rn = ph.sb("rn", [P, GT * 2 * H])
        pt = ph.sb("pt", [P, GT, 2 * H, PARTS, HD], BF16)
        stage = ph.sb("stage", [2 * HROWS, 2, NPAIR, GT, P], BF16)

        b0 = ph.ps("b0", [P, GT, P])
        b1 = ph.ps("b1", [P, GT, P])
        bqk = [ph.ps("bqk0", [P, 2 * D]), ph.ps("bqk1", [P, 2 * D])]
        bv = ph.ps("bv", [P, GT, D])
        bp = [ph.ps("bp0", [P, NPAIR, P], BF16), ph.ps("bp1", [P, NPAIR, P], BF16)]
        parts = [d["parts_q"], d["parts_k"]]

        def heads(tile):
            return tile.rearrange("p t (g e) -> p (t g) e", e=HD)

        def part(n):
            return pt[:, :, :, n, :].rearrange("p t g e -> p (t g) e")

        with nc.Block() as block:
            @block.gpsimd
            def _(pool):
                def body(n, par):
                    y = n - 1
                    if live(n, NG):
                        after(pool, mv_ready, n + 1)
                        pool.tensor_tensor(var[:, :], mv[:, :, 1], w.lneps[:, :], ALU.add).then_inc(var_ready, 1)
                        after(pool, var_ready, n + 1)
                        pool.tensor_tensor(rstd[:, :], var[:, :], w.minushalf[:, 0:GT], ALU.pow).then_inc(rstd_ready, 1)
                        after(pool, ss_ready, n + 1)
                        after(pool, qn_ready, n)
                        pool.tensor_tensor(ms[:, :], ss[:, :], w.rmseps[:, :], ALU.add).then_inc(ms_ready, 1)
                        after(pool, ms_ready, n + 1)
                        pool.tensor_tensor(rn[:, :], ms[:, :], w.minushalf[:, :], ALU.pow).then_inc(rn_ready, 1)
                pipelined(pool, NG, 2, 0, body)

            @block.vector
            def _(dve):
                def body(n, par):
                    y, yp = n - 1, 1 - par
                    if live(n, NG):
                        for t in range(GT):
                            last = dve.bn_stats(st6[:, t, :], w.x[:, n * GT + t, :])
                        last.then_inc(bn_done, 1)
                        dve.wait_ge(bn_done, n + 1)
                        after(dve, h_ready, n)
                    if live(y, NG):
                        after(dve, rn_ready, y + 1)
                        dve.tensor_tensor(heads(qk[:, yp, :, :]), heads(qk[:, yp, :, :]),
                                          rn[:, :].unsqueeze(2).broadcast_to([P, GT * 2 * H, HD]), ALU.mult).then_inc(qn_ready, 1)
                    if live(n, NG):
                        for t in range(GT):
                            last = dve.bn_aggr(mv[:, t, :], st6[:, t, :])
                        last.then_inc(mv_ready, 1)
                    if live(y, NG):
                        dve.wait_ge(qn_ready, y + 1)
                        for i in range(2):
                            for t in range(GT):
                                v = qk[:, yp, t, D * i:D * i + D].rearrange("p (h e) -> p h e", e=HD)
                                last = dve.tensor_tensor(v, v, w.wqk[:, i, :].unsqueeze(1).broadcast_to([P, H, HD]), ALU.mult)
                        last.then_inc(qw_ready, 1)
                    if live(n, NG):
                        dve.wait_ge(rstd_ready, n + 1)
                        after(dve, ht_ps, 2 * n)
                        for t in range(GT):
                            last = dve.tensor_scalar(hn[:, t, :], w.x[:, n * GT + t, :], mv[:, t, 0:1],
                                                     rstd[:, t:t + 1], ALU.subtract, ALU.mult)
                        last.then_inc(h_ready, 1)
                    if live(y, NG):
                        dve.wait_ge(part1, y + 1)
                        dve.tensor_tensor(heads(sq[:, :, :]), heads(qk[:, yp, :, :]), part(0), ALU.subtract).then_inc(rest1, 1)
                        dve.wait_ge(part2, y + 1)
                        dve.tensor_tensor(part(2), heads(sq[:, :, :]), part(1), ALU.subtract).then_inc(part3, 1)
                    if live(n, NG):
                        for t in range(GT):
                            after(dve, qk_ps, GT * n + t + 1)
                            dve.tensor_tensor(qk[:, par, t, :], bqk[t % 2][:, :], w.bb[:, 0:2 * D], ALU.add).then_inc(qk_read, 1)
                        after(dve, v_ps, n + 1)
                        dve.tensor_tensor(
                            w.mix[:, n // (NG // B), :, bass.ds((n % (NG // B)) * GT, GT), :],
                            bv[:, :, :].rearrange("p t (h e) -> p h t e", h=H),
                            w.bb[:, 2 * D:3 * D].rearrange("p (h e) -> p h e", h=H).unsqueeze(2).broadcast_to([P, H, GT, HD]),
                            ALU.add).then_inc(v_read, 1)
                        after(dve, sq_ready, n + 1)
                        after(dve, ms_ready, n)
                        dve.tensor_reduce(ss[:, :], heads(sq[:, :, :]), AX.X, ALU.add).then_inc(ss_ready, 1)
                pipelined(dve, NG, 3, 1, body)

            @block.scalar
            def _(act):
                def body(n, par):
                    y, yp = n - 1, 1 - par
                    if live(n, NG):
                        for c, bank in enumerate((b0, b1)):
                            after(act, ht_ps, 2 * n + c + 1)
                            if c == 0:
                                after(act, v_ps, n)
                            act.activation(ht[:, c, :, :], bank[:, :, :], ACT.Copy).then_inc(ht_ready, 1)
                    if live(y, NG):
                        after(act, qw_ready, y + 1)
                        after(act, pt_ps, 2 * GT * y)
                        act.activation(part(0), heads(qk[:, yp, :, :]), ACT.Copy).then_inc(part1, 1)
                        after(act, rest1, y + 1)
                        act.activation(part(1), heads(sq[:, :, :]), ACT.Copy).then_inc(part2, 1)
                    if live(n, NG):
                        after(act, qk_read, GT * n + GT)
                        after(act, part3, n)
                        act.activation(sq[:, :, :], qk[:, par, :, :], ACT.Square).then_inc(sq_ready, 1)
                    if live(y, NG):
                        after(act, stored, 32 * y)
                        for t in range(GT):
                            for i in range(2):
                                after(act, pt_ps, 2 * GT * y + 2 * t + i + 1)
                                act.activation(stage[:, i, :, t, :], bp[i][0:2 * HROWS, :, :], ACT.Copy).then_inc(pt_ready, 1)
                pipelined(act, NG, 3, 1, body)

            @block.tensor
            def _(pe):
                def body(n, par):
                    y = n - 1
                    if live(n, NG):
                        after(pe, h_ready, n + 1)
                        after(pe, ht_ready, 2 * n)
                        for c, bank in enumerate((b0, b1)):
                            for t in range(GT):
                                mm = pe.transpose(bank[:, t, :], hn[:, t, P * c:P * c + P], w.ident[:, :])
                            mm.then_inc(ht_ps, 1)
                        after(pe, ht_ready, 2 * n + 2)
                        for t in range(GT):
                            after(pe, qk_read, GT * n + t - 1)
                            for c in range(C):
                                mm = pe.matmul(bqk[t % 2][:, :], ht[:, c, t, :], w.wb[:, c, 0:2 * D],
                                               start=(c == 0), stop=(c == C - 1))
                            mm.then_inc(qk_ps, 1)
                        after(pe, v_read, n)
                        for t in range(GT):
                            for c in range(C):
                                mm = pe.matmul(bv[:, t, :], ht[:, c, t, :], w.wb[:, c, 2 * D:3 * D],
                                               start=(c == 0), stop=(c == C - 1))
                        mm.then_inc(v_ps, 1)
                    if live(y, NG):
                        after(pe, part3, y + 1)
                        for t in range(GT):
                            for i in range(2):
                                after(pe, pt_ready, 2 * GT * y + 2 * t + i - 1)
                                for g in range(NPAIR):
                                    h = H * i + 2 * g
                                    mm = pe.transpose(
                                        bp[i][0:2 * HROWS, g, :],
                                        pt[:, t, h:h + 2, :, :].rearrange("p h n e -> p (h n e)"), w.identb[:, :])
                                mm.then_inc(pt_ps, 1)
                pipelined(pe, NG, 3, 1, body)

            @block.sync
            def _(sp):
                def body(n, par):
                    sp.wait_ge(pt_ready, 2 * GT)
                    after(sp, pt_ready, 2 * GT * (n + 1))
                    for i in range(2):
                        rows = parts[i].rearrange("(b g h) r (s c) -> b s (h r) g c", b=B, h=2, s=NG // B)
                        sp.dma_start(rows[n // (NG // B), n % (NG // B)],
                                     stage[:, i, :, :, :].rearrange("p g t c -> p g (t c)")).then_inc(stored, 16)
                pipelined(sp, NG, 2, 0, body)
                sp.wait_ge(stored, 32 * NG)


def load_stacks(sp, d, hh, qs, ks, sem):
    q, k = d["parts_q"][hh], d["parts_k"][hh]
    sp.dma_start(qs[0:HROWS, :], q).then_inc(sem, 16)
    sp.dma_start(qs[HROWS:HROWS + 2 * HD, :], q[0:2 * HD, :]).then_inc(sem, 16)
    sp.dma_start(qs[HROWS + 2 * HD:SROWS, :], q[0:HD, :]).then_inc(sem, 16)
    sp.dma_start(qs[SROWS:KROWS, :], d["mrow"][bass.ds(hh, 1), :]).then_inc(sem, 16)
    row = 0
    for n, copies in enumerate((3, 2, 1)):
        for _ in range(copies):
            sp.dma_start(ks[row:row + HD, :], k[HD * n:HD * n + HD, :]).then_inc(sem, 16)
            row += HD


STACK_DMAS = 10


def score_maxima(nc, w, d):
    with Phase(nc, "mx") as ph:
        loaded, ones, s_ps, s_read, neg_ready, t_ps, row_ready, stored = [ph.sem(s) for s in (
            "loaded ones s_ps s_read neg_ready t_ps row_ready stored").split()]
        qs = ph.sb("qs", [KROWS, T], BF16)
        ks = ph.sb("ks", [KROWS, T], BF16)
        neg = ph.sb("neg", [P, KT])
        row = ph.sb("row", [KT, P], BF16)
        sps = ph.ps("sps", [P, T])
        tps = ph.ps("tps", [KT, P])
        with nc.Block() as block:
            @block.sync
            def _(sp):
                unbounded = sp.value_load(w.flag[0:1, 0:1], min_val=0, max_val=1)
                with sp.If(unbounded > 0):
                    sp.sem_inc(stored, 16)
                    with sp.Fori(0, B * H) as hh:
                        load_stacks(sp, d, hh, qs, ks, loaded)
                        sp.wait_ge(row_ready, hh + 1)
                        sp.dma_start(d["mrow"][bass.ds(hh, 1), :].rearrange("a (t p) -> (a t) p", p=P), row[:, :]).then_inc(stored, 16)
                    sp.wait_ge(stored, 16 * B * H + 16)
                    sp.nop()

            @block.gpsimd
            def _(pool):
                pool.memset(ks[SROWS:KROWS, :], 1.0).then_inc(ones, 1)

            @block.tensor
            def _(pe):
                unbounded = pe.value_load(w.flag[0:1, 0:1], min_val=0, max_val=1)
                with pe.If(unbounded > 0):
                    pe.wait_ge(ones, 1)
                    with pe.Fori(0, B * H) as hh:
                        pe.wait_ge(loaded, 16 * STACK_DMAS * (hh + 1))
                        for t in range(KT):
                            if t:
                                pe.wait_ge(s_read, KT * hh + t)
                            for c in range(4):
                                mm = pe.matmul(sps[:, 512 * c:512 * c + 512], qs[:, P * t:P * t + P],
                                               ks[:, 512 * c:512 * c + 512], start=True, stop=True)
                            mm.then_inc(s_ps, 1)
                        pe.wait_ge(neg_ready, hh + 1)
                        pe.transpose(tps[:, :], neg[:, :], w.ident[:, :]).then_inc(t_ps, 1)
                    pe.nop()

            @block.vector
            def _(dve):
                unbounded = dve.value_load(w.flag[0:1, 0:1], min_val=0, max_val=1)
                with dve.If(unbounded > 0):
                    with dve.Fori(0, B * H) as hh:
                        for t in range(KT):
                            dve.wait_ge(s_ps, KT * hh + t + 1)
                            ins = dve.tensor_reduce(neg[:, t:t + 1], sps[:, :], AX.X, ALU.max, negate=True)
                            ins.then_inc(s_read if t < KT - 1 else neg_ready, 1)
                            if t == KT - 1:
                                dve.wait_ge(neg_ready, hh + 1)
                                dve.sem_inc(s_read, 1)
                        dve.wait_ge(t_ps, hh + 1)
                        dve.wait_ge(stored, 16 * hh + 16)
                        dve.tensor_copy(row[:, :], tps[:, :]).then_inc(row_ready, 1)
                    dve.nop()


def attention_b(nc, w, d):
    with Phase(nc, "sa") as ph:
        loaded = [ph.sem("loaded0"), ph.sem("loaded1")]
        cleared, ones_ready, v_ready, s_ps, p_ready, z_ps, zt_ready, ztok_ps, rden_ready, z_ready = [ph.sem(s) for s in (
            "cleared ones_ready v_ready s_ps p_ready z_ps zt_ready ztok_ps rden_ready z_ready").split()]
        QC = 4
        W = T // QC
        UNITS = KT * QC
        SIZES = [3] * 10 + [2] + [3] * 10 + [2]
        GROUPS = len(SIZES)
        starts = [sum(SIZES[:g]) for g in range(GROUPS)]
        PB = 4
        qs = [ph.sb(f"qs{i}", [KROWS, T], BF16) for i in range(2)]
        ks = [ph.sb(f"ks{i}", [KROWS, T], BF16) for i in range(2)]
        vs = ph.sb("vs", [P, 2, KT, V1])
        pr = ph.sb("pr", [P, PB, 3, W])
        zt = ph.sb("zt", [P, QC, P])
        rden = ph.sb("rden", [P, QC, 4])
        bs = [ph.ps("bs0", [P, 3, W]), ph.ps("bs1", [P, 3, W])]
        bz = [ph.ps("bz0", [P, 4, P]), ph.ps("bz1", [P, 4, P])]
        heads = w.mix[:, :, :, :, :].rearrange("p b h t e -> p (b h) t e")
        LAG = 2
        fours = [(starts[g - LAG] + SIZES[g - LAG]) // QC if g >= LAG else 0 for g in range(GROUPS)]
        last_four = [(starts[g] + SIZES[g] - 1) // QC for g in range(GROUPS)]
        N = B * H

        with nc.Block() as block:
            @block.sync
            def _(sp):
                def body(n, par):
                    if not isinstance(n, int):
                        sp.wait_ge(s_ps, GROUPS)
                    after(sp, s_ps, GROUPS * (n - 1))
                    load_stacks(sp, d, n, qs[par], ks[par], loaded[par])
                pipelined(sp, N, 2, 0, body)

            @block.gpsimd
            def _(pool):
                pool.memset(vs[:, :, :, :], 1.0).then_inc(ones_ready, 1)
                pool.wait_ge(ones_ready, 1)

                def body(n, par):
                    after(pool, z_ps, KT * (n - 1))
                    pool.tensor_copy(vs[:, par, :, 0:HD], heads[:, n, :, :]).then_inc(v_ready, 1)
                pipelined(pool, N, 2, 0, body)

            @block.scalar
            def _(act):
                def body(n, par):
                    for g in range(GROUPS):
                        at = GROUPS * n + g
                        act.wait_ge(s_ps, at + 1)
                        if g >= PB:
                            act.wait_ge(z_ps, KT * n + last_four[g - PB] + 1)
                        else:
                            after(act, z_ps, KT * (n - 1) + last_four[g - PB + GROUPS] + 1)
                        s = SIZES[g]
                        act.activation(pr[:, (GROUPS * par + g) % PB, 0:s, :], bs[g % 2][:, 0:s, :], ACT.Exp).then_inc(p_ready, 1)
                pipelined(act, N, 2, 0, body)

            @block.vector
            def _(dve):
                for i in range(2):
                    dve.memset(ks[i][SROWS:KROWS, :], 1.0).then_inc(cleared, 1)
                    dve.memset(bz[i][:, :, :], 0.0).then_inc(cleared, 1)

                def body(n, par):
                    after(dve, z_ps, KT * (n + 1))
                    after(dve, ztok_ps, n)
                    dve.tensor_copy(zt[:, :, :], bz[par][:, :, :]).then_inc(zt_ready, 1)
                    after(dve, ztok_ps, n + 1)
                    tok = bz[par][:, :, :].rearrange("p i (j s) -> p i j s", j=QC)
                    dve.reciprocal(rden[:, :, :], tok[:, :, :, HD]).then_inc(rden_ready, 1)
                    dve.wait_ge(rden_ready, n + 1)
                    dve.tensor_tensor(heads[:, n, :, :].rearrange("p (j i) e -> p i j e", j=QC), tok[:, :, :, 0:HD],
                                      rden[:, :, :].unsqueeze(3).broadcast_to([P, QC, 4, HD]), ALU.mult).then_inc(z_ready, 1)
                pipelined(dve, N, 2, 0, body)

            @block.tensor
            def _(pe):
                pe.wait_ge(cleared, 4)

                def products(n, par, lo, hi):
                    for f in range(lo, hi):
                        for j in range(QC):
                            u = QC * f + j
                            g = max(i for i in range(GROUPS) if starts[i] <= u)
                            buf = (GROUPS * par + g) % PB
                            mm = pe.matmul(bz[par][32 * j:32 * j + V1, :, :], vs[:, par, f, :],
                                           pr[:, buf, u - starts[g], :], start=(f == 0), stop=(f == KT - 1))
                        mm.then_inc(z_ps, 1)

                def tokens(n, par):
                    after(pe, zt_ready, n + 1)
                    for i in range(4):
                        mm = pe.transpose(bz[par][:, i, :], zt[:, i, :], w.ident[:, :])
                    mm.then_inc(ztok_ps, 1)

                def body(n, par):
                    done = 0
                    for g in range(GROUPS):
                        if g == 0:
                            pe.wait_ge(loaded[par], 16 * STACK_DMAS * ((n - par) // 2 + 1) if isinstance(n, int)
                                       else 8 * STACK_DMAS * (n - par) + 16 * STACK_DMAS)
                        after(pe, p_ready, GROUPS * n + g - 1)
                        for u in range(starts[g], starts[g] + SIZES[g]):
                            t, j = divmod(u, QC)
                            mm = pe.matmul(bs[g % 2][:, u - starts[g], :], ks[par][:, P * t:P * t + P],
                                           qs[par][:, W * j:W * j + W], start=True, stop=True)
                        mm.then_inc(s_ps, 1)
                        if g < LAG and live(n - 1, N):
                            products(n - 1, 1 - par, tail[g], tail[g + 1])
                        if g == 4 and live(n - 1, N):
                            tokens(n - 1, 1 - par)
                        if g == LAG:
                            after(pe, v_ready, n + 1)
                            after(pe, z_ready, n - 1)
                        products(n, par, done, fours[g])
                        done = max(done, fours[g])

                tail = [fours[GROUPS - 1]] + [(starts[g] + SIZES[g]) // QC for g in (GROUPS - 2, GROUPS - 1)]

                pipelined(pe, N, 2, 0, body)
                for g in range(LAG):
                    pe.wait_ge(p_ready, GROUPS * N - (LAG - 1) + g)
                    products(N - 1, (N - 1) % 2, tail[g], tail[g + 1])
                tokens(N - 1, (N - 1) % 2)


class Kept:
    pass


def build(nc, d, out):
    with ExitStack() as ctx:
        def sb(name, shape, dt=F32):
            return ctx.enter_context(nc.sbuf_tensor(name, shape, dt))

        w = Kept()
        w.x = sb("x", [P, NT, D])
        w.mix = sb("mix", [P, B, H, TB, HD])
        w.wa = sb("wa", [P, C, 3 * D])
        w.wb = sb("wb", [P, C, 3 * D])
        w.woa = sb("woa", [P, C, D])
        w.wob = sb("wob", [P, C, D])
        w.wf = sb("wf", [P, C, 2 * D + E])
        w.ba = sb("ba", [P, 3 * D])
        w.bb = sb("bb", [P, 3 * D])
        w.boa = sb("boa", [P, D])
        w.bob = sb("bob", [P, D])
        w.bf = sb("bf", [P, 2 * D])
        w.wqk = sb("wqk", [P, 2, HD])
        w.omega = sb("omega", [P, C, H // C * FD])
        w.ident = sb("ident", [P, P])
        w.identb = sb("identb", [P, P], BF16)
        w.mask = sb("mask", [P, P])
        w.minushalf = sb("minushalf", [P, GT * 2 * H])
        w.lneps = sb("lneps", [P, GT])
        w.rmseps = sb("rmseps", [P, GT * 2 * H])
        w.one = sb("one", [P, 1])
        w.keep = sb("keep", [P, NT])
        w.fnode = sb("fnode", [P, 1])
        w.fweight = sb("fweight", [P, 1])
        w.flo = sb("flo", [P, 1])
        w.fhi = sb("fhi", [P, 1])
        w.fneg = sb("fneg", [P, 1])
        w.fscale = sb("fscale", [P, 1])
        w.flag = sb("flag", [1, 1], I32)
        setup(nc, w, d)
        attention_a(nc, w, d)
        project_and_ffn(nc, w, d, "f1", w.woa, w.boa, None)
        prepare_b(nc, w, d)
        score_maxima(nc, w, d)
        attention_b(nc, w, d)
        project_and_ffn(nc, w, d, "f2", w.wob, w.bob, out)


_NAMES = ["L0_attn_a_x", "L0_attn_a_Wqkv", "L0_attn_a_bqkv", "L0_attn_a_Wout", "L0_attn_a_bout", "L0_attn_a_omega",
          "L0_attn_a_quad_nodes", "L0_attn_a_quad_weights", "L0_attn_b_bqkv", "L0_attn_b_bo", "L0_attn_b_wq",
          "L0_attn_b_wk", "L0_ffn_gate_w", "L0_ffn_b0", "L0_ffn_b1"]
_TRANSPOSED = {"attn_b_WqkvT": "L0_attn_b_Wqkv", "attn_b_WoT": "L0_attn_b_Wo", "ffn_w0T": "L0_ffn_w0",
               "ffn_w1T": "L0_ffn_w1"}


def kernel(**inputs):
    import concourse.bacc as bacc
    from concourse.bass_utils import run_bass_kernel_spmd

    nc = bacc.Bacc("TRN2", target_bir_lowering=False, num_devices=1)
    arrays = {name: np.ascontiguousarray(inputs[name]) for name in _NAMES}
    arrays.update({name: np.ascontiguousarray(np.asarray(inputs[src]).T) for name, src in _TRANSPOSED.items()})
    d = {name: nc.dram_tensor(f"in_{name}", a.shape, mybir.dt.from_np(a.dtype), kind="ExternalInput").ap()
         for name, a in arrays.items()}
    d["parts_q"] = nc.dram_tensor("parts_q", (B * H, HROWS, T), BF16, kind="Internal").ap()
    d["parts_k"] = nc.dram_tensor("parts_k", (B * H, HROWS, T), BF16, kind="Internal").ap()
    d["mrow"] = nc.dram_tensor("mrow", (B * H, T), BF16, kind="Internal").ap()
    out = nc.dram_tensor("out", (B, T, D), F32, kind="ExternalOutput").ap()
    build(nc, d, out)
    r = run_bass_kernel_spmd(nc, [{f"in_{name}": a for name, a in arrays.items()}], core_ids=[0])
    return r.results[0]["out"]
```

```python
from contextlib import ExitStack

import numpy as np

import concourse.bass as bass
from concourse import mybir

F32 = mybir.dt.float32
BF16 = mybir.dt.bfloat16
I32 = mybir.dt.int32
ALU = mybir.AluOpType
ACT = mybir.ActivationFunctionType
AX = mybir.AxisListType

P = 128
B, T, D = 2, 2048, 256
H = 16
HD = D // H
M, R = 32, 2
FD = R * M
NPAIR = H // 2
NT = B * T // P
TB = T // P
GT = 4
NG = NT // GT
C = D // P
V1 = HD + 1
E = 8
ZW = D + E // 2
LN_EPS = 1e-5
RMS_EPS = 1e-6
NORM_FLOOR = 1e-12
CLIP = 20.0
DEN_FLOOR = 1e-6
SAFE_SCORE = 60.0
PARTS = 3
HROWS = PARTS * HD
SROWS = 2 * HROWS
KROWS = SROWS + 1
KT = T // P


def after(eng, sem, count):
    if isinstance(count, int) and count <= 0:
        return
    eng.wait_ge(sem, count)


def live(i, n):
    return not isinstance(i, int) or 0 <= i < n


def pipelined(eng, n, lead, tail, body):
    for i in range(lead):
        body(i, i % 2)
    turns = (n - lead) // 2
    with eng.Fori(0, turns) as q:
        for u in range(2):
            body(2 * q + (lead + u), (lead + u) % 2)
    for i in range(lead + 2 * turns, n + tail):
        body(i, i % 2)


class Phase:

    def __init__(self, nc, tag):
        self.nc, self.tag, self.ctx, self.sems = nc, tag, ExitStack(), []

    def __enter__(self):
        self.ctx.__enter__()
        return self

    def __exit__(self, *e):
        self.nc.clear_and_free_semaphores(self.sems)
        self.nc.all_engine_barrier()
        return self.ctx.__exit__(*e)

    def sb(self, name, shape, dt=F32):
        return self.ctx.enter_context(self.nc.sbuf_tensor(f"{self.tag}_{name}", shape, dt))

    def ps(self, name, shape, dt=F32):
        return self.ctx.enter_context(self.nc.psum_tensor(f"{self.tag}_{name}", shape, dt))

    def sem(self, name):
        self.sems.append(self.nc.alloc_semaphore(f"{self.tag}_{name}"))
        return self.sems[-1]


def setup(nc, w, d):
    with Phase(nc, "setup") as ph:
        loaded = ph.sem("loaded")
        zeroed = ph.sem("zeroed")
        diagonal = ph.sem("diagonal")
        mrow_out = ph.sem("mrow_out")
        derived = ph.sem("derived")
        rooted = ph.sem("rooted")
        omega_in = ph.sem("omega_in")
        zrow = ph.sb("zrow", [32, T], BF16)
        roots = ph.sb("roots", [P, R])
        nodes = ph.sb("nodes", [P, R])
        half = ph.sb("half", [P, R])
        bothw = ph.sb("bothw", [P, 2, HD])
        wrow = ph.sb("wrow", [1, 3, HD])
        top = ph.sb("top", [1, 1])

        def row(src, n=P):
            return src.unsqueeze(0).broadcast_to([n] + list(src.shape))

        loads = [
            (w.wa[:, :, :], d["L0_attn_a_Wqkv"].rearrange("(c p) n -> p c n", p=P)),
            (w.wb[:, :, :], d["attn_b_WqkvT"].rearrange("(c p) n -> p c n", p=P)),
            (w.woa[:, :, :], d["L0_attn_a_Wout"].rearrange("(c p) n -> p c n", p=P)),
            (w.wob[:, :, :], d["attn_b_WoT"].rearrange("(c p) n -> p c n", p=P)),
            (w.wf[:, :, 0:D], d["ffn_w0T"].rearrange("(c p) n -> p c n", p=P)),
            (w.wf[:, :, D:ZW], d["L0_ffn_gate_w"][:, 0:E // 2].rearrange("(c p) n -> p c n", p=P)),
            (w.wf[:, :, ZW:ZW + D], d["ffn_w1T"].rearrange("(c p) n -> p c n", p=P)),
            (w.wf[:, :, ZW + D:2 * ZW], d["L0_ffn_gate_w"][:, E // 2:E].rearrange("(c p) n -> p c n", p=P)),
            (w.ba[:, :], row(d["L0_attn_a_bqkv"])),
            (w.bb[:, :], row(d["L0_attn_b_bqkv"])),
            (w.boa[:, :], row(d["L0_attn_a_bout"])),
            (w.bob[:, :], row(d["L0_attn_b_bo"])),
            (w.bf[:, 0, 0:D], row(d["L0_ffn_b0"])),
            (w.bf[:, 1, 0:D], row(d["L0_ffn_b1"])),
            (bothw[:, 0, :], row(d["L0_attn_b_wq"])),
            (bothw[:, 1, :], row(d["L0_attn_b_wk"])),
            (wrow[0:1, 0, :], row(d["L0_attn_b_wq"], 1)),
            (wrow[0:1, 1, :], row(d["L0_attn_b_wk"], 1)),
            (nodes[:, :], row(d["L0_attn_a_quad_nodes"])),
        ]
        for q in range(P // M):
            r = q % R
            part = slice(M * q, M * q + M)
            loads.append((w.fnode[part, 0:1], row(d["L0_attn_a_quad_nodes"][r:r + 1], M)))
            loads.append((w.fweight[part, 0:1], row(d["L0_attn_a_quad_weights"][r:r + 1], M)))

        with nc.Block() as block:
            @block.sync
            def _(sp):
                for dst, src in loads:
                    sp.dma_start(dst, src).then_inc(loaded, 16)
                sp.wait_ge(zeroed, 2)
                for h in range(H):
                    c, hh = divmod(h, H // C)
                    sp.dma_start(
                        w.omega[HD * hh:HD * hh + HD, c, FD * hh:FD * hh + FD].rearrange("d (r m) -> d r m", r=R),
                        d["L0_attn_a_omega"][:, h].rearrange("r d m -> d r m"),
                    ).then_inc(omega_in, 16)
                sp.dma_start(d["mrow"], zrow[:, :]).then_inc(mrow_out, 16)
                sp.wait_ge(mrow_out, 16)

            @block.gpsimd
            def _(pool):
                pool.memset(w.omega[:, :, :], 0.0).then_inc(zeroed, 1)
                pool.memset(zrow[:, :], 0.0).then_inc(zeroed, 1)
                pool.memset(w.ident[:, :], 0.0).then_inc(zeroed, 1)
                pool.memset(w.mask[:, :], 1.0).then_inc(zeroed, 1)
                pool.memset(w.minushalf[:, :], -0.5).then_inc(zeroed, 1)
                pool.memset(half[:, :], 0.5).then_inc(zeroed, 1)
                pool.memset(w.keep[:, :], 1.0).then_inc(zeroed, 1)
                pool.memset(w.lneps[:, :], LN_EPS).then_inc(zeroed, 1)
                pool.memset(w.bf[:, :, D:ZW], 0.0).then_inc(zeroed, 1)
                pool.memset(w.minusone[:, :], -1.0).then_inc(zeroed, 1)
                pool.memset(w.three[:, :], 3.0).then_inc(zeroed, 1)
                pool.memset(w.one[:, :], 1.0).then_inc(zeroed, 1)
                pool.wait_ge(zeroed, 12)
                pool.memset(w.keep[:, TB - 1:TB], 0.0)
                pool.affine_select(out=w.ident[:, :], in_=w.ident[:, :], compare_op=ALU.not_equal, fill=1.0,
                                   base=0, pattern=[[-1, P]], channel_multiplier=1).then_inc(diagonal, 1)
                pool.affine_select(out=w.mask[:, :], in_=w.mask[:, :], compare_op=ALU.is_ge, fill=0.0,
                                   base=0, pattern=[[1, P]], channel_multiplier=-1)
                pool.wait_ge(derived, 1)
                pool.tensor_tensor(roots[:, :], nodes[:, :], half[:, :], ALU.pow).then_inc(rooted, 1)

            @block.vector
            def _(dve):
                dve.wait_ge(loaded, 16 * len(loads))
                dve.tensor_scalar(nodes[:, :], nodes[:, :], 0.0, 2.0, ALU.max, ALU.mult).then_inc(derived, 1)
                dve.tensor_scalar(w.flo[:, :], w.fnode[:, :], -CLIP, None, ALU.add)
                dve.tensor_scalar(w.fhi[:, :], w.fnode[:, :], CLIP, None, ALU.add)
                dve.tensor_scalar(w.fneg[:, :], w.fnode[:, :], -1.0, None, ALU.mult)
                dve.tensor_scalar(w.fscale[:, :], w.fweight[:, :], 0.0, 1.0 / M, ALU.max, ALU.mult)
                dve.scalar_tensor_tensor(out=w.wqk[:, :], in0=bothw[:, 0, :], scalar=float(HD), in1=bothw[:, 1, :],
                                         op0=ALU.mult, op1=ALU.mult)
                dve.wait_ge(diagonal, 1)
                dve.tensor_copy(w.identb[:, :], w.ident[:, :])
                dve.tensor_tensor(wrow[:, 2, :], wrow[:, 0, :], wrow[:, 1, :], ALU.mult).then_inc(derived, 1)
                dve.wait_ge(derived, 2)
                dve.tensor_reduce(top[:, :], wrow[:, 2, :], AX.X, ALU.max, apply_absolute_value=True).then_inc(derived, 1)
                dve.wait_ge(derived, 3)
                dve.tensor_scalar(w.flag[:, :], top[:, :], SAFE_SCORE / HD, None, ALU.is_gt)
                dve.wait_ge(rooted, 1)
                dve.wait_ge(omega_in, 16 * H)
                om = w.omega[:, :, :].rearrange("p c (h r m) -> p (c h) r m", r=R, m=M)
                for r in range(R):
                    dve.tensor_scalar(om[:, :, r, :], om[:, :, r, :], roots[:, r:r + 1], None, ALU.mult)


def attention_a(nc, w, d):
    with Phase(nc, "la") as ph:
        x_in = [ph.sem("x_in0"), ph.sem("x_in1")]
        (cleared, bn_done, mv_ready, var_ready, rstd_ready, h_ready, ht_ps, ht_ready, qkv_ps, qkv_read, sq_ready,
         ss_ready, ssm_ready, rn_ready, qn_ready, qkt_ps, qkt_ready, pq_ps, argq_ready, qf_ready, pk_ps, argk_ready,
         kexp_ready, kf_ready, kt_ps, kt_ready, at_ps, at_ready, ctx_ps, st_ps, st_ready, s_ps, s_ready, ct_ready,
         ctok_ps, den_ready, rden_ready, ctx_ready, vb_ready) = [ph.sem(s) for s in (
             "cleared bn_done mv_ready var_ready rstd_ready h_ready ht_ps ht_ready qkv_ps qkv_read sq_ready "
             "ss_ready ssm_ready rn_ready qn_ready qkt_ps qkt_ready pq_ps argq_ready qf_ready pk_ps argk_ready "
             "kexp_ready kf_ready kt_ps kt_ready at_ps at_ready ctx_ps st_ps st_ready s_ps s_ready ct_ready "
             "ctok_ps den_ready rden_ready ctx_ready vb_ready").split()]

        st6 = ph.sb("st6", [P, 2, 6])
        mv = ph.sb("mv", [P, 2, 2])
        var = ph.sb("var", [P, 2, 1])
        rstd = ph.sb("rstd", [P, 2, 1])
        hn = ph.sb("hn", [P, 2, D])
        ht = ph.sb("ht", [P, 2, C, P])
        qk = ph.sb("qk", [P, 2, 2 * D])
        vs = ph.sb("vs", [P, 2, D])
        vb = ph.sb("vb", [P, 2, H, V1])
        sq = ph.sb("sq", [P, 2 * D])
        ss = ph.sb("ss", [P, 2, 2 * H])
        ssm = ph.sb("ssm", [P, 2, 2 * H])
        rn = ph.sb("rn", [P, 2, 2 * H])
        qn = ph.sb("qn", [P, 2, 2 * D])
        qkt = ph.sb("qkt", [P, 2, 2 * C, P])
        argq = ph.sb("argq", [P, NPAIR, P])
        argk = ph.sb("argk", [P, NPAIR, P])
        kexp = ph.sb("kexp", [P, NPAIR, P])
        qf = ph.sb("qf", [P, 2, NPAIR, 2, P])
        kf = ph.sb("kf", [P, 2, NPAIR, P])
        kt = ph.sb("kt", [P, 2, NPAIR, P])
        at = ph.sb("at", [P, 2, NPAIR, 2, P])
        stt = ph.sb("stt", [P, 4, P])
        state = ph.sb("state", [P, H, V1])
        ct = ph.sb("ct", [P, 4, P])
        den = ph.sb("den", [P, 2, H])
        rden = ph.sb("rden", [P, 2, H])

        b0 = ph.ps("b0", [P, 4, P])
        b1 = ph.ps("b1", [P, 2 * D])
        b2 = ph.ps("b2", [P, 2 * D])
        b34 = ph.ps("b34", [P, NPAIR, P])
        b5 = ph.ps("b5", [P, 4, P])
        b6 = ph.ps("b6", [P, 4, P])
        b7 = ph.ps("b7", [P, 4, P])
        b56 = [b5, b6]

        xs = d["L0_attn_a_x"].rearrange("b (t p) d -> (b t) p d", p=P)
        mix = w.mix[:, :, :, :, :]

        def slots(bank):
            return bank[:, :, :].rearrange("p g (j s) -> p g j s", j=4)

        with nc.Block() as block:
            @block.sync
            def _(sp):
                def body(n, par):
                    if not isinstance(n, int):
                        sp.wait_ge(x_in[par], 16)
                    after(sp, x_in[par], 16 * ((n - par) // 2) if isinstance(n, int) else 8 * (n - par))
                    sp.dma_start(w.x[:, n, :], xs[n]).then_inc(x_in[par], 16)
                pipelined(sp, NT, 4, 0, body)

            @block.gpsimd
            def _(pool):
                pool.memset(vb[:, :, :, :], 1.0).then_inc(cleared, 1)
                pool.memset(qf[:, :, :, :, :], 0.0).then_inc(cleared, 1)
                pool.memset(state[:, :, :], 0.0).then_inc(cleared, 1)
                pool.wait_ge(cleared, 3)

                def body(n, par):
                    i, j = n - 1, n - 2
                    if live(j, NT):
                        after(pool, qkv_read, j + 1)
                        after(pool, ctx_ps, j - 1)
                        pool.tensor_tensor(vb[:, par, :, 0:HD], vs[:, par, :].rearrange("p (h e) -> p h e", h=H),
                                           w.one[:, 0:1].unsqueeze(2).broadcast_to([P, H, HD]), ALU.mult).then_inc(vb_ready, 1)
                    if live(i, NT):
                        after(pool, qkv_read, i + 1)
                        after(pool, ss_ready, i)
                        pool.tensor_tensor(sq[:, :], qk[:, 1 - par, :], qk[:, 1 - par, :], ALU.mult).then_inc(sq_ready, 1)
                        after(pool, ssm_ready, i + 1)
                        after(pool, qn_ready, i - 1)
                        pool.tensor_tensor(rn[:, 1 - par, :], ssm[:, 1 - par, :], w.minushalf[:, 0:2 * H], ALU.pow).then_inc(rn_ready, 1)
                    if live(n, NT):
                        after(pool, mv_ready, n + 1)
                        after(pool, rstd_ready, n - 1)
                        pool.tensor_tensor(var[:, par, :], mv[:, par, 1:2], w.lneps[:, 0:1], ALU.add).then_inc(var_ready, 1)
                        after(pool, var_ready, n + 1)
                        after(pool, h_ready, n - 1)
                        pool.tensor_tensor(rstd[:, par, :], var[:, par, :], w.minushalf[:, 0:1], ALU.pow).then_inc(rstd_ready, 1)
                pipelined(pool, NT, 5, 3, body)

            @block.vector
            def _(dve):
                dve.memset(b7[:, :, :], 0.0).then_inc(cleared, 1)

                def body(n, par):
                    i, j, k = n - 1, n - 2, n - 3
                    if live(j, NT):
                        after(dve, pq_ps, j + 1)
                        after(dve, qf_ready, j)
                        dve.tensor_scalar(argq[:, :, :], b34[:, :, :], w.flo[:, 0:1], w.fhi[:, 0:1],
                                          ALU.max, ALU.min).then_inc(argq_ready, 1)
                    if live(i, NT):
                        after(dve, qkv_ps, i + 1)
                        after(dve, sq_ready, i - 1)
                        dve.tensor_tensor(qk[:, 1 - par, :], b1[:, :], w.ba[:, 0:2 * D], ALU.add)
                        after(dve, vb_ready, i - 1)
                        dve.tensor_tensor(vs[:, 1 - par, :], b2[:, 0:D], w.ba[:, 2 * D:3 * D], ALU.add).then_inc(qkv_read, 1)
                    if live(j, NT):
                        after(dve, pk_ps, j + 1)
                        after(dve, kexp_ready, j)
                        dve.tensor_scalar(argk[:, :, :], b34[:, :, :], w.flo[:, 0:1], w.fhi[:, 0:1],
                                          ALU.max, ALU.min).then_inc(argk_ready, 1)
                    if live(i, NT):
                        after(dve, sq_ready, i + 1)
                        after(dve, ssm_ready, i - 1)
                        dve.tensor_reduce(ss[:, 1 - par, :], sq[:, :].rearrange("p (g e) -> p g e", e=HD),
                                          AX.X, ALU.add).then_inc(ss_ready, 1)
                        after(dve, ss_ready, i + 1)
                        dve.tensor_scalar(ssm[:, 1 - par, :], ss[:, 1 - par, :], NORM_FLOOR ** 2, None,
                                          ALU.max).then_inc(ssm_ready, 1)
                    if live(k, NT):
                        for r in range(4):
                            after(dve, at_ps, 4 * k + r + 1)
                            if r == 0:
                                after(dve, ctx_ps, k - 1)
                            dve.tensor_tensor(
                                at[:, 1 - par, 2 * r:2 * r + 2, :, :].rearrange("p g e t -> p (g e) t"),
                                b56[r % 2][:, :, :], w.mask[:, :].unsqueeze(1).broadcast_to([P, 4, P]),
                                ALU.mult).then_inc(at_ready, 1)
                            if r == 1 and live(j, NT):
                                after(dve, kexp_ready, j + 1)
                                after(dve, kt_ps, j - 1)
                                dve.tensor_scalar(kf[:, par, :, :], kexp[:, :, :], w.fscale[:, 0:1], None,
                                                  ALU.mult).then_inc(kf_ready, 1)
                    elif live(j, NT):
                        after(dve, kexp_ready, j + 1)
                        dve.tensor_scalar(kf[:, par, :, :], kexp[:, :, :], w.fscale[:, 0:1], None,
                                          ALU.mult).then_inc(kf_ready, 1)
                    if live(n, NT):
                        count = 16 * ((n - par) // 2 + 1) if isinstance(n, int) else 8 * (n - par) + 16
                        dve.wait_ge(x_in[par], count)
                        after(dve, mv_ready, n - 1)
                        dve.bn_stats(st6[:, par, :], w.x[:, n, :]).then_inc(bn_done, 1)
                        dve.wait_ge(bn_done, n + 1)
                        after(dve, rstd_ready, n - 1)
                    if live(i, NT):
                        after(dve, rn_ready, i + 1)
                        after(dve, qkt_ps, i - 1)
                        dve.tensor_tensor(
                            qn[:, 1 - par, :].rearrange("p (g e) -> p g e", e=HD),
                            qk[:, 1 - par, :].rearrange("p (g e) -> p g e", e=HD),
                            rn[:, 1 - par, :].unsqueeze(2).broadcast_to([P, 2 * H, HD]),
                            ALU.mult).then_inc(qn_ready, 1)
                    if live(n, NT):
                        dve.bn_aggr(mv[:, par, :], st6[:, par, :]).then_inc(mv_ready, 1)
                    if live(k, NT):
                        after(dve, s_ps, k + 1)
                        after(dve, ctx_ps, k + 1)
                        after(dve, s_ready, k)
                        dve.scalar_tensor_tensor(
                            out=state[:, :, :], in0=state[:, :, :], scalar=w.keep[:, bass.ds(k, 1)],
                            in1=b6[:, :, :].rearrange("p g (j s) -> p (g j) s", j=4)[:, :, 0:V1],
                            op0=ALU.mult, op1=ALU.add).then_inc(s_ready, 1)
                    if live(n, NT):
                        after(dve, rstd_ready, n + 1)
                        after(dve, ht_ps, n - 1)
                        dve.tensor_scalar(hn[:, par, :], w.x[:, n, :], mv[:, par, 0:1], rstd[:, par, :],
                                          ALU.subtract, ALU.mult).then_inc(h_ready, 1)
                    if live(k, NT):
                        after(dve, ctok_ps, k + 1)
                        tok = slots(b7)
                        kp = 1 - par
                        dve.tensor_scalar(den[:, kp, :].rearrange("p (g j) -> p g j", j=4), tok[:, :, :, HD],
                                          DEN_FLOOR, None, ALU.max).then_inc(den_ready, 1)
                        dve.wait_ge(den_ready, k + 1)
                        dve.reciprocal(rden[:, kp, :], den[:, kp, :]).then_inc(rden_ready, 1)
                        dve.wait_ge(rden_ready, k + 1)
                        out = mix[:, k // TB, :, k % TB, :].rearrange("p (g j) e -> p g j e", j=4)
                        dve.tensor_tensor(
                            out, tok[:, :, :, 0:HD],
                            rden[:, kp, :].rearrange("p (g j) -> p g j", j=4).unsqueeze(3).broadcast_to([P, 4, 4, HD]),
                            ALU.mult).then_inc(ctx_ready, 1)
                pipelined(dve, NT, 5, 3, body)

            @block.scalar
            def _(act):
                act.wait_ge(cleared, 4)

                def body(n, par):
                    i, j, k = n - 1, n - 2, n - 3
                    if live(i, NT):
                        after(act, ht_ps, i + 1)
                        after(act, qkv_ps, i - 1)
                        act.activation(ht[:, 1 - par, :, :], b0[:, 0:C, :], ACT.Copy).then_inc(ht_ready, 1)
                    if live(j, NT):
                        after(act, argq_ready, j + 1)
                        after(act, ctx_ps, j - 1)
                        act.activation(qf[0:FD, par, :, 0, :], argq[0:FD, :, :], ACT.Exp, bias=w.fneg[0:FD, 0:1])
                        act.activation(qf[FD:P, par, :, 1, :], argq[FD:P, :, :], ACT.Exp,
                                       bias=w.fneg[FD:P, 0:1]).then_inc(qf_ready, 1)
                        after(act, argk_ready, j + 1)
                        after(act, kf_ready, j)
                        act.activation(kexp[:, :, :], argk[:, :, :], ACT.Exp, bias=w.fneg[:, 0:1]).then_inc(kexp_ready, 1)
                    if live(k, NT):
                        after(act, st_ps, k + 1)
                        after(act, s_ps, k)
                        act.activation(stt[:, :, :], b5[:, :, :], ACT.Copy, scale=w.keep[:, bass.ds(k, 1)]).then_inc(st_ready, 1)
                        after(act, ctx_ps, k + 1)
                        after(act, ctok_ps, k)
                        act.activation(ct[:, :, :], b7[:, :, :], ACT.Copy).then_inc(ct_ready, 1)
                    if live(j, NT):
                        after(act, kt_ps, j + 1)
                        after(act, st_ps, j - 1)
                        act.activation(kt[:, par, :, :], b34[:, :, :], ACT.Copy).then_inc(kt_ready, 1)
                    if live(i, NT):
                        after(act, qkt_ps, i + 1)
                        after(act, pk_ps, i - 1)
                        act.activation(qkt[:, 1 - par, :, :], b0[:, :, :], ACT.Copy).then_inc(qkt_ready, 1)
                pipelined(act, NT, 5, 3, body)

            @block.tensor
            def _(pe):
                def project(half, par):
                    for g in range(NPAIR):
                        c, gg = divmod(g, NPAIR // C)
                        mm = pe.matmul(b34[:, g, :], w.omega[:, c, P * gg:P * gg + P], qkt[:, par, half + c, :],
                                       start=True, stop=True)
                    return mm

                def body(n, par):
                    i, j, k = n - 1, n - 2, n - 3
                    ip, jp, kp = 1 - par, par, 1 - par
                    if live(i, NT):
                        after(pe, h_ready, i + 1)
                        after(pe, qkt_ready, i)
                        for c in range(C):
                            mm = pe.transpose(b0[:, c, :], hn[:, ip, P * c:P * c + P], w.ident[:, :])
                        mm.then_inc(ht_ps, 1)
                    if live(j, NT):
                        after(pe, qkt_ready, j + 1)
                        after(pe, kt_ready, j)
                        project(0, jp).then_inc(pq_ps, 1)
                    if live(i, NT):
                        after(pe, ht_ready, i + 1)
                        after(pe, qkv_read, i)
                        for bank, lo, hi in ((b1, 0, 2 * D), (b2, 2 * D, 3 * D)):
                            for c in range(C):
                                mm = pe.matmul(bank[:, 0:hi - lo], ht[:, ip, c, :], w.wa[:, c, lo:hi],
                                               start=(c == 0), stop=(c == C - 1))
                        mm.then_inc(qkv_ps, 1)
                    if live(j, NT):
                        after(pe, argq_ready, j + 1)
                        project(C, jp).then_inc(pk_ps, 1)
                    if live(k, NT):
                        after(pe, kf_ready, k + 1)
                        after(pe, qf_ready, k + 1)
                        for r in range(4):
                            if r < 2:
                                after(pe, st_ready if r == 0 else s_ready, k)
                            else:
                                after(pe, at_ready, 4 * k + r - 1)
                            for g in (2 * r, 2 * r + 1):
                                mm = pe.matmul(b56[r % 2][:, 2 * (g % 2):2 * (g % 2) + 2, :], kf[:, kp, g, :],
                                               qf[:, kp, g, :, :], start=True, stop=True)
                            mm.then_inc(at_ps, 1)
                        after(pe, kt_ready, k + 1)
                        after(pe, vb_ready, k + 1)
                        after(pe, at_ready, 4 * k + 3)
                        for h in range(H):
                            q, s = divmod(h, 4)
                            mm = pe.matmul(b5[32 * s:32 * s + V1, q, :], vb[:, kp, h, :], kt[:, kp, h // 2, :],
                                           start=True, stop=True)
                        mm.then_inc(st_ps, 1)
                        after(pe, at_ready, 4 * k + 4)
                        after(pe, s_ready, k)
                        after(pe, ctx_ready, k)
                        if isinstance(k, int) and k == 0:
                            pe.wait_ge(cleared, 4)
                        for q in range(4):
                            for s in range(4):
                                h = 4 * q + s
                                pe.matmul(b7[32 * s:32 * s + V1, q, :], state[:, h, :], qf[:, kp, h // 2, h % 2, :],
                                          start=True, stop=False)
                            for s in range(4):
                                h = 4 * q + s
                                mm = pe.matmul(b7[32 * s:32 * s + V1, q, :], vb[:, kp, h, :],
                                               at[:, kp, h // 2, h % 2, :], start=False, stop=True)
                        mm.then_inc(ctx_ps, 1)
                    if live(j, NT):
                        after(pe, kf_ready, j + 1)
                        after(pe, argk_ready, j + 1)
                        for g in range(NPAIR):
                            mm = pe.transpose(b34[:, g, :], kf[:, jp, g, :], w.ident[:, :])
                        mm.then_inc(kt_ps, 1)
                    if live(k, NT):
                        after(pe, st_ready, k + 1)
                        for q in range(4):
                            mm = pe.transpose(b6[:, q, :], stt[:, q, :], w.ident[:, :])
                        mm.then_inc(s_ps, 1)
                        after(pe, ct_ready, k + 1)
                        for q in range(4):
                            mm = pe.transpose(b7[:, q, :], ct[:, q, :], w.ident[:, :])
                        mm.then_inc(ctok_ps, 1)
                    if live(i, NT):
                        after(pe, qn_ready, i + 1)
                        after(pe, ht_ready, i + 1)
                        for c in range(2 * C):
                            mm = pe.transpose(b0[:, c, :], qn[:, ip, P * c:P * c + P], w.ident[:, :])
                        mm.then_inc(qkt_ps, 1)
                pipelined(pe, NT, 5, 3, body)


def normalise(pool, w, mv, var, rstd, mr, nmr, g, sems):
    mv_ready, var_ready, rstd_ready, mr_ready, nmr_ready, h_ready = sems
    after(pool, mv_ready, g + 1)
    pool.tensor_tensor(var[:, :], mv[:, :, 1], w.lneps[:, :], ALU.add).then_inc(var_ready, 1)
    after(pool, var_ready, g + 1)
    after(pool, h_ready, g)
    pool.tensor_tensor(rstd[:, :], var[:, :], w.minushalf[:, 0:GT], ALU.pow).then_inc(rstd_ready, 1)
    after(pool, rstd_ready, g + 1)
    pool.tensor_tensor(mr[:, :], mv[:, :, 0], rstd[:, :], ALU.mult).then_inc(mr_ready, 1)
    after(pool, mr_ready, g + 1)
    pool.tensor_tensor(nmr[:, :], mr[:, :], w.minusone[:, :], ALU.mult).then_inc(nmr_ready, 1)


def project_and_ffn(nc, w, d, tag, wo, bo, out):
    with Phase(nc, tag) as ph:
        (staged, xb_ready, ctx_ps, ct_ready, proj_ps, x1_ready, bn_done, mv_ready, var_ready, rstd_ready, mr_ready,
         nmr_ready, h_ready, ht_ps, ht_ready, z_ps, z_read, th_ready, lg_ready, top_ready, diff_ready, exp_ready,
         sum_ready, rsum_ready, above_ready, count_ready, tie_ready, rank_ready, pick_ready, gates_ready, u_ready,
         half_done, x2_ready, stored) = [ph.sem(s) for s in (
             "staged xb_ready ctx_ps ct_ready proj_ps x1_ready bn_done mv_ready var_ready rstd_ready mr_ready "
             "nmr_ready h_ready ht_ps ht_ready z_ps z_read th_ready lg_ready top_ready diff_ready exp_ready "
             "sum_ready rsum_ready above_ready count_ready tie_ready rank_ready pick_ready gates_ready u_ready "
             "half_done x2_ready stored").split()]
        cs = ph.sb("cs", [P, GT, D])
        ct = ph.sb("ct", [P, C, GT, P])
        st6 = ph.sb("st6", [P, GT, 6])
        mv = ph.sb("mv", [P, GT, 2])
        var = ph.sb("var", [P, GT])
        rstd = ph.sb("rstd", [P, GT])
        mr = ph.sb("mr", [P, GT])
        nmr = ph.sb("nmr", [P, GT])
        hn = ph.sb("hn", [P, GT, D])
        ht = ph.sb("ht", [P, C, GT, P])
        z = ph.sb("z", [P, 2, GT, 2, ZW])
        th = ph.sb("th", [P, GT, 2, D])
        lg = ph.sb("lg", [P, GT, E])
        top = ph.sb("top", [P, GT])
        diff = ph.sb("diff", [P, GT, E])
        ex = ph.sb("ex", [P, GT, E])
        total = ph.sb("total", [P, GT])
        half_r = ph.sb("half_r", [P, GT])
        above = ph.sb("above", [P, GT, E])
        rank = ph.sb("rank", [P, GT])
        tie = ph.sb("tie", [P, GT])
        pick = ph.sb("pick", [P, 2, GT])
        gates = ph.sb("gates", [P, 2, GT])

        bt = [ph.ps("bt0", [P, GT, P]), ph.ps("bt1", [P, GT, P])]
        proj = [ph.ps("proj0", [P, 2, D]), ph.ps("proj1", [P, 2, D])]
        bz = [ph.ps("bz0", [P, 2, 2 * D]), ph.ps("bz1", [P, 2, 2 * D])]

        def xg(g, t0=0, n=GT):
            return w.x[:, bass.ds(g * GT + t0, n), :]

        def experts(zp):
            return z[:, zp, :, :, :].rearrange("p t e c -> p (t e) c")[:, :, 0:D]

        with nc.Block() as block:
            @block.gpsimd
            def _(pool):
                def body(n, par):
                    g = n - 1
                    if live(n, NG):
                        pool.tensor_tensor(xg(n), xg(n), bo[:, :].unsqueeze(1).broadcast_to([P, GT, D]),
                                           ALU.add).then_inc(xb_ready, 1)
                    if live(g, NG):
                        normalise(pool, w, mv, var, rstd, mr, nmr, g,
                                  (mv_ready, var_ready, rstd_ready, mr_ready, nmr_ready, h_ready))
                pipelined(pool, NG, 4, 1, body)

            @block.vector
            def _(dve):
                def body(n, par):
                    g, i, y = n - 1, n - 2, n - 3
                    zp = 1 - par
                    if live(y, NG):
                        after(dve, z_read, GT * y + GT)
                        dve.tensor_copy(lg[:, :, :].rearrange("p t (e c) -> p t e c", e=2),
                                        z[:, zp, :, :, D:ZW]).then_inc(lg_ready, 1)
                        dve.wait_ge(lg_ready, y + 1)
                        dve.tensor_reduce(top[:, :], lg[:, :, :], AX.X, ALU.max).then_inc(top_ready, 1)
                        dve.tensor_tensor(above[:, :, :], lg[:, :, :], lg[:, :, 1:2].broadcast_to([P, GT, E]),
                                          ALU.is_gt).then_inc(above_ready, 1)
                        dve.tensor_tensor(tie[:, :], lg[:, :, 0], lg[:, :, 1], ALU.is_equal).then_inc(tie_ready, 1)
                        dve.wait_ge(top_ready, y + 1)
                        after(dve, exp_ready, y)
                        dve.tensor_tensor(diff[:, :, :], lg[:, :, :], top[:, :].unsqueeze(2).broadcast_to([P, GT, E]),
                                          ALU.subtract).then_inc(diff_ready, 1)
                        dve.wait_ge(above_ready, y + 1)
                        dve.tensor_reduce(rank[:, :], above[:, :, :], AX.X, ALU.add).then_inc(count_ready, 1)
                        dve.tensor_tensor(pick[:, 0, :], lg[:, :, 0], top[:, :], ALU.is_equal)
                        dve.wait_ge(count_ready, y + 1)
                        dve.wait_ge(tie_ready, y + 1)
                        dve.tensor_tensor(rank[:, :], rank[:, :], tie[:, :], ALU.add).then_inc(rank_ready, 1)
                    if live(g, NG):
                        after(dve, proj_ps, 2 * g + 2)
                        after(dve, xb_ready, g + 1)
                        for hf in range(2):
                            last = dve.tensor_tensor(xg(g, 2 * hf, 2), proj[hf][:, :, :], xg(g, 2 * hf, 2), ALU.add)
                        last.then_inc(x1_ready, 1)
                    if live(y, NG):
                        dve.wait_ge(exp_ready, y + 1)
                        dve.tensor_reduce(total[:, :], ex[:, :, :], AX.X, ALU.add).then_inc(sum_ready, 1)
                        dve.wait_ge(rank_ready, y + 1)
                        dve.scalar_tensor_tensor(out=pick[:, 1, :], in0=rank[:, :], scalar=1.0, in1=ex[:, :, 1],
                                                 op0=ALU.is_equal, op1=ALU.mult).then_inc(pick_ready, 1)
                        dve.wait_ge(sum_ready, y + 1)
                        dve.reciprocal(half_r[:, :], total[:, :]).then_inc(rsum_ready, 1)
                    if live(g, NG):
                        dve.wait_ge(x1_ready, g + 1)
                        after(dve, mv_ready, g)
                    if live(y, NG):
                        dve.wait_ge(rsum_ready, y + 1)
                        dve.wait_ge(pick_ready, y + 1)
                        for e in range(2):
                            last = dve.scalar_tensor_tensor(out=gates[:, e, :], in0=pick[:, e, :], scalar=0.5,
                                                            in1=half_r[:, :], op0=ALU.mult, op1=ALU.mult)
                        last.then_inc(gates_ready, 1)
                    if live(g, NG):
                        for t in range(GT):
                            last = dve.bn_stats(st6[:, t, :], w.x[:, g * GT + t, :])
                        last.then_inc(bn_done, 1)
                        dve.wait_ge(bn_done, g + 1)
                        after(dve, nmr_ready, g)
                    if live(y, NG):
                        after(dve, th_ready, y + 1)
                        dve.scalar_tensor_tensor(out=experts(zp), in0=th[:, :, :, :].rearrange("p t e c -> p (t e) c"),
                                                 scalar=1.0, in1=experts(zp), op0=ALU.add, op1=ALU.mult).then_inc(u_ready, 1)
                    if live(g, NG):
                        for t in range(GT):
                            last = dve.bn_aggr(mv[:, t, :], st6[:, t, :])
                        last.then_inc(mv_ready, 1)

                    def add_expert(e):
                        for t in range(GT):
                            xt = w.x[:, y * GT + t, :]
                            last = dve.scalar_tensor_tensor(out=xt, in0=z[:, zp, t, e, 0:D],
                                                            scalar=gates[:, e, t:t + 1], in1=xt,
                                                            op0=ALU.mult, op1=ALU.add)
                        last.then_inc(x2_ready if e else half_done, 1)

                    def read_z(t):
                        after(dve, z_ps, GT * i + t + 1)
                        if t == 0:
                            after(dve, x2_ready, i - 1)
                        dve.tensor_tensor(z[:, par, t, :, :], bz[t % 2][:, :, 0:ZW], w.bf[:, :, :],
                                          ALU.add).then_inc(z_read, 1)

                    if live(y, NG):
                        dve.wait_ge(u_ready, y + 1)
                        dve.wait_ge(gates_ready, y + 1)
                        dve.wait_ge(h_ready, y + 1)
                        add_expert(0)
                    if live(i, NG):
                        read_z(0)
                        read_z(1)
                    if live(y, NG):
                        dve.wait_ge(half_done, y + 1)
                        add_expert(1)
                    if live(i, NG):
                        read_z(2)
                        read_z(3)
                pipelined(dve, NG, 4, 3, body)

            @block.scalar
            def _(act):
                def body(n, par):
                    g, i, y = n - 1, n - 2, n - 3
                    if live(n, NG):
                        after(act, ctx_ps, 2 * n)
                        act.activation(cs[:, :, :].rearrange("p t (h e) -> p h t e", h=H),
                                       w.mix[:, n // (NG // B), :, bass.ds((n % (NG // B)) * GT, GT), :],
                                       ACT.Copy).then_inc(staged, 1)
                    if live(y, NG):
                        after(act, z_read, GT * y + GT)
                        after(act, u_ready, y)
                        act.activation(th[:, :, :, :].rearrange("p t e c -> p (t e) c"), experts(1 - par),
                                       ACT.Tanh, scale=0.5).then_inc(th_ready, 1)
                        after(act, diff_ready, y + 1)
                        after(act, pick_ready, y)
                        act.activation(ex[:, :, :], diff[:, :, :], ACT.Exp).then_inc(exp_ready, 1)
                    if live(i, NG):
                        for c in range(C):
                            after(act, ht_ps, 2 * i + c + 1)
                            if c == 0:
                                after(act, z_ps, GT * i)
                            act.activation(ht[:, c, :, :], bt[c][:, :, :], ACT.Copy).then_inc(ht_ready, 1)
                    if live(n, NG):
                        for c in range(C):
                            after(act, ctx_ps, 2 * n + c + 1)
                            if c == 0:
                                after(act, proj_ps, 2 * n)
                            act.activation(ct[:, c, :, :], bt[c][:, :, :], ACT.Copy).then_inc(ct_ready, 1)
                    if live(g, NG):
                        after(act, nmr_ready, g + 1)
                        after(act, ht_ps, 2 * g)
                        for t in range(GT):
                            last = act.activation(hn[:, t, :], w.x[:, g * GT + t, :], ACT.Identity,
                                                  scale=rstd[:, t:t + 1], bias=nmr[:, t:t + 1])
                        last.then_inc(h_ready, 1)
                pipelined(act, NG, 4, 3, body)

            @block.tensor
            def _(pe):
                def body(n, par):
                    g, i = n - 1, n - 2
                    if live(g, NG):
                        after(pe, ct_ready, 2 * g + 2)
                        after(pe, x1_ready, g)
                        for hf in range(2):
                            for t in range(2):
                                for c in range(C):
                                    mm = pe.matmul(proj[hf][:, t, :], ct[:, c, 2 * hf + t, :], wo[:, c, :],
                                                   start=(c == 0), stop=(c == C - 1))
                            mm.then_inc(proj_ps, 1)
                    if live(i, NG):
                        after(pe, h_ready, i + 1)
                        for c in range(C):
                            after(pe, ct_ready, min(2 * (n - 1) + c + 1, 2 * NG) if isinstance(n, int) else 2 * n + (c - 1))
                            for t in range(GT):
                                mm = pe.transpose(bt[c][:, t, :], hn[:, t, P * c:P * c + P], w.ident[:, :])
                            mm.then_inc(ht_ps, 1)
                    if live(n, NG):
                        after(pe, staged, n + 1)
                        for c in range(C):
                            after(pe, ht_ready, 2 * i + c + 1)
                            for t in range(GT):
                                mm = pe.transpose(bt[c][:, t, :], cs[:, t, P * c:P * c + P], w.ident[:, :])
                            mm.then_inc(ctx_ps, 1)
                    if live(i, NG):
                        after(pe, ht_ready, 2 * i + 2)
                        for t in range(GT):
                            after(pe, z_read, GT * i + t - 1)
                            for e in range(2):
                                for c in range(C):
                                    mm = pe.matmul(bz[t % 2][:, e, 0:ZW], ht[:, c, t, :], w.wf[:, c, ZW * e:ZW * e + ZW],
                                                   start=(c == 0), stop=(c == C - 1))
                            mm.then_inc(z_ps, 1)
                pipelined(pe, NG, 4, 2, body)

            @block.sync
            def _(sp):
                if out is None:
                    return
                rows = out.rearrange("b (g t p) d -> (b g) p t d", p=P, t=GT)

                def body(n, par):
                    sp.wait_ge(x2_ready, 1)
                    after(sp, x2_ready, n + 1)
                    sp.dma_start(rows[n], xg(n)).then_inc(stored, 16)
                pipelined(sp, NG, 2, 0, body)
                sp.wait_ge(stored, 16 * NG)


def prepare_b(nc, w, d):
    with Phase(nc, "pb") as ph:
        (bn_done, mv_ready, var_ready, rstd_ready, mr_ready, nmr_ready, h_ready, ht_ps, ht_ready, qk_ps, qk_read, v_ps,
         v_read, sq_ready, ss_ready, ms_ready, root_ready, inv_ready, square_ready, error_ready, factor_ready, rn_ready,
         qn_ready, kw_ready, part1, rest1, part2, part3, pt_ps, pt_ready) = [ph.sem(s) for s in (
             "bn_done mv_ready var_ready rstd_ready mr_ready nmr_ready h_ready ht_ps ht_ready qk_ps qk_read v_ps "
             "v_read sq_ready ss_ready ms_ready root_ready inv_ready square_ready error_ready factor_ready rn_ready "
             "qn_ready kw_ready part1 rest1 part2 part3 pt_ps pt_ready").split()]
        stored = [ph.sem("stored0"), ph.sem("stored1")]
        st6 = ph.sb("st6", [P, GT, 6])
        mv = ph.sb("mv", [P, GT, 2])
        var = ph.sb("var", [P, GT])
        rstd = ph.sb("rstd", [P, GT])
        mr = ph.sb("mr", [P, GT])
        nmr = ph.sb("nmr", [P, GT])
        hn = ph.sb("hn", [P, GT, D])
        ht = ph.sb("ht", [P, C, GT, P])
        qk = ph.sb("qk", [P, 2, GT, 2 * D])
        sq = ph.sb("sq", [P, GT, 2 * D])
        rest = ph.sb("rest", [P, GT, 2 * D])
        HG = GT // 2 * 2 * H
        ss, ms, root, inv, half_inv, square, error, factor, rn = [ph.sb(s, [P, 2, HG]) for s in (
            "ss", "ms", "root", "inv", "half_inv", "square", "error", "factor", "rn")]
        pt = ph.sb("pt", [P, 2, GT, 2 * H, PARTS, HD], BF16)
        stage = ph.sb("stage", [2 * HROWS, 2, 2, NPAIR, GT, P], BF16)

        b0 = ph.ps("b0", [P, GT, P])
        b1 = ph.ps("b1", [P, GT, P])
        bqk = [ph.ps("bqk0", [P, 2 * D]), ph.ps("bqk1", [P, 2 * D])]
        bv = ph.ps("bv", [P, GT, D])
        bp = [ph.ps("bp0", [P, NPAIR, P], BF16), ph.ps("bp1", [P, NPAIR, P], BF16)]
        parts = [d["parts_q"], d["parts_k"]]

        def heads(tile, hf):
            return tile[:, 2 * hf:2 * hf + 2, :].rearrange("p t (g e) -> p (t g) e", e=HD)

        def part(pp, n, hf):
            return pt[:, pp, 2 * hf:2 * hf + 2, :, n, :].rearrange("p t g e -> p (t g) e")

        with nc.Block() as block:
            @block.gpsimd
            def _(pool):
                def newton(k, hf):
                    after(pool, inv_ready, k + 1)
                    pool.tensor_tensor(square[:, hf, :], inv[:, hf, :], inv[:, hf, :], ALU.mult).then_inc(square_ready, 1)
                    after(pool, square_ready, k + 1)
                    pool.tensor_tensor(error[:, hf, :], square[:, hf, :], ms[:, hf, :], ALU.mult).then_inc(error_ready, 1)
                    after(pool, error_ready, k + 1)
                    pool.tensor_tensor(factor[:, hf, :], error[:, hf, :], w.three[:, 0:1].broadcast_to([P, HG]),
                                       ALU.subtract).then_inc(factor_ready, 1)
                    pool.tensor_tensor(half_inv[:, hf, :], inv[:, hf, :], w.minushalf[:, 0:1].broadcast_to([P, HG]),
                                       ALU.mult).then_inc(factor_ready, 1)
                    after(pool, factor_ready, 2 * k + 2)
                    after(pool, qn_ready, k - 1)
                    pool.tensor_tensor(rn[:, hf, :], half_inv[:, hf, :], factor[:, hf, :], ALU.mult).then_inc(rn_ready, 1)

                def weigh(y, yp, hf):
                    after(pool, qn_ready, 2 * y + hf + 1)
                    k = qk[:, yp, 2 * hf:2 * hf + 2, D:2 * D].rearrange("p t (h e) -> p t h e", e=HD)
                    for t in range(2):
                        last = pool.tensor_tensor(k[:, t], k[:, t], w.wqk[:, :].unsqueeze(1).broadcast_to([P, H, HD]), ALU.mult)
                    last.then_inc(kw_ready, 1)

                def body(n, par):
                    i, y = n - 1, n - 2
                    if live(y, NG):
                        weigh(y, par, 0)
                        newton(2 * y + 1, 1)
                    if live(n, NG):
                        normalise(pool, w, mv, var, rstd, mr, nmr, n,
                                  (mv_ready, var_ready, rstd_ready, mr_ready, nmr_ready, h_ready))
                    if live(y, NG):
                        weigh(y, par, 1)
                    if live(i, NG):
                        newton(2 * i, 0)
                pipelined(pool, NG, 4, 2, body)

            @block.vector
            def _(dve):
                def norms(k, hf):
                    after(dve, sq_ready, k + 1)
                    dve.tensor_reduce(ss[:, hf, :], heads(sq, hf), AX.X, ALU.add).then_inc(ss_ready, 1)
                    dve.wait_ge(ss_ready, k + 1)
                    after(dve, rn_ready, k - 1)
                    dve.tensor_scalar(ms[:, hf, :], ss[:, hf, :], HD * RMS_EPS, None, ALU.add).then_inc(ms_ready, 1)

                def invert(k, hf):
                    after(dve, root_ready, k + 1)
                    dve.reciprocal(inv[:, hf, :], root[:, hf, :]).then_inc(inv_ready, 1)

                def scale(y, yp, hf):
                    v = heads(qk[:, yp, :, :], hf)
                    after(dve, rn_ready, 2 * y + hf + 1)
                    dve.tensor_tensor(v, v, rn[:, hf, :].unsqueeze(2).broadcast_to([P, HG, HD]), ALU.mult).then_inc(qn_ready, 1)

                def first_rest(y, yp, hf):
                    after(dve, part1, 2 * y + hf + 1)
                    after(dve, part3, 2 * y + hf - 1)
                    dve.tensor_tensor(heads(rest, hf), heads(qk[:, yp, :, :], hf), part(yp, 0, hf), ALU.subtract).then_inc(rest1, 1)

                def last_part(y, yp, hf):
                    after(dve, part2, 2 * y + hf + 1)
                    dve.tensor_tensor(part(yp, 2, hf), heads(rest, hf), part(yp, 1, hf), ALU.subtract).then_inc(part3, 1)

                def read_qk(i, ip, t):
                    after(dve, qk_ps, GT * i + t + 1)
                    if t == 0:
                        after(dve, part1, 2 * (i - 1))
                        after(dve, rest1, 2 * (i - 1))
                    dve.tensor_tensor(qk[:, ip, t, :], bqk[t % 2][:, :], w.bb[:, 0:2 * D], ALU.add).then_inc(qk_read, 1)

                def body(n, par):
                    i, y = n - 1, n - 2
                    ip, yp = 1 - par, par
                    if live(n, NG):
                        after(dve, mv_ready, n)
                    if live(y, NG):
                        scale(y, yp, 0)
                        norms(2 * y + 1, 1)
                        invert(2 * y + 1, 1)
                    if live(n, NG):
                        for t in range(GT):
                            last = dve.bn_stats(st6[:, t, :], w.x[:, n * GT + t, :])
                        last.then_inc(bn_done, 1)
                        dve.wait_ge(bn_done, n + 1)
                        after(dve, nmr_ready, n)
                    if live(i, NG):
                        read_qk(i, ip, 0)
                    if live(n, NG):
                        for t in range(GT):
                            last = dve.bn_aggr(mv[:, t, :], st6[:, t, :])
                        last.then_inc(mv_ready, 1)
                    if live(y, NG):
                        first_rest(y, yp, 0)
                        scale(y, yp, 1)
                    if live(i, NG):
                        read_qk(i, ip, 1)
                    if live(y, NG):
                        last_part(y, yp, 0)
                    if live(i, NG):
                        norms(2 * i, 0)
                    if live(y, NG):
                        first_rest(y, yp, 1)
                    if live(i, NG):
                        invert(2 * i, 0)
                        read_qk(i, ip, 2)
                    if live(y, NG):
                        last_part(y, yp, 1)
                    if live(i, NG):
                        read_qk(i, ip, 3)
                        after(dve, v_ps, i + 1)
                        dve.tensor_tensor(
                            w.mix[:, i // (NG // B), :, bass.ds((i % (NG // B)) * GT, GT), :],
                            bv[:, :, :].rearrange("p t (h e) -> p h t e", h=H),
                            w.bb[:, 2 * D:3 * D].rearrange("p (h e) -> p h e", h=H).unsqueeze(2).broadcast_to([P, H, GT, HD]),
                            ALU.add).then_inc(v_read, 1)
                pipelined(dve, NG, 4, 2, body)

            @block.scalar
            def _(act):
                def square_half(i, ip, hf):
                    after(act, qk_read, GT * i + 2 * hf + 2)
                    after(act, ss_ready, 2 * i + hf - 1)
                    act.activation(heads(sq, hf), heads(qk[:, ip, :, :], hf), ACT.Square).then_inc(sq_ready, 1)

                def take_root(k, hf):
                    after(act, ms_ready, k + 1)
                    act.activation(root[:, hf, :], ms[:, hf, :], ACT.Sqrt).then_inc(root_ready, 1)

                def first_part(y, yp, hf):
                    after(act, kw_ready, 2 * y + hf + 1)
                    after(act, pt_ps, 2 * GT * (y - 1))
                    act.activation(part(yp, 0, hf), heads(qk[:, yp, :, :], hf), ACT.Copy).then_inc(part1, 1)

                def second_part(y, yp, hf):
                    after(act, rest1, 2 * y + hf + 1)
                    act.activation(part(yp, 1, hf), heads(rest, hf), ACT.Copy).then_inc(part2, 1)

                def stage_parts(s, sp_, t, i):
                    after(act, pt_ps, 2 * GT * s + 2 * t + i + 1)
                    if t == 0:
                        if isinstance(s, int):
                            after(act, stored[sp_], 32 * ((s - sp_) // 2))
                        else:
                            act.wait_ge(stored[sp_], 16 * (s - sp_))
                    act.activation(stage[:, sp_, i, :, t, :], bp[i][0:2 * HROWS, :, :], ACT.Copy).then_inc(pt_ready, 1)

                def body(n, par):
                    i, y, s = n - 1, n - 2, n - 3
                    ip, yp, sp_ = 1 - par, par, 1 - par
                    if live(i, NG):
                        for c, bank in enumerate((b0, b1)):
                            after(act, ht_ps, 2 * i + c + 1)
                            if c == 0:
                                after(act, v_ps, i)
                            act.activation(ht[:, c, :, :], bank[:, :, :], ACT.Copy).then_inc(ht_ready, 1)
                    if live(y, NG):
                        take_root(2 * y + 1, 1)
                    if live(s, NG):
                        stage_parts(s, sp_, 0, 0)
                    if live(y, NG):
                        first_part(y, yp, 0)
                    if live(s, NG):
                        stage_parts(s, sp_, 0, 1)
                    if live(y, NG):
                        second_part(y, yp, 0)
                    if live(s, NG):
                        stage_parts(s, sp_, 1, 0)
                        stage_parts(s, sp_, 1, 1)
                    if live(i, NG):
                        square_half(i, ip, 0)
                    if live(y, NG):
                        first_part(y, yp, 1)
                    if live(i, NG):
                        take_root(2 * i, 0)
                    if live(s, NG):
                        stage_parts(s, sp_, 2, 0)
                    if live(y, NG):
                        second_part(y, yp, 1)
                    if live(s, NG):
                        stage_parts(s, sp_, 2, 1)
                    if live(n, NG):
                        after(act, nmr_ready, n + 1)
                        after(act, ht_ps, 2 * n)
                        for t in range(GT):
                            last = act.activation(hn[:, t, :], w.x[:, n * GT + t, :], ACT.Identity,
                                                  scale=rstd[:, t:t + 1], bias=nmr[:, t:t + 1])
                        last.then_inc(h_ready, 1)
                    if live(s, NG):
                        stage_parts(s, sp_, 3, 0)
                        stage_parts(s, sp_, 3, 1)
                    if live(i, NG):
                        square_half(i, ip, 1)
                pipelined(act, NG, 4, 3, body)

            @block.tensor
            def _(pe):
                def transpose_parts(s, sp_, t, i):
                    after(pe, part3, 2 * s + t // 2 + 1)
                    after(pe, pt_ready, 2 * GT * s + 2 * t + i - 1)
                    for g in range(NPAIR):
                        h = H * i + 2 * g
                        mm = pe.transpose(bp[i][0:2 * HROWS, g, :],
                                          pt[:, sp_, t, h:h + 2, :, :].rearrange("p h n e -> p (h n e)"), w.identb[:, :])
                    mm.then_inc(pt_ps, 1)

                def body(n, par):
                    i, s, sp_ = n - 1, n - 3, 1 - par
                    if live(i, NG):
                        after(pe, h_ready, i + 1)
                        after(pe, ht_ready, 2 * i)
                        for c, bank in enumerate((b0, b1)):
                            for t in range(GT):
                                mm = pe.transpose(bank[:, t, :], hn[:, t, P * c:P * c + P], w.ident[:, :])
                            mm.then_inc(ht_ps, 1)
                    for t in range(GT):
                        if live(s, NG):
                            transpose_parts(s, sp_, t, 0)
                        if live(i, NG):
                            after(pe, ht_ready, 2 * i + 2)
                            after(pe, qk_read, GT * i + t - 1)
                            for c in range(C):
                                mm = pe.matmul(bqk[t % 2][:, :], ht[:, c, t, :], w.wb[:, c, 0:2 * D],
                                               start=(c == 0), stop=(c == C - 1))
                            mm.then_inc(qk_ps, 1)
                        if live(s, NG):
                            transpose_parts(s, sp_, t, 1)
                        if live(i, NG):
                            after(pe, v_read, i)
                            for c in range(C):
                                mm = pe.matmul(bv[:, t, :], ht[:, c, t, :], w.wb[:, c, 2 * D:3 * D],
                                               start=(c == 0), stop=(c == C - 1))
                            if t == GT - 1:
                                mm.then_inc(v_ps, 1)
                pipelined(pe, NG, 4, 3, body)

            @block.sync
            def _(sp):
                def body(n, par):
                    sp.wait_ge(pt_ready, 2 * GT)
                    after(sp, pt_ready, 2 * GT * (n + 1))
                    for i in range(2):
                        rows = parts[i].rearrange("(b g h) r (s c) -> b s (h r) g c", b=B, h=2, s=NG // B)
                        sp.dma_start(rows[n // (NG // B), n % (NG // B)],
                                     stage[:, par, i, :, :, :].rearrange("p g t c -> p g (t c)")).then_inc(stored[par], 16)
                pipelined(sp, NG, 2, 0, body)
                for q in range(2):
                    sp.wait_ge(stored[q], 16 * NG)


def load_stacks(sp, d, hh, qs, ks, sem):
    q, k = d["parts_q"][hh], d["parts_k"][hh]
    sp.dma_start(qs[0:HROWS, :], q).then_inc(sem, 16)
    sp.dma_start(qs[HROWS:HROWS + 2 * HD, :], q[0:2 * HD, :]).then_inc(sem, 16)
    sp.dma_start(qs[HROWS + 2 * HD:SROWS, :], q[0:HD, :]).then_inc(sem, 16)
    sp.dma_start(qs[SROWS:KROWS, :], d["mrow"][bass.ds(hh, 1), :]).then_inc(sem, 16)
    row = 0
    for n, copies in enumerate((3, 2, 1)):
        for _ in range(copies):
            sp.dma_start(ks[row:row + HD, :], k[HD * n:HD * n + HD, :]).then_inc(sem, 16)
            row += HD


STACK_DMAS = 10


def score_maxima(nc, w, d):
    with Phase(nc, "mx") as ph:
        loaded, ones, s_ps, s_read, neg_ready, t_ps, row_ready, stored = [ph.sem(s) for s in (
            "loaded ones s_ps s_read neg_ready t_ps row_ready stored").split()]
        qs = ph.sb("qs", [KROWS, T], BF16)
        ks = ph.sb("ks", [KROWS, T], BF16)
        neg = ph.sb("neg", [P, KT])
        row = ph.sb("row", [KT, P], BF16)
        sps = ph.ps("sps", [P, T])
        tps = ph.ps("tps", [KT, P])
        with nc.Block() as block:
            @block.sync
            def _(sp):
                unbounded = sp.value_load(w.flag[0:1, 0:1], min_val=0, max_val=1)
                with sp.If(unbounded > 0):
                    sp.sem_inc(stored, 16)
                    with sp.Fori(0, B * H) as hh:
                        load_stacks(sp, d, hh, qs, ks, loaded)
                        sp.wait_ge(row_ready, hh + 1)
                        sp.dma_start(d["mrow"][bass.ds(hh, 1), :].rearrange("a (t p) -> (a t) p", p=P), row[:, :]).then_inc(stored, 16)
                    sp.wait_ge(stored, 16 * B * H + 16)
                    sp.nop()

            @block.gpsimd
            def _(pool):
                pool.memset(ks[SROWS:KROWS, :], 1.0).then_inc(ones, 1)

            @block.tensor
            def _(pe):
                unbounded = pe.value_load(w.flag[0:1, 0:1], min_val=0, max_val=1)
                with pe.If(unbounded > 0):
                    pe.wait_ge(ones, 1)
                    with pe.Fori(0, B * H) as hh:
                        pe.wait_ge(loaded, 16 * STACK_DMAS * (hh + 1))
                        for t in range(KT):
                            if t:
                                pe.wait_ge(s_read, KT * hh + t)
                            for c in range(4):
                                mm = pe.matmul(sps[:, 512 * c:512 * c + 512], qs[:, P * t:P * t + P],
                                               ks[:, 512 * c:512 * c + 512], start=True, stop=True)
                            mm.then_inc(s_ps, 1)
                        pe.wait_ge(neg_ready, hh + 1)
                        pe.transpose(tps[:, :], neg[:, :], w.ident[:, :]).then_inc(t_ps, 1)
                    pe.nop()

            @block.vector
            def _(dve):
                unbounded = dve.value_load(w.flag[0:1, 0:1], min_val=0, max_val=1)
                with dve.If(unbounded > 0):
                    with dve.Fori(0, B * H) as hh:
                        for t in range(KT):
                            dve.wait_ge(s_ps, KT * hh + t + 1)
                            ins = dve.tensor_reduce(neg[:, t:t + 1], sps[:, :], AX.X, ALU.max, negate=True)
                            ins.then_inc(s_read if t < KT - 1 else neg_ready, 1)
                            if t == KT - 1:
                                dve.wait_ge(neg_ready, hh + 1)
                                dve.sem_inc(s_read, 1)
                        dve.wait_ge(t_ps, hh + 1)
                        dve.wait_ge(stored, 16 * hh + 16)
                        dve.tensor_copy(row[:, :], tps[:, :]).then_inc(row_ready, 1)
                    dve.nop()


def attention_b(nc, w, d):
    with Phase(nc, "sa") as ph:
        loaded = [ph.sem("loaded0"), ph.sem("loaded1")]
        cleared, ones_ready, v_ready, s_ps, p_ready, z_ps, zt_ready, ztok_ps, rden_ready, z_ready = [ph.sem(s) for s in (
            "cleared ones_ready v_ready s_ps p_ready z_ps zt_ready ztok_ps rden_ready z_ready").split()]
        QC = 4
        W = T // QC
        UNITS = KT * QC
        SIZES = [3] * 10 + [2] + [3] * 10 + [2]
        GROUPS = len(SIZES)
        starts = [sum(SIZES[:g]) for g in range(GROUPS)]
        PB = 4
        qs = [ph.sb(f"qs{i}", [KROWS, T], BF16) for i in range(2)]
        ks = [ph.sb(f"ks{i}", [KROWS, T], BF16) for i in range(2)]
        vs = ph.sb("vs", [P, 2, KT, V1])
        pr = ph.sb("pr", [P, PB, 3, W])
        zt = ph.sb("zt", [P, QC, P])
        rden = ph.sb("rden", [P, QC, 4])
        bs = [ph.ps("bs0", [P, 3, W]), ph.ps("bs1", [P, 3, W])]
        bz = [ph.ps("bz0", [P, 4, P]), ph.ps("bz1", [P, 4, P])]
        heads = w.mix[:, :, :, :, :].rearrange("p b h t e -> p (b h) t e")
        LAG = 2
        fours = [(starts[g - LAG] + SIZES[g - LAG]) // QC if g >= LAG else 0 for g in range(GROUPS)]
        last_four = [(starts[g] + SIZES[g] - 1) // QC for g in range(GROUPS)]
        N = B * H

        with nc.Block() as block:
            @block.sync
            def _(sp):
                def body(n, par):
                    if not isinstance(n, int):
                        sp.wait_ge(s_ps, GROUPS)
                    after(sp, s_ps, GROUPS * (n - 1))
                    load_stacks(sp, d, n, qs[par], ks[par], loaded[par])
                pipelined(sp, N, 2, 0, body)

            @block.gpsimd
            def _(pool):
                pool.memset(vs[:, :, :, :], 1.0).then_inc(ones_ready, 1)
                pool.wait_ge(ones_ready, 1)

                def body(n, par):
                    after(pool, z_ps, KT * (n - 1))
                    pool.tensor_copy(vs[:, par, :, 0:HD], heads[:, n, :, :]).then_inc(v_ready, 1)
                pipelined(pool, N, 2, 0, body)

            @block.scalar
            def _(act):
                def body(n, par):
                    for g in range(GROUPS):
                        at = GROUPS * n + g
                        act.wait_ge(s_ps, at + 1)
                        if g >= PB:
                            act.wait_ge(z_ps, KT * n + last_four[g - PB] + 1)
                        else:
                            after(act, z_ps, KT * (n - 1) + last_four[g - PB + GROUPS] + 1)
                        s = SIZES[g]
                        act.activation(pr[:, (GROUPS * par + g) % PB, 0:s, :], bs[g % 2][:, 0:s, :], ACT.Exp).then_inc(p_ready, 1)
                pipelined(act, N, 2, 0, body)

            @block.vector
            def _(dve):
                for i in range(2):
                    dve.memset(ks[i][SROWS:KROWS, :], 1.0).then_inc(cleared, 1)
                    dve.memset(bz[i][:, :, :], 0.0).then_inc(cleared, 1)

                def body(n, par):
                    after(dve, z_ps, KT * (n + 1))
                    after(dve, ztok_ps, n)
                    dve.tensor_copy(zt[:, :, :], bz[par][:, :, :]).then_inc(zt_ready, 1)
                    after(dve, ztok_ps, n + 1)
                    tok = bz[par][:, :, :].rearrange("p i (j s) -> p i j s", j=QC)
                    dve.reciprocal(rden[:, :, :], tok[:, :, :, HD]).then_inc(rden_ready, 1)
                    dve.wait_ge(rden_ready, n + 1)
                    dve.tensor_tensor(heads[:, n, :, :].rearrange("p (j i) e -> p i j e", j=QC), tok[:, :, :, 0:HD],
                                      rden[:, :, :].unsqueeze(3).broadcast_to([P, QC, 4, HD]), ALU.mult).then_inc(z_ready, 1)
                pipelined(dve, N, 2, 0, body)

            @block.tensor
            def _(pe):
                pe.wait_ge(cleared, 4)

                def products(n, par, lo, hi):
                    for f in range(lo, hi):
                        for j in range(QC):
                            u = QC * f + j
                            g = max(i for i in range(GROUPS) if starts[i] <= u)
                            buf = (GROUPS * par + g) % PB
                            mm = pe.matmul(bz[par][32 * j:32 * j + V1, :, :], vs[:, par, f, :],
                                           pr[:, buf, u - starts[g], :], start=(f == 0), stop=(f == KT - 1))
                        mm.then_inc(z_ps, 1)

                def tokens(n, par):
                    after(pe, zt_ready, n + 1)
                    for i in range(4):
                        mm = pe.transpose(bz[par][:, i, :], zt[:, i, :], w.ident[:, :])
                    mm.then_inc(ztok_ps, 1)

                def body(n, par):
                    done = 0
                    for g in range(GROUPS):
                        if g == 0:
                            pe.wait_ge(loaded[par], 16 * STACK_DMAS * ((n - par) // 2 + 1) if isinstance(n, int)
                                       else 8 * STACK_DMAS * (n - par) + 16 * STACK_DMAS)
                        after(pe, p_ready, GROUPS * n + g - 1)
                        for u in range(starts[g], starts[g] + SIZES[g]):
                            t, j = divmod(u, QC)
                            mm = pe.matmul(bs[g % 2][:, u - starts[g], :], ks[par][:, P * t:P * t + P],
                                           qs[par][:, W * j:W * j + W], start=True, stop=True)
                        mm.then_inc(s_ps, 1)
                        if g < LAG and live(n - 1, N):
                            products(n - 1, 1 - par, tail[g], tail[g + 1])
                        if g == 4 and live(n - 1, N):
                            tokens(n - 1, 1 - par)
                        if g == LAG:
                            after(pe, v_ready, n + 1)
                            after(pe, z_ready, n - 1)
                        products(n, par, done, fours[g])
                        done = max(done, fours[g])

                tail = [fours[GROUPS - 1]] + [(starts[g] + SIZES[g]) // QC for g in (GROUPS - 2, GROUPS - 1)]

                pipelined(pe, N, 2, 0, body)
                for g in range(LAG):
                    pe.wait_ge(p_ready, GROUPS * N - (LAG - 1) + g)
                    products(N - 1, (N - 1) % 2, tail[g], tail[g + 1])
                tokens(N - 1, (N - 1) % 2)


class Kept:
    pass


def build(nc, d, out):
    with ExitStack() as ctx:
        def sb(name, shape, dt=F32):
            return ctx.enter_context(nc.sbuf_tensor(name, shape, dt))

        w = Kept()
        w.x = sb("x", [P, NT, D])
        w.mix = sb("mix", [P, B, H, TB, HD])
        w.wa = sb("wa", [P, C, 3 * D])
        w.wb = sb("wb", [P, C, 3 * D])
        w.woa = sb("woa", [P, C, D])
        w.wob = sb("wob", [P, C, D])
        w.wf = sb("wf", [P, C, 2 * ZW])
        w.ba = sb("ba", [P, 3 * D])
        w.bb = sb("bb", [P, 3 * D])
        w.boa = sb("boa", [P, D])
        w.bob = sb("bob", [P, D])
        w.bf = sb("bf", [P, 2, ZW])
        w.wqk = sb("wqk", [P, HD])
        w.omega = sb("omega", [P, C, H // C * FD])
        w.ident = sb("ident", [P, P])
        w.identb = sb("identb", [P, P], BF16)
        w.mask = sb("mask", [P, P])
        w.minushalf = sb("minushalf", [P, 2 * H])
        w.minusone = sb("minusone", [P, GT])
        w.three = sb("three", [P, 1])
        w.lneps = sb("lneps", [P, GT])
        w.one = sb("one", [P, 1])
        w.keep = sb("keep", [P, NT])
        w.fnode = sb("fnode", [P, 1])
        w.fweight = sb("fweight", [P, 1])
        w.flo = sb("flo", [P, 1])
        w.fhi = sb("fhi", [P, 1])
        w.fneg = sb("fneg", [P, 1])
        w.fscale = sb("fscale", [P, 1])
        w.flag = sb("flag", [1, 1], I32)
        setup(nc, w, d)
        attention_a(nc, w, d)
        project_and_ffn(nc, w, d, "f1", w.woa, w.boa, None)
        prepare_b(nc, w, d)
        score_maxima(nc, w, d)
        attention_b(nc, w, d)
        project_and_ffn(nc, w, d, "f2", w.wob, w.bob, out)


_NAMES = ["L0_attn_a_x", "L0_attn_a_Wqkv", "L0_attn_a_bqkv", "L0_attn_a_Wout", "L0_attn_a_bout", "L0_attn_a_omega",
          "L0_attn_a_quad_nodes", "L0_attn_a_quad_weights", "L0_attn_b_bqkv", "L0_attn_b_bo", "L0_attn_b_wq",
          "L0_attn_b_wk", "L0_ffn_gate_w", "L0_ffn_b0", "L0_ffn_b1"]
_TRANSPOSED = {"attn_b_WqkvT": "L0_attn_b_Wqkv", "attn_b_WoT": "L0_attn_b_Wo", "ffn_w0T": "L0_ffn_w0",
               "ffn_w1T": "L0_ffn_w1"}


def kernel(**inputs):
    import concourse.bacc as bacc
    from concourse.bass_utils import run_bass_kernel_spmd

    nc = bacc.Bacc("TRN2", target_bir_lowering=False, num_devices=1)
    arrays = {name: np.ascontiguousarray(inputs[name]) for name in _NAMES}
    arrays.update({name: np.ascontiguousarray(np.asarray(inputs[src]).T) for name, src in _TRANSPOSED.items()})
    d = {name: nc.dram_tensor(f"in_{name}", a.shape, mybir.dt.from_np(a.dtype), kind="ExternalInput").ap()
         for name, a in arrays.items()}
    d["parts_q"] = nc.dram_tensor("parts_q", (B * H, HROWS, T), BF16, kind="Internal").ap()
    d["parts_k"] = nc.dram_tensor("parts_k", (B * H, HROWS, T), BF16, kind="Internal").ap()
    d["mrow"] = nc.dram_tensor("mrow", (B * H, T), BF16, kind="Internal").ap()
    out = nc.dram_tensor("out", (B, T, D), F32, kind="ExternalOutput").ap()
    build(nc, d, out)
    r = run_bass_kernel_spmd(nc, [{f"in_{name}": a for name, a in arrays.items()}], core_ids=[0])
    return r.results[0]["out"]
```

```python
from contextlib import ExitStack

import numpy as np

import concourse.bass as bass
from concourse import mybir

F32 = mybir.dt.float32
BF16 = mybir.dt.bfloat16
I32 = mybir.dt.int32
ALU = mybir.AluOpType
ACT = mybir.ActivationFunctionType
AX = mybir.AxisListType

P = 128
B, T, D = 2, 2048, 256
H = 16
HD = D // H
M, R = 32, 2
FD = R * M
NPAIR = H // 2
SLOTS = P // (2 * HD)
NT = B * T // P
TB = T // P
GT = 4
NG = NT // GT
C = D // P
V1 = HD + 1
E = 8
ZW = D + E // 2
LN_EPS = 1e-5
RMS_EPS = 1e-6
NORM_FLOOR = 1e-12
CLIP = 20.0
DEN_FLOOR = 1e-6
SAFE_SCORE = 60.0
PARTS = 3
HROWS = PARTS * HD
SROWS = 2 * HROWS
KROWS = SROWS + 1
KT = T // P


def after(eng, sem, count):
    if isinstance(count, int) and count <= 0:
        return
    eng.wait_ge(sem, count)


def live(i, n):
    return not isinstance(i, int) or 0 <= i < n


def pipelined(eng, n, lead, tail, body):
    for i in range(lead):
        body(i, i % 2)
    turns = (n - lead) // 2
    with eng.Fori(0, turns) as q:
        for u in range(2):
            body(2 * q + (lead + u), (lead + u) % 2)
    for i in range(lead + 2 * turns, n + tail):
        body(i, i % 2)


class Phase:

    def __init__(self, nc, tag):
        self.nc, self.tag, self.ctx, self.sems = nc, tag, ExitStack(), []

    def __enter__(self):
        self.ctx.__enter__()
        return self

    def __exit__(self, *e):
        self.nc.clear_and_free_semaphores(self.sems)
        self.nc.all_engine_barrier()
        return self.ctx.__exit__(*e)

    def sb(self, name, shape, dt=F32):
        return self.ctx.enter_context(self.nc.sbuf_tensor(f"{self.tag}_{name}", shape, dt))

    def ps(self, name, shape, dt=F32):
        return self.ctx.enter_context(self.nc.psum_tensor(f"{self.tag}_{name}", shape, dt))

    def sem(self, name):
        self.sems.append(self.nc.alloc_semaphore(f"{self.tag}_{name}"))
        return self.sems[-1]


def setup(nc, w, d):
    with Phase(nc, "setup") as ph:
        loaded = ph.sem("loaded")
        zeroed = ph.sem("zeroed")
        diagonal = ph.sem("diagonal")
        derived = ph.sem("derived")
        nodes = ph.sb("nodes", [P, R])
        half = ph.sb("half", [P, R])
        bothw = ph.sb("bothw", [P, 2, HD])
        wrow = ph.sb("wrow", [1, 3, HD])
        top = ph.sb("top", [1, 1])

        def row(src, n=P):
            return src.unsqueeze(0).broadcast_to([n] + list(src.shape))

        loads = [
            (w.wa[:, :, :], d["L0_attn_a_Wqkv"].rearrange("(c p) n -> p c n", p=P)),
            (w.ba[:, :], row(d["L0_attn_a_bqkv"])),
            (nodes[:, :], row(d["L0_attn_a_quad_nodes"])),
            (bothw[:, 0, :], row(d["L0_attn_b_wq"])),
            (bothw[:, 1, :], row(d["L0_attn_b_wk"])),
            (wrow[0:1, 0, :], row(d["L0_attn_b_wq"], 1)),
            (wrow[0:1, 1, :], row(d["L0_attn_b_wk"], 1)),
        ]
        features = []
        for q in range(P // M):
            r = q % R
            part = slice(M * q, M * q + M)
            features.append((w.fnode[part, 0:1], row(d["L0_attn_a_quad_nodes"][r:r + 1], M)))
            features.append((w.fweight[part, 0:1], row(d["L0_attn_a_quad_weights"][r:r + 1], M)))

        with nc.Block() as block:
            @block.sync
            def _(sp):
                for dst, src in loads:
                    sp.dma_start(dst, src).then_inc(loaded, 16)

            @block.scalar
            def _(act):
                for dst, src in features:
                    act.dma_start(dst, src).then_inc(loaded, 16)
                act.wait_ge(zeroed, 1)
                act.dma_start(d["mrow"], w.zrow[:, :]).then_inc(w.mrow_out, 16)

            @block.gpsimd
            def _(pool):
                pool.memset(w.zrow[:, :], 0.0).then_inc(zeroed, 1)
                pool.memset(w.ident[:, :], 0.0).then_inc(zeroed, 1)
                pool.memset(w.mask[:, :], 1.0).then_inc(zeroed, 1)
                pool.memset(w.minushalf[:, :], -0.5).then_inc(zeroed, 1)
                pool.memset(half[:, :], 0.5).then_inc(zeroed, 1)
                pool.memset(w.keep[:, :], 1.0).then_inc(zeroed, 1)
                pool.memset(w.lneps[:, :], LN_EPS).then_inc(zeroed, 1)
                pool.memset(w.bf[:, :, D:ZW], 0.0).then_inc(zeroed, 1)
                pool.memset(w.minusone[:, :], -1.0).then_inc(zeroed, 1)
                pool.memset(w.three[:, :], 3.0).then_inc(zeroed, 1)
                pool.memset(w.one[:, :], 1.0).then_inc(zeroed, 1)
                pool.wait_ge(zeroed, 11)
                pool.memset(w.keep[:, TB - 1:TB], 0.0)
                pool.affine_select(out=w.ident[:, :], in_=w.ident[:, :], compare_op=ALU.not_equal, fill=1.0,
                                   base=0, pattern=[[-1, P]], channel_multiplier=1).then_inc(diagonal, 1)
                pool.affine_select(out=w.mask[:, :], in_=w.mask[:, :], compare_op=ALU.is_ge, fill=0.0,
                                   base=0, pattern=[[1, P]], channel_multiplier=-1)
                pool.wait_ge(derived, 1)
                pool.tensor_tensor(w.roots[:, :], nodes[:, :], half[:, :], ALU.pow)

            @block.vector
            def _(dve):
                dve.wait_ge(loaded, 16 * (len(loads) + len(features)))
                dve.tensor_scalar(nodes[:, :], nodes[:, :], 0.0, 2.0, ALU.max, ALU.mult).then_inc(derived, 1)
                dve.tensor_scalar(w.flo[:, :], w.fnode[:, :], -CLIP, None, ALU.add)
                dve.tensor_scalar(w.fhi[:, :], w.fnode[:, :], CLIP, None, ALU.add)
                dve.tensor_scalar(w.fneg[:, :], w.fnode[:, :], -1.0, None, ALU.mult)
                dve.tensor_scalar(w.fscale[:, :], w.fweight[:, :], 0.0, 1.0 / M, ALU.max, ALU.mult)
                dve.scalar_tensor_tensor(out=w.wqk[:, :], in0=bothw[:, 0, :], scalar=float(HD), in1=bothw[:, 1, :],
                                         op0=ALU.mult, op1=ALU.mult)
                dve.wait_ge(diagonal, 1)
                dve.tensor_copy(w.identb[:, :], w.ident[:, :])
                dve.tensor_tensor(wrow[:, 2, :], wrow[:, 0, :], wrow[:, 1, :], ALU.mult).then_inc(derived, 1)
                dve.wait_ge(derived, 2)
                dve.tensor_reduce(top[:, :], wrow[:, 2, :], AX.X, ALU.max, apply_absolute_value=True).then_inc(derived, 1)
                dve.wait_ge(derived, 3)
                dve.tensor_scalar(w.flag[:, :], top[:, :], SAFE_SCORE / HD, None, ALU.is_gt)


def attention_a(nc, w, d):
    with Phase(nc, "la") as ph:
        x_in = [ph.sem("x_in0"), ph.sem("x_in1")]
        om_cleared, omega_in, split, later_in = [ph.sem(s) for s in "om_cleared omega_in split later_in".split()]
        (cleared, bn_done, mv_ready, var_ready, rstd_ready, h_ready, ht_ps, ht_ready, qkv_ps, qkv_read, sq_ready,
         ss_ready, ssm_ready, rn_ready, qn_ready, part1, rest1, part2, part3, qkt_ps, qkt_ready, pq_ps, argq_ready,
         qf_ready, pk_ps, argk_ready, kexp_ready, kf_ready, kt_ps, kt_ready, at_ps, at_ready, ctx_ps, st_ps, st_ready,
         s_ps, s_ready, ct_ready, ctok_ps, den_ready, rden_ready, ctx_ready, vb_ready) = [ph.sem(s) for s in (
             "cleared bn_done mv_ready var_ready rstd_ready h_ready ht_ps ht_ready qkv_ps qkv_read sq_ready "
             "ss_ready ssm_ready rn_ready qn_ready part1 rest1 part2 part3 qkt_ps qkt_ready pq_ps argq_ready "
             "qf_ready pk_ps argk_ready kexp_ready kf_ready kt_ps kt_ready at_ps at_ready ctx_ps st_ps st_ready "
             "s_ps s_ready ct_ready ctok_ps den_ready rden_ready ctx_ready vb_ready").split()]

        om = ph.sb("om", [P, NPAIR, P])
        st6 = ph.sb("st6", [P, 2, 6])
        mv = ph.sb("mv", [P, 2, 2])
        var = ph.sb("var", [P, 2, 1])
        rstd = ph.sb("rstd", [P, 2, 1])
        hn = ph.sb("hn", [P, 2, D])
        ht = ph.sb("ht", [P, 2, C, P])
        qk = ph.sb("qk", [P, 2, 2 * D])
        vs = ph.sb("vs", [P, 2, D])
        vb = ph.sb("vb", [P, 2, H, V1])
        sq = ph.sb("sq", [P, 2 * D])
        ss = ph.sb("ss", [P, 2, 2 * H])
        ssm = ph.sb("ssm", [P, 2, 2 * H])
        rn = ph.sb("rn", [P, 2, 2 * H])
        qn = ph.sb("qn", [P, 2 * D])
        rest = ph.sb("rest", [P, 2 * D])
        pt = ph.sb("pt", [P, 2 * NPAIR, SLOTS, 2 * HD], BF16)
        qkt = ph.sb("qkt", [P, 2, NPAIR, P], BF16)
        argq = ph.sb("argq", [P, NPAIR, P])
        argk = ph.sb("argk", [P, NPAIR, P])
        kexp = ph.sb("kexp", [P, NPAIR, P])
        qf = ph.sb("qf", [P, 2, NPAIR, 2, P])
        kf = ph.sb("kf", [P, 2, NPAIR, P])
        kt = ph.sb("kt", [P, 2, NPAIR, P])
        at = ph.sb("at", [P, 2, NPAIR, 2, P])
        stt = ph.sb("stt", [P, 4, P])
        state = ph.sb("state", [P, H, V1])
        ct = ph.sb("ct", [P, 4, P])
        den = ph.sb("den", [P, 2, H])
        rden = ph.sb("rden", [P, 2, H])

        b0 = ph.ps("b0", [P, NPAIR, P], BF16)
        b1 = ph.ps("b1", [P, 2 * D])
        b2 = ph.ps("b2", [P, 2 * D])
        b34 = ph.ps("b34", [P, NPAIR, P])
        b5 = ph.ps("b5", [P, 4, P])
        b6 = ph.ps("b6", [P, 4, P])
        b7 = ph.ps("b7", [P, 4, P])
        b56 = [b5, b6]
        shares = b1[:, :].rearrange("p (q f) -> p q f", q=4)

        xs = d["L0_attn_a_x"].rearrange("b (t p) d -> (b t) p d", p=P)

        def row(src):
            return src.unsqueeze(0).broadcast_to([P] + list(src.shape))

        later = [
            (w.woa[:, :, :], d["L0_attn_a_Wout"].rearrange("(c p) n -> p c n", p=P)),
            (w.wf[:, :, 0:D], d["ffn_w0T"].rearrange("(c p) n -> p c n", p=P)),
            (w.wf[:, :, D:ZW], d["L0_ffn_gate_w"][:, 0:E // 2].rearrange("(c p) n -> p c n", p=P)),
            (w.wf[:, :, ZW:ZW + D], d["ffn_w1T"].rearrange("(c p) n -> p c n", p=P)),
            (w.wf[:, :, ZW + D:2 * ZW], d["L0_ffn_gate_w"][:, E // 2:E].rearrange("(c p) n -> p c n", p=P)),
            (w.wb[:, :, :], d["attn_b_WqkvT"].rearrange("(c p) n -> p c n", p=P)),
            (w.wob[:, :, :], d["attn_b_WoT"].rearrange("(c p) n -> p c n", p=P)),
            (w.boa[:, :], row(d["L0_attn_a_bout"])),
            (w.bf[:, 0, 0:D], row(d["L0_ffn_b0"])),
            (w.bf[:, 1, 0:D], row(d["L0_ffn_b1"])),
            (w.bb[:, :], row(d["L0_attn_b_bqkv"])),
            (w.bob[:, :], row(d["L0_attn_b_bo"])),
        ]
        mix = w.mix[:, :, :, :, :]

        def slots(bank):
            return bank[:, :, :].rearrange("p g (j s) -> p g j s", j=4)

        def pairs(tile):
            return tile[:, :].rearrange("p (g e) -> p g e", e=2 * HD)

        with nc.Block() as block:
            @block.sync
            def _(sp):
                def body(n, par):
                    if not isinstance(n, int):
                        sp.wait_ge(x_in[par], 16)
                    after(sp, x_in[par], 16 * ((n - par) // 2) if isinstance(n, int) else 8 * (n - par))
                    sp.dma_start(w.x[:, n, :], xs[n]).then_inc(x_in[par], 16)
                    if isinstance(n, int) and n == 3:
                        sp.wait_ge(om_cleared, 1)
                        for slot in range(SLOTS):
                            for a in range(2):
                                for r in range(R):
                                    lo = 2 * HD * slot + HD * a
                                    sp.dma_start(
                                        om[lo:lo + HD, :, FD * a + M * r:FD * a + M * r + M],
                                        d["L0_attn_a_omega"][r].rearrange("(g a) d m -> a d g m", a=2)[a],
                                    ).then_inc(omega_in, 16)
                        for dst, src in later:
                            sp.dma_start(dst, src).then_inc(later_in, 16)
                pipelined(sp, NT, 4, 0, body)
                sp.wait_ge(later_in, 16 * len(later))
                sp.wait_ge(w.mrow_out, 16)

            @block.gpsimd
            def _(pool):
                pool.memset(om[:, :, :], 0.0).then_inc(om_cleared, 1)

                def body(n, par):
                    i, f = n - 1, n - 3
                    if isinstance(n, int) and n == 1:
                        pool.memset(vb[:, :, :, :], 1.0).then_inc(cleared, 1)
                        pool.memset(qf[:, 1, :, :, :], 0.0).then_inc(cleared, 1)
                        pool.memset(state[:, :, :], 0.0).then_inc(cleared, 1)
                    if isinstance(f, int) and f == 0:
                        pool.wait_ge(cleared, 5)
                    if live(f, NT):
                        after(pool, qkv_read, f + 1)
                        after(pool, ctx_ps, f - 1)
                        pool.tensor_tensor(vb[:, 1 - par, :, 0:HD], vs[:, 1 - par, :].rearrange("p (h e) -> p h e", h=H),
                                           w.one[:, 0:1].unsqueeze(2).broadcast_to([P, H, HD]), ALU.mult).then_inc(vb_ready, 1)
                    if live(n, NT):
                        after(pool, mv_ready, n + 1)
                        after(pool, rstd_ready, n - 1)
                        pool.tensor_tensor(var[:, par, :], mv[:, par, 1:2], w.lneps[:, 0:1], ALU.add).then_inc(var_ready, 1)
                        after(pool, var_ready, n + 1)
                        after(pool, h_ready, n - 1)
                        pool.tensor_tensor(rstd[:, par, :], var[:, par, :], w.minushalf[:, 0:1], ALU.pow).then_inc(rstd_ready, 1)
                    if live(i, NT):
                        after(pool, qkv_read, i + 1)
                        after(pool, ss_ready, i)
                        pool.tensor_tensor(sq[:, :], qk[:, 1 - par, :], qk[:, 1 - par, :], ALU.mult).then_inc(sq_ready, 1)
                    if live(i, NT):
                        after(pool, ssm_ready, i + 1)
                        after(pool, qn_ready, i - 1)
                        pool.tensor_tensor(rn[:, 1 - par, :], ssm[:, 1 - par, :], w.minushalf[:, 0:2 * H], ALU.pow).then_inc(rn_ready, 1)
                pipelined(pool, NT, 6, 4, body)

            @block.vector
            def _(dve):
                def split_omega():
                    dve.wait_ge(omega_in, 16 * 2 * SLOTS * R)
                    heads = om[:, :, :].rearrange("p g (a r m) -> p (g a) r m", r=R, m=M)
                    for r in range(R):
                        last = dve.tensor_scalar(heads[:, :, r, :], heads[:, :, r, :], w.roots[:, r:r + 1], None, ALU.mult)
                    last.then_inc(split, 1)
                    dve.wait_ge(split, 1)
                    dve.tensor_copy(w.omega_a[:, :, :], om[:, :, :]).then_inc(split, 1)
                    dve.wait_ge(split, 2)
                    dve.tensor_tensor(om[:, :, :], om[:, :, :], w.omega_a[:, :, :], ALU.subtract).then_inc(split, 1)
                    dve.wait_ge(split, 3)
                    dve.tensor_copy(w.omega_b[:, :, :], om[:, :, :]).then_inc(split, 1)
                    dve.wait_ge(split, 4)
                    w3 = slice(3 * 2 * HD, P)
                    dve.tensor_tensor(w.omega_a[w3, :, :], om[w3, :, :], w.omega_b[w3, :, :], ALU.subtract).then_inc(split, 1)
                    dve.wait_ge(split, 5)
                    dve.memset(w.omega_b[2 * 2 * HD:P, :, :], 0.0).then_inc(split, 1)

                def body(n, par):
                    i, j, f, k = n - 1, n - 2, n - 3, n - 4

                    def mask_scores(r):
                        after(dve, at_ps, 4 * k + r + 1)
                        if r == 0:
                            after(dve, ctx_ps, k - 1)
                        dve.tensor_tensor(
                            at[:, par, 2 * r:2 * r + 2, :, :].rearrange("p g e t -> p (g e) t"),
                            b56[r % 2][:, :, :], w.mask[:, :].unsqueeze(1).broadcast_to([P, 4, P]),
                            ALU.mult).then_inc(at_ready, 1)

                    def clip(arg, ready, source):
                        dve.tensor_scalar(arg[:, :, :], source[:, :, :], w.flo[:, 0:1], w.fhi[:, 0:1],
                                          ALU.max, ALU.min).then_inc(ready, 1)

                    if live(n, NT):
                        count = 16 * ((n - par) // 2 + 1) if isinstance(n, int) else 8 * (n - par) + 16
                        dve.wait_ge(x_in[par], count)
                        after(dve, mv_ready, n - 1)
                        dve.bn_stats(st6[:, par, :], w.x[:, n, :]).then_inc(bn_done, 1)
                        dve.wait_ge(bn_done, n + 1)
                        after(dve, rstd_ready, n - 1)
                        if isinstance(n, int):
                            dve.bn_aggr(mv[:, par, :], st6[:, par, :]).then_inc(mv_ready, 1)
                    if isinstance(n, int) and n == 1:
                        dve.memset(b7[:, :, :], 0.0).then_inc(cleared, 1)
                        dve.memset(qf[:, 0, :, :, :], 0.0).then_inc(cleared, 1)
                    if isinstance(n, int) and n == 2:
                        split_omega()
                    if live(i, NT):
                        after(dve, qkv_ps, i + 1)
                        after(dve, sq_ready, i - 1)
                        dve.tensor_tensor(qk[:, 1 - par, :], b1[:, :], w.ba[:, 0:2 * D], ALU.add)
                        after(dve, vb_ready, i - 1)
                        dve.tensor_tensor(vs[:, 1 - par, :], b2[:, 0:D], w.ba[:, 2 * D:3 * D], ALU.add).then_inc(qkv_read, 1)
                    if not isinstance(n, int):
                        dve.bn_aggr(mv[:, par, :], st6[:, par, :]).then_inc(mv_ready, 1)
                    if live(f, NT):
                        after(dve, pq_ps, f + 1)
                        after(dve, qf_ready, f)
                        clip(argq, argq_ready, b34)
                    if live(k, NT):
                        mask_scores(0)
                        mask_scores(1)
                    if live(n, NT):
                        after(dve, rstd_ready, n + 1)
                        after(dve, ht_ps, n - 1)
                        dve.tensor_scalar(hn[:, par, :], w.x[:, n, :], mv[:, par, 0:1], rstd[:, par, :],
                                          ALU.subtract, ALU.mult).then_inc(h_ready, 1)
                    if live(i, NT):
                        after(dve, sq_ready, i + 1)
                        after(dve, ssm_ready, i - 1)
                        dve.tensor_reduce(ss[:, 1 - par, :], sq[:, :].rearrange("p (g e) -> p g e", e=HD),
                                          AX.X, ALU.add).then_inc(ss_ready, 1)
                        after(dve, ss_ready, i + 1)
                        dve.tensor_scalar(ssm[:, 1 - par, :], ss[:, 1 - par, :], NORM_FLOOR ** 2, None,
                                          ALU.max).then_inc(ssm_ready, 1)
                    if live(f, NT):
                        after(dve, pk_ps, f + 1)
                        after(dve, kexp_ready, f)
                        clip(argk, argk_ready, b34)
                    if live(k, NT):
                        mask_scores(2)
                        mask_scores(3)
                    if live(j, NT):
                        after(dve, rn_ready, j + 1)
                        after(dve, rest1, j)
                        dve.tensor_tensor(
                            qn[:, :].rearrange("p (g e) -> p g e", e=HD),
                            qk[:, par, :].rearrange("p (g e) -> p g e", e=HD),
                            rn[:, par, :].unsqueeze(2).broadcast_to([P, 2 * H, HD]),
                            ALU.mult).then_inc(qn_ready, 1)
                    if live(f, NT):
                        after(dve, kexp_ready, f + 1)
                        after(dve, kt_ps, f - 1)
                        dve.tensor_scalar(kf[:, 1 - par, :, :], kexp[:, :, :], w.fscale[:, 0:1], None,
                                          ALU.mult).then_inc(kf_ready, 1)
                    if live(j, NT):
                        after(dve, part1, j + 1)
                        after(dve, part3, j)
                        dve.tensor_tensor(pairs(rest), pairs(qn), pt[:, :, 0, :], ALU.subtract).then_inc(rest1, 1)
                    if live(k, NT):
                        after(dve, s_ps, k + 1)
                        after(dve, ctx_ps, k + 1)
                        after(dve, s_ready, k)
                        dve.scalar_tensor_tensor(
                            out=state[:, :, :], in0=state[:, :, :], scalar=w.keep[:, bass.ds(k, 1)],
                            in1=b6[:, :, :].rearrange("p g (j s) -> p (g j) s", j=4)[:, :, 0:V1],
                            op0=ALU.mult, op1=ALU.add).then_inc(s_ready, 1)
                    if live(j, NT):
                        after(dve, part2, j + 1)
                        dve.tensor_tensor(pt[:, :, 2, :], pairs(rest), pt[:, :, 1, :], ALU.subtract).then_inc(part3, 1)
                    if live(k, NT):
                        after(dve, ctok_ps, k + 1)
                        tok = slots(b7)
                        dve.tensor_scalar(den[:, par, :].rearrange("p (g j) -> p g j", j=4), tok[:, :, :, HD],
                                          DEN_FLOOR, None, ALU.max).then_inc(den_ready, 1)
                        dve.wait_ge(den_ready, k + 1)
                        dve.reciprocal(rden[:, par, :], den[:, par, :]).then_inc(rden_ready, 1)
                        dve.wait_ge(rden_ready, k + 1)
                        out = mix[:, k // TB, :, k % TB, :].rearrange("p (g j) e -> p g j e", j=4)
                        dve.tensor_tensor(
                            out, tok[:, :, :, 0:HD],
                            rden[:, par, :].rearrange("p (g j) -> p g j", j=4).unsqueeze(3).broadcast_to([P, 4, 4, HD]),
                            ALU.mult).then_inc(ctx_ready, 1)
                pipelined(dve, NT, 6, 4, body)

            @block.scalar
            def _(act):
                def body(n, par):
                    j, f, k = n - 2, n - 3, n - 4
                    if isinstance(f, int) and f == 0:
                        act.wait_ge(cleared, 5)

                    def copy_parts(half):
                        after(act, qkt_ps, 2 * f + half + 1)
                        after(act, pk_ps if half else pq_ps, f)
                        act.activation(qkt[:, half, :, :], b0[:, :, :], ACT.Copy).then_inc(qkt_ready, 1)

                    if live(f, NT):
                        copy_parts(0)
                        copy_parts(1)
                        after(act, argq_ready, f + 1)
                        after(act, ctx_ps, f - 1)
                        act.activation(qf[0:FD, 1 - par, :, 0, :], argq[0:FD, :, :], ACT.Exp, bias=w.fneg[0:FD, 0:1])
                        act.activation(qf[FD:P, 1 - par, :, 1, :], argq[FD:P, :, :], ACT.Exp,
                                       bias=w.fneg[FD:P, 0:1]).then_inc(qf_ready, 1)
                        after(act, argk_ready, f + 1)
                        after(act, kf_ready, f)
                        act.activation(kexp[:, :, :], argk[:, :, :], ACT.Exp, bias=w.fneg[:, 0:1]).then_inc(kexp_ready, 1)
                    if live(k, NT):
                        after(act, st_ps, k + 1)
                        after(act, s_ps, k)
                        act.activation(stt[:, :, :], shares, ACT.Copy, scale=w.keep[:, bass.ds(k, 1)]).then_inc(st_ready, 1)
                    if live(j, NT):
                        after(act, qn_ready, j + 1)
                        after(act, qkt_ps, 2 * j)
                        act.activation(pt[:, :, 0, :], pairs(qn), ACT.Copy).then_inc(part1, 1)
                        act.activation(pt[:, :, 3, :], pairs(qn), ACT.Copy)
                    if live(k, NT):
                        after(act, ctx_ps, k + 1)
                        after(act, ctok_ps, k)
                        act.activation(ct[:, :, :], b7[:, :, :], ACT.Copy).then_inc(ct_ready, 1)
                    if live(j, NT):
                        after(act, rest1, j + 1)
                        act.activation(pt[:, :, 1, :], pairs(rest), ACT.Copy).then_inc(part2, 1)
                    if live(n, NT):
                        after(act, ht_ps, n + 1)
                        after(act, qkv_ps, n - 1)
                        act.activation(ht[:, par, :, :], b2[:, D:2 * D].rearrange("p (c k) -> p c k", c=C),
                                       ACT.Copy).then_inc(ht_ready, 1)
                    if live(f, NT):
                        after(act, kt_ps, f + 1)
                        after(act, st_ps, f - 1)
                        act.activation(kt[:, 1 - par, :, :], b34[:, :, :], ACT.Copy).then_inc(kt_ready, 1)
                pipelined(act, NT, 6, 4, body)

            @block.tensor
            def _(pe):
                def project(half):
                    for g in range(NPAIR):
                        pe.matmul(b34[:, g, :], w.omega_a[:, g, :], qkt[:, half, g, :], start=True, stop=False)
                        mm = pe.matmul(b34[:, g, :], w.omega_b[:, g, :], qkt[:, half, g, :], start=False, stop=True)
                    return mm

                def body(n, par):
                    i, j, f, k = n - 1, n - 2, n - 3, n - 4
                    ip, fp, kp = 1 - par, 1 - par, par

                    def scores(r):
                        if r == 0:
                            after(pe, kf_ready, k + 1)
                            after(pe, qf_ready, k + 1)
                        if r < 2:
                            after(pe, at_ready if r == 0 else s_ready, 4 * k - 1 if r == 0 else k)
                        else:
                            after(pe, at_ready, 4 * k + r - 1)
                        for g in (2 * r, 2 * r + 1):
                            mm = pe.matmul(b56[r % 2][:, 2 * (g % 2):2 * (g % 2) + 2, :], kf[:, kp, g, :],
                                           qf[:, kp, g, :, :], start=True, stop=True)
                        mm.then_inc(at_ps, 1)

                    def transpose_parts(half):
                        after(pe, part3, f + 1)
                        after(pe, qkt_ready, 2 * f + half)
                        for g in range(NPAIR):
                            mm = pe.transpose(b0[:, g, :], pt[:, NPAIR * half + g, :, :].rearrange("p s e -> p (s e)"),
                                              w.identb[:, :])
                        mm.then_inc(qkt_ps, 1)

                    if live(f, NT):
                        transpose_parts(0)
                    if live(i, NT):
                        after(pe, ht_ready, i + 1)
                        after(pe, qkv_read, i)
                        after(pe, st_ready, i - 3)
                        for bank, lo, hi in ((b1, 0, 2 * D), (b2, 2 * D, 3 * D)):
                            for c in range(C):
                                mm = pe.matmul(bank[:, 0:hi - lo], ht[:, ip, c, :], w.wa[:, c, lo:hi],
                                               start=(c == 0), stop=(c == C - 1))
                        mm.then_inc(qkv_ps, 1)
                    if live(f, NT):
                        transpose_parts(1)
                        if isinstance(f, int) and f == 0:
                            pe.wait_ge(split, 6)
                        after(pe, qkt_ready, 2 * f + 1)
                        after(pe, kt_ready, f)
                        project(0).then_inc(pq_ps, 1)
                    if live(k, NT):
                        scores(0)
                        scores(1)
                    if live(f, NT):
                        after(pe, argq_ready, f + 1)
                        after(pe, qkt_ready, 2 * f + 2)
                        project(1).then_inc(pk_ps, 1)
                    if live(k, NT):
                        scores(2)
                        scores(3)
                    if live(k, NT):
                        after(pe, kt_ready, k + 1)
                        after(pe, vb_ready, k + 1)
                        after(pe, qkv_read, min(k + 4, NT) if isinstance(k, int) else k + 4)
                        for h in range(H):
                            q, s = divmod(h, 4)
                            mm = pe.matmul(shares[32 * s:32 * s + V1, q, :], vb[:, kp, h, :], kt[:, kp, h // 2, :],
                                           start=True, stop=True)
                        mm.then_inc(st_ps, 1)
                        after(pe, s_ready, k)
                        after(pe, ctx_ready, k)
                        if isinstance(k, int) and k == 0:
                            pe.wait_ge(cleared, 5)
                        for q in range(4):
                            for s in range(4):
                                h = 4 * q + s
                                pe.matmul(b7[32 * s:32 * s + V1, q, :], state[:, h, :], qf[:, kp, h // 2, h % 2, :],
                                          start=True, stop=False)
                            after(pe, at_ready, 4 * k + q + 1)
                            for s in range(4):
                                h = 4 * q + s
                                mm = pe.matmul(b7[32 * s:32 * s + V1, q, :], vb[:, kp, h, :],
                                               at[:, kp, h // 2, h % 2, :], start=False, stop=True)
                        mm.then_inc(ctx_ps, 1)
                        after(pe, st_ready, k + 1)
                        for q in range(4):
                            mm = pe.transpose(b6[:, q, :], stt[:, q, :], w.ident[:, :])
                        mm.then_inc(s_ps, 1)
                    if live(n, NT):
                        after(pe, h_ready, n + 1)
                        after(pe, ht_ready, n)
                        after(pe, qkv_read, n)
                        for c in range(C):
                            mm = pe.transpose(b2[:, D + P * c:D + P * c + P], hn[:, par, P * c:P * c + P], w.ident[:, :])
                        mm.then_inc(ht_ps, 1)
                    if live(f, NT):
                        after(pe, kf_ready, f + 1)
                        after(pe, argk_ready, f + 1)
                        for g in range(NPAIR):
                            mm = pe.transpose(b34[:, g, :], kf[:, fp, g, :], w.ident[:, :])
                        mm.then_inc(kt_ps, 1)
                    if live(k, NT):
                        after(pe, ct_ready, k + 1)
                        for q in range(4):
                            mm = pe.transpose(b7[:, q, :], ct[:, q, :], w.ident[:, :])
                        mm.then_inc(ctok_ps, 1)
                pipelined(pe, NT, 6, 4, body)


def normalise(pool, w, mv, var, rstd, mr, nmr, g, sems):
    mv_ready, var_ready, rstd_ready, mr_ready, nmr_ready, h_ready = sems
    after(pool, mv_ready, g + 1)
    pool.tensor_tensor(var[:, :], mv[:, :, 1], w.lneps[:, :], ALU.add).then_inc(var_ready, 1)
    after(pool, var_ready, g + 1)
    after(pool, h_ready, g)
    pool.tensor_tensor(rstd[:, :], var[:, :], w.minushalf[:, 0:GT], ALU.pow).then_inc(rstd_ready, 1)
    after(pool, rstd_ready, g + 1)
    pool.tensor_tensor(mr[:, :], mv[:, :, 0], rstd[:, :], ALU.mult).then_inc(mr_ready, 1)
    after(pool, mr_ready, g + 1)
    pool.tensor_tensor(nmr[:, :], mr[:, :], w.minusone[:, :], ALU.mult).then_inc(nmr_ready, 1)


def project_and_ffn(nc, w, d, tag, wo, bo, out):
    with Phase(nc, tag) as ph:
        (staged, xb_ready, ctx_ps, ct_ready, proj_ps, x1_ready, bn_done, mv_ready, var_ready, rstd_ready, mr_ready,
         nmr_ready, h_ready, ht_ps, ht_ready, z_ps, z_read, th_ready, lg_ready, top_ready, diff_ready, exp_ready,
         sum_ready, rsum_ready, above_ready, count_ready, tie_ready, rank_ready, pick_ready, gates_ready, u_ready,
         half_done, x2_ready, stored) = [ph.sem(s) for s in (
             "staged xb_ready ctx_ps ct_ready proj_ps x1_ready bn_done mv_ready var_ready rstd_ready mr_ready "
             "nmr_ready h_ready ht_ps ht_ready z_ps z_read th_ready lg_ready top_ready diff_ready exp_ready "
             "sum_ready rsum_ready above_ready count_ready tie_ready rank_ready pick_ready gates_ready u_ready "
             "half_done x2_ready stored").split()]
        cs = ph.sb("cs", [P, GT, D])
        ct = ph.sb("ct", [P, C, GT, P])
        st6 = ph.sb("st6", [P, GT, 6])
        mv = ph.sb("mv", [P, GT, 2])
        var = ph.sb("var", [P, GT])
        rstd = ph.sb("rstd", [P, GT])
        mr = ph.sb("mr", [P, GT])
        nmr = ph.sb("nmr", [P, GT])
        hn = ph.sb("hn", [P, GT, D])
        ht = ph.sb("ht", [P, C, GT, P])
        z = ph.sb("z", [P, 2, GT, 2, ZW])
        th = ph.sb("th", [P, GT, 2, D])
        lg = ph.sb("lg", [P, GT, E])
        top = ph.sb("top", [P, GT])
        diff = ph.sb("diff", [P, GT, E])
        ex = ph.sb("ex", [P, GT, E])
        total = ph.sb("total", [P, GT])
        half_r = ph.sb("half_r", [P, GT])
        above = ph.sb("above", [P, GT, E])
        rank = ph.sb("rank", [P, GT])
        tie = ph.sb("tie", [P, GT])
        pick = ph.sb("pick", [P, 2, GT])
        gates = ph.sb("gates", [P, 2, GT])

        bt = [ph.ps("bt0", [P, GT, P]), ph.ps("bt1", [P, GT, P])]
        proj = [ph.ps("proj0", [P, 2, D]), ph.ps("proj1", [P, 2, D])]
        bz = [ph.ps("bz0", [P, 2, 2 * D]), ph.ps("bz1", [P, 2, 2 * D])]

        def xg(g, t0=0, n=GT):
            return w.x[:, bass.ds(g * GT + t0, n), :]

        def experts(zp, hf):
            return z[:, zp, 2 * hf:2 * hf + 2, :, :].rearrange("p t e c -> p (t e) c")[:, :, 0:D]

        def tanhs(hf):
            return th[:, 2 * hf:2 * hf + 2, :, :].rearrange("p t e c -> p (t e) c")

        with nc.Block() as block:
            @block.gpsimd
            def _(pool):
                def body(n, par):
                    g = n - 1
                    if live(n, NG):
                        pool.tensor_tensor(xg(n), xg(n), bo[:, :].unsqueeze(1).broadcast_to([P, GT, D]),
                                           ALU.add).then_inc(xb_ready, 1)
                    if live(g, NG):
                        normalise(pool, w, mv, var, rstd, mr, nmr, g,
                                  (mv_ready, var_ready, rstd_ready, mr_ready, nmr_ready, h_ready))
                pipelined(pool, NG, 4, 1, body)

            @block.vector
            def _(dve):
                def body(n, par):
                    g, i, y = n - 1, n - 2, n - 3
                    zp = 1 - par
                    if live(y, NG):
                        after(dve, z_read, GT * y + GT)
                        dve.tensor_copy(lg[:, :, :].rearrange("p t (e c) -> p t e c", e=2),
                                        z[:, zp, :, :, D:ZW]).then_inc(lg_ready, 1)
                        dve.wait_ge(lg_ready, y + 1)
                        dve.tensor_reduce(top[:, :], lg[:, :, :], AX.X, ALU.max).then_inc(top_ready, 1)
                        dve.tensor_tensor(above[:, :, :], lg[:, :, :], lg[:, :, 1:2].broadcast_to([P, GT, E]),
                                          ALU.is_gt).then_inc(above_ready, 1)
                        dve.tensor_tensor(tie[:, :], lg[:, :, 0], lg[:, :, 1], ALU.is_equal).then_inc(tie_ready, 1)
                        dve.wait_ge(top_ready, y + 1)
                        after(dve, exp_ready, y)
                        dve.tensor_tensor(diff[:, :, :], lg[:, :, :], top[:, :].unsqueeze(2).broadcast_to([P, GT, E]),
                                          ALU.subtract).then_inc(diff_ready, 1)
                        dve.wait_ge(above_ready, y + 1)
                        dve.tensor_reduce(rank[:, :], above[:, :, :], AX.X, ALU.add).then_inc(count_ready, 1)
                        dve.tensor_tensor(pick[:, 0, :], lg[:, :, 0], top[:, :], ALU.is_equal)
                        dve.wait_ge(count_ready, y + 1)
                        dve.wait_ge(tie_ready, y + 1)
                        dve.tensor_tensor(rank[:, :], rank[:, :], tie[:, :], ALU.add).then_inc(rank_ready, 1)
                        for hf in range(2):
                            after(dve, th_ready, 2 * y + hf + 1)
                            dve.scalar_tensor_tensor(out=experts(zp, hf), in0=tanhs(hf), scalar=1.0, in1=experts(zp, hf),
                                                     op0=ALU.add, op1=ALU.mult).then_inc(u_ready, 1)
                        dve.wait_ge(exp_ready, y + 1)
                        dve.tensor_reduce(total[:, :], ex[:, :, :], AX.X, ALU.add).then_inc(sum_ready, 1)
                        dve.wait_ge(rank_ready, y + 1)
                        dve.scalar_tensor_tensor(out=pick[:, 1, :], in0=rank[:, :], scalar=1.0, in1=ex[:, :, 1],
                                                 op0=ALU.is_equal, op1=ALU.mult).then_inc(pick_ready, 1)
                        dve.wait_ge(sum_ready, y + 1)
                        dve.reciprocal(half_r[:, :], total[:, :]).then_inc(rsum_ready, 1)
                    if live(g, NG):
                        after(dve, proj_ps, 2 * g + 2)
                        after(dve, xb_ready, g + 1)
                        for hf in range(2):
                            last = dve.tensor_tensor(xg(g, 2 * hf, 2), proj[hf][:, :, :], xg(g, 2 * hf, 2), ALU.add)
                        last.then_inc(x1_ready, 1)
                        dve.wait_ge(x1_ready, g + 1)
                        after(dve, mv_ready, g)
                    if live(y, NG):
                        dve.wait_ge(rsum_ready, y + 1)
                        dve.wait_ge(pick_ready, y + 1)
                        for e in range(2):
                            last = dve.scalar_tensor_tensor(out=gates[:, e, :], in0=pick[:, e, :], scalar=0.5,
                                                            in1=half_r[:, :], op0=ALU.mult, op1=ALU.mult)
                        last.then_inc(gates_ready, 1)

                    def add_expert(e):
                        for t in range(GT):
                            xt = w.x[:, y * GT + t, :]
                            last = dve.scalar_tensor_tensor(out=xt, in0=z[:, zp, t, e, 0:D],
                                                            scalar=gates[:, e, t:t + 1], in1=xt,
                                                            op0=ALU.mult, op1=ALU.add)
                        last.then_inc(x2_ready if e else half_done, 1)

                    def read_z(t):
                        after(dve, z_ps, GT * i + t + 1)
                        if t == 0:
                            after(dve, x2_ready, i - 1)
                        dve.tensor_tensor(z[:, par, t, :, :], bz[t % 2][:, :, 0:ZW], w.bf[:, :, :],
                                          ALU.add).then_inc(z_read, 1)

                    if live(g, NG):
                        for t in range(GT):
                            last = dve.bn_stats(st6[:, t, :], w.x[:, g * GT + t, :])
                        last.then_inc(bn_done, 1)
                        dve.wait_ge(bn_done, g + 1)
                        after(dve, nmr_ready, g)
                    if live(i, NG):
                        read_z(0)
                    if live(g, NG):
                        for t in range(GT):
                            last = dve.bn_aggr(mv[:, t, :], st6[:, t, :])
                        last.then_inc(mv_ready, 1)
                    if live(y, NG):
                        dve.wait_ge(u_ready, 2 * y + 2)
                        dve.wait_ge(gates_ready, y + 1)
                        dve.wait_ge(h_ready, y + 1)
                        add_expert(0)
                    if live(i, NG):
                        read_z(1)
                    if live(y, NG):
                        dve.wait_ge(half_done, y + 1)
                        add_expert(1)
                    if live(i, NG):
                        read_z(2)
                        read_z(3)
                pipelined(dve, NG, 4, 3, body)

            @block.scalar
            def _(act):
                def take_tanh(g, zp, hf):
                    after(act, z_read, GT * g + 2 * hf + 2)
                    after(act, u_ready, 2 * g + hf - 1)
                    act.activation(tanhs(hf), experts(zp, hf), ACT.Tanh, scale=0.5).then_inc(th_ready, 1)

                def body(n, par):
                    g, i, y = n - 1, n - 2, n - 3
                    if live(y, NG):
                        take_tanh(y, 1 - par, 1)
                        after(act, diff_ready, y + 1)
                        after(act, pick_ready, y)
                        act.activation(ex[:, :, :], diff[:, :, :], ACT.Exp).then_inc(exp_ready, 1)
                    if live(n, NG):
                        after(act, ctx_ps, 2 * n)
                        act.activation(cs[:, :, :].rearrange("p t (h e) -> p h t e", h=H),
                                       w.mix[:, n // (NG // B), :, bass.ds((n % (NG // B)) * GT, GT), :],
                                       ACT.Copy).then_inc(staged, 1)
                    if live(i, NG):
                        for c in range(C):
                            after(act, ht_ps, 2 * i + c + 1)
                            if c == 0:
                                after(act, z_ps, GT * i)
                            act.activation(ht[:, c, :, :], bt[c][:, :, :], ACT.Copy).then_inc(ht_ready, 1)
                    if live(n, NG):
                        for c in range(C):
                            after(act, ctx_ps, 2 * n + c + 1)
                            if c == 0:
                                after(act, proj_ps, 2 * n)
                            act.activation(ct[:, c, :, :], bt[c][:, :, :], ACT.Copy).then_inc(ct_ready, 1)
                    if live(g, NG):
                        after(act, nmr_ready, g + 1)
                        after(act, ht_ps, 2 * g)
                        for t in range(GT):
                            last = act.activation(hn[:, t, :], w.x[:, g * GT + t, :], ACT.Identity,
                                                  scale=rstd[:, t:t + 1], bias=nmr[:, t:t + 1])
                        last.then_inc(h_ready, 1)
                    if live(i, NG):
                        take_tanh(i, par, 0)
                pipelined(act, NG, 4, 3, body)

            @block.tensor
            def _(pe):
                def body(n, par):
                    g, i = n - 1, n - 2
                    if live(i, NG):
                        after(pe, h_ready, i + 1)
                        for c in range(C):
                            after(pe, ct_ready, min(2 * (n - 1) + c + 1, 2 * NG) if isinstance(n, int) else 2 * n + (c - 1))
                            for t in range(GT):
                                mm = pe.transpose(bt[c][:, t, :], hn[:, t, P * c:P * c + P], w.ident[:, :])
                            mm.then_inc(ht_ps, 1)
                    if live(g, NG):
                        after(pe, ct_ready, 2 * g + 2)
                        after(pe, x1_ready, g)
                        for hf in range(2):
                            for t in range(2):
                                for c in range(C):
                                    mm = pe.matmul(proj[hf][:, t, :], ct[:, c, 2 * hf + t, :], wo[:, c, :],
                                                   start=(c == 0), stop=(c == C - 1))
                            mm.then_inc(proj_ps, 1)
                    if live(n, NG):
                        after(pe, staged, n + 1)
                        for c in range(C):
                            after(pe, ht_ready, 2 * i + c + 1)
                            for t in range(GT):
                                mm = pe.transpose(bt[c][:, t, :], cs[:, t, P * c:P * c + P], w.ident[:, :])
                            mm.then_inc(ctx_ps, 1)
                    if live(i, NG):
                        after(pe, ht_ready, 2 * i + 2)
                        for t in range(GT):
                            after(pe, z_read, GT * i + t - 1)
                            for e in range(2):
                                for c in range(C):
                                    mm = pe.matmul(bz[t % 2][:, e, 0:ZW], ht[:, c, t, :], w.wf[:, c, ZW * e:ZW * e + ZW],
                                                   start=(c == 0), stop=(c == C - 1))
                            mm.then_inc(z_ps, 1)
                pipelined(pe, NG, 4, 2, body)

            @block.sync
            def _(sp):
                if out is None:
                    return
                rows = out.rearrange("b (g t p) d -> (b g) p t d", p=P, t=GT)

                def body(n, par):
                    sp.wait_ge(x2_ready, 1)
                    after(sp, x2_ready, n + 1)
                    sp.dma_start(rows[n], xg(n)).then_inc(stored, 16)
                pipelined(sp, NG, 2, 0, body)
                sp.wait_ge(stored, 16 * NG)


def prepare_b(nc, w, d):
    with Phase(nc, "pb") as ph:
        (bn_done, mv_ready, var_ready, rstd_ready, mr_ready, nmr_ready, h_ready, ht_ps, ht_ready, qk_ps, qk_read, v_ps,
         v_read, ss_ready, ms_ready, root_ready, inv_ready, square_ready, error_ready, factor_ready, rn_ready,
         qn_ready, kw_ready, part1, rest1, part2, part3, pt_ps, pt_ready) = [ph.sem(s) for s in (
             "bn_done mv_ready var_ready rstd_ready mr_ready nmr_ready h_ready ht_ps ht_ready qk_ps qk_read v_ps "
             "v_read ss_ready ms_ready root_ready inv_ready square_ready error_ready factor_ready rn_ready "
             "qn_ready kw_ready part1 rest1 part2 part3 pt_ps pt_ready").split()]
        stored = [ph.sem("stored0"), ph.sem("stored1")]
        last_pt_ready = ph.sem("last_pt_ready")
        sq_ready = [ph.sem("sq_ready0"), ph.sem("sq_ready1")]
        st6 = ph.sb("st6", [P, GT, 6])
        mv = ph.sb("mv", [P, GT, 2])
        var = ph.sb("var", [P, GT])
        rstd = ph.sb("rstd", [P, GT])
        mr = ph.sb("mr", [P, GT])
        nmr = ph.sb("nmr", [P, GT])
        hn = ph.sb("hn", [P, GT, D])
        ht = ph.sb("ht", [P, C, GT, P])
        qk = ph.sb("qk", [P, 2, GT, 2 * D])
        sq = ph.sb("sq", [P, GT, 2 * D])
        rest = ph.sb("rest", [P, GT, 2 * D])
        BLOCKS = 2 * GT
        COPIES = BLOCKS - 1
        HG = GT // 2 * 2 * H
        ss, ms, root, inv, half_inv, square, error, factor, rn = [ph.sb(s, [P, 2, HG]) for s in (
            "ss", "ms", "root", "inv", "half_inv", "square", "error", "factor", "rn")]
        pt = ph.sb("pt", [P, 2, GT, 2 * H, PARTS, HD], BF16)
        stage = ph.sb("stage", [2 * HROWS, 2, 2, NPAIR, GT, P], BF16)

        b0 = ph.ps("b0", [P, GT, P])
        b1 = ph.ps("b1", [P, GT, P])
        bqk = [ph.ps("bqk0", [P, 2 * D]), ph.ps("bqk1", [P, 2 * D])]
        bv = ph.ps("bv", [P, GT, D])
        bp = [ph.ps("bp0", [P, NPAIR, P], BF16), ph.ps("bp1", [P, NPAIR, P], BF16)]
        parts = [d["parts_q"], d["parts_k"]]

        def heads(tile, hf):
            return tile[:, 2 * hf:2 * hf + 2, :].rearrange("p t (g e) -> p (t g) e", e=HD)

        def part(pp, n, hf):
            return pt[:, pp, 2 * hf:2 * hf + 2, :, n, :].rearrange("p t g e -> p (t g) e")

        def wait_stored(eng, s, parity):
            if isinstance(s, int):
                after(eng, stored[parity], 32 * ((s - parity) // 2))
            else:
                eng.wait_ge(stored[parity], 16 * (s - parity))

        with nc.Block() as block:
            @block.gpsimd
            def _(pool):
                def newton(k, hf):
                    after(pool, inv_ready, k + 1)
                    pool.tensor_tensor(square[:, hf, :], inv[:, hf, :], inv[:, hf, :], ALU.mult).then_inc(square_ready, 1)
                    after(pool, square_ready, k + 1)
                    pool.tensor_tensor(error[:, hf, :], square[:, hf, :], ms[:, hf, :], ALU.mult).then_inc(error_ready, 1)
                    after(pool, error_ready, k + 1)
                    pool.tensor_tensor(factor[:, hf, :], error[:, hf, :], w.three[:, 0:1].broadcast_to([P, HG]),
                                       ALU.subtract).then_inc(factor_ready, 1)
                    pool.tensor_tensor(half_inv[:, hf, :], inv[:, hf, :], w.minushalf[:, 0:1].broadcast_to([P, HG]),
                                       ALU.mult).then_inc(factor_ready, 1)
                    after(pool, factor_ready, 2 * k + 2)
                    after(pool, qn_ready, k - 1)
                    pool.tensor_tensor(rn[:, hf, :], half_inv[:, hf, :], factor[:, hf, :], ALU.mult).then_inc(rn_ready, 1)

                def weigh(y, yp, hf):
                    after(pool, qn_ready, 2 * y + hf + 1)
                    k = qk[:, yp, 2 * hf:2 * hf + 2, D:2 * D].rearrange("p t (h e) -> p t h e", e=HD)
                    for t in range(2):
                        last = pool.tensor_tensor(k[:, t], k[:, t], w.wqk[:, :].unsqueeze(1).broadcast_to([P, H, HD]), ALU.mult)
                    last.then_inc(kw_ready, 1)

                def body(n, par):
                    i, y = n - 1, n - 2
                    if live(y, NG):
                        weigh(y, par, 0)
                        newton(2 * y + 1, 1)
                    if live(n, NG):
                        normalise(pool, w, mv, var, rstd, mr, nmr, n,
                                  (mv_ready, var_ready, rstd_ready, mr_ready, nmr_ready, h_ready))
                    if live(y, NG):
                        weigh(y, par, 1)
                    if live(i, NG):
                        after(pool, qk_read, GT * i + 2)
                        after(pool, ss_ready, 2 * i - 1)
                        pool.tensor_tensor(heads(sq, 0), heads(qk[:, 1 - par, :, :], 0), heads(qk[:, 1 - par, :, :], 0),
                                           ALU.mult).then_inc(sq_ready[0], 1)
                        newton(2 * i, 0)
                pipelined(pool, NG, 4, 2, body)

            @block.vector
            def _(dve):
                def norms(g, hf):
                    k = 2 * g + hf
                    after(dve, sq_ready[hf], g + 1)
                    dve.tensor_reduce(ss[:, hf, :], heads(sq, hf), AX.X, ALU.add).then_inc(ss_ready, 1)
                    dve.wait_ge(ss_ready, k + 1)
                    after(dve, rn_ready, k - 1)
                    dve.tensor_scalar(ms[:, hf, :], ss[:, hf, :], HD * RMS_EPS, None, ALU.add).then_inc(ms_ready, 1)

                def invert(g, hf):
                    k = 2 * g + hf
                    after(dve, root_ready, k + 1)
                    dve.reciprocal(inv[:, hf, :], root[:, hf, :]).then_inc(inv_ready, 1)

                def scale(y, yp, hf):
                    v = heads(qk[:, yp, :, :], hf)
                    after(dve, rn_ready, 2 * y + hf + 1)
                    dve.tensor_tensor(v, v, rn[:, hf, :].unsqueeze(2).broadcast_to([P, HG, HD]), ALU.mult).then_inc(qn_ready, 1)

                def first_rest(y, yp, hf):
                    after(dve, part1, 2 * y + hf + 1)
                    after(dve, part3, 2 * y + hf - 1)
                    dve.tensor_tensor(heads(rest, hf), heads(qk[:, yp, :, :], hf), part(yp, 0, hf), ALU.subtract).then_inc(rest1, 1)

                def last_part(y, yp, hf):
                    after(dve, part2, 2 * y + hf + 1)
                    dve.tensor_tensor(part(yp, 2, hf), heads(rest, hf), part(yp, 1, hf), ALU.subtract).then_inc(part3, 1)

                def read_qk(i, ip, t):
                    after(dve, qk_ps, GT * i + t + 1)
                    if t == 0:
                        after(dve, part1, 2 * (i - 1))
                        after(dve, rest1, 2 * (i - 1))
                    dve.tensor_tensor(qk[:, ip, t, :], bqk[t % 2][:, :], w.bb[:, 0:2 * D], ALU.add).then_inc(qk_read, 1)

                def body(n, par):
                    i, y, s = n - 1, n - 2, n - 3
                    ip, yp = 1 - par, par
                    if live(n, NG):
                        after(dve, mv_ready, n)
                    if live(y, NG):
                        scale(y, yp, 0)
                        norms(y, 1)
                    if live(n, NG):
                        for t in range(GT):
                            last = dve.bn_stats(st6[:, t, :], w.x[:, n * GT + t, :])
                        last.then_inc(bn_done, 1)
                    if live(y, NG):
                        invert(y, 1)
                    if live(n, NG):
                        dve.wait_ge(bn_done, n + 1)
                        after(dve, nmr_ready, n)
                    if live(i, NG):
                        read_qk(i, ip, 0)
                    if live(n, NG):
                        for t in range(GT):
                            last = dve.bn_aggr(mv[:, t, :], st6[:, t, :])
                        last.then_inc(mv_ready, 1)
                    if live(y, NG):
                        first_rest(y, yp, 0)
                        scale(y, yp, 1)
                    if live(i, NG):
                        read_qk(i, ip, 1)
                    if live(y, NG):
                        last_part(y, yp, 0)
                    if live(i, NG):
                        read_qk(i, ip, 2)
                    if live(y, NG):
                        first_rest(y, yp, 1)
                    if live(i, NG):
                        norms(i, 0)
                    if live(y, NG):
                        last_part(y, yp, 1)
                    if live(i, NG):
                        invert(i, 0)
                        read_qk(i, ip, 3)
                    if live(s, NG):
                        after(dve, pt_ps, BLOCKS * (s + 1))
                        wait_stored(dve, s, ip)
                        dve.tensor_copy(stage[:, ip, 1, :, GT - 1, :], bp[1][0:2 * HROWS, :, :]).then_inc(last_pt_ready, 1)
                    if live(i, NG):
                        after(dve, v_ps, i + 1)
                        dve.tensor_tensor(
                            w.mix[:, i // (NG // B), :, bass.ds((i % (NG // B)) * GT, GT), :],
                            bv[:, :, :].rearrange("p t (h e) -> p h t e", h=H),
                            w.bb[:, 2 * D:3 * D].rearrange("p (h e) -> p h e", h=H).unsqueeze(2).broadcast_to([P, H, GT, HD]),
                            ALU.add).then_inc(v_read, 1)
                pipelined(dve, NG, 4, 3, body)

            @block.scalar
            def _(act):
                def square_second(y, yp):
                    after(act, qk_read, GT * y + GT)
                    after(act, ss_ready, 2 * y)
                    act.activation(heads(sq, 1), heads(qk[:, yp, :, :], 1), ACT.Square).then_inc(sq_ready[1], 1)

                def take_root(k, hf):
                    after(act, ms_ready, k + 1)
                    act.activation(root[:, hf, :], ms[:, hf, :], ACT.Sqrt).then_inc(root_ready, 1)

                def first_part(y, yp, hf):
                    after(act, kw_ready, 2 * y + hf + 1)
                    after(act, pt_ps, BLOCKS * (y - 1))
                    act.activation(part(yp, 0, hf), heads(qk[:, yp, :, :], hf), ACT.Copy).then_inc(part1, 1)

                def second_part(y, yp, hf):
                    after(act, rest1, 2 * y + hf + 1)
                    act.activation(part(yp, 1, hf), heads(rest, hf), ACT.Copy).then_inc(part2, 1)

                def norm(g, t0):
                    if t0 == 0:
                        after(act, nmr_ready, g + 1)
                        after(act, ht_ps, 2 * g)
                    for t in (t0, t0 + 1):
                        last = act.activation(hn[:, t, :], w.x[:, g * GT + t, :], ACT.Identity,
                                              scale=rstd[:, t:t + 1], bias=nmr[:, t:t + 1])
                    return last

                def stage_parts(s, sp_, t, i):
                    after(act, pt_ps, BLOCKS * s + 2 * t + i + 1)
                    if t == 0:
                        wait_stored(act, s, sp_)
                    act.activation(stage[:, sp_, i, :, t, :], bp[i][0:2 * HROWS, :, :], ACT.Copy).then_inc(pt_ready, 1)

                def body(n, par):
                    i, y, s = n - 1, n - 2, n - 3
                    ip, yp, sp_ = 1 - par, par, 1 - par
                    if live(i, NG):
                        for c, bank in enumerate((b0, b1)):
                            after(act, ht_ps, 2 * i + c + 1)
                            if c == 0:
                                after(act, v_ps, i)
                            act.activation(ht[:, c, :, :], bank[:, :, :], ACT.Copy).then_inc(ht_ready, 1)
                    if live(y, NG):
                        square_second(y, yp)
                    if live(s, NG):
                        stage_parts(s, sp_, 0, 0)
                    if live(y, NG):
                        take_root(2 * y + 1, 1)
                        first_part(y, yp, 0)
                    if live(s, NG):
                        stage_parts(s, sp_, 0, 1)
                        stage_parts(s, sp_, 1, 0)
                    if live(y, NG):
                        second_part(y, yp, 0)
                    if live(s, NG):
                        stage_parts(s, sp_, 1, 1)
                        stage_parts(s, sp_, 2, 0)
                    if live(y, NG):
                        first_part(y, yp, 1)
                    if live(n, NG):
                        norm(n, 0)
                    if live(s, NG):
                        stage_parts(s, sp_, 2, 1)
                    if live(y, NG):
                        second_part(y, yp, 1)
                    if live(n, NG):
                        norm(n, 2).then_inc(h_ready, 1)
                    if live(i, NG):
                        take_root(2 * i, 0)
                    if live(s, NG):
                        stage_parts(s, sp_, 3, 0)
                pipelined(act, NG, 4, 3, body)

            @block.tensor
            def _(pe):
                def transpose_parts(s, sp_, t, i):
                    after(pe, part3, 2 * s + t // 2 + 1)
                    if 2 * t + i == 1:
                        after(pe, last_pt_ready, s)
                    else:
                        after(pe, pt_ready, COPIES * s + max(2 * t + i - 1, 0))
                    for g in range(NPAIR):
                        h = H * i + 2 * g
                        mm = pe.transpose(bp[i][0:2 * HROWS, g, :],
                                          pt[:, sp_, t, h:h + 2, :, :].rearrange("p h n e -> p (h n e)"), w.identb[:, :])
                    mm.then_inc(pt_ps, 1)

                def body(n, par):
                    i, s, sp_ = n - 1, n - 3, 1 - par
                    if live(i, NG):
                        after(pe, h_ready, i + 1)
                        after(pe, ht_ready, 2 * i)
                        for c, bank in enumerate((b0, b1)):
                            for t in range(GT):
                                mm = pe.transpose(bank[:, t, :], hn[:, t, P * c:P * c + P], w.ident[:, :])
                            mm.then_inc(ht_ps, 1)
                    for t in range(GT):
                        if live(s, NG):
                            transpose_parts(s, sp_, t, 0)
                        if live(i, NG):
                            after(pe, ht_ready, 2 * i + 2)
                            after(pe, qk_read, GT * i + t - 1)
                            for c in range(C):
                                mm = pe.matmul(bqk[t % 2][:, :], ht[:, c, t, :], w.wb[:, c, 0:2 * D],
                                               start=(c == 0), stop=(c == C - 1))
                            mm.then_inc(qk_ps, 1)
                        if live(s, NG):
                            transpose_parts(s, sp_, t, 1)
                        if live(i, NG):
                            after(pe, v_read, i)
                            for c in range(C):
                                mm = pe.matmul(bv[:, t, :], ht[:, c, t, :], w.wb[:, c, 2 * D:3 * D],
                                               start=(c == 0), stop=(c == C - 1))
                            if t == GT - 1:
                                mm.then_inc(v_ps, 1)
                pipelined(pe, NG, 4, 3, body)

            @block.sync
            def _(sp):
                def body(n, par):
                    sp.wait_ge(pt_ready, COPIES)
                    after(sp, pt_ready, COPIES * (n + 1))
                    after(sp, last_pt_ready, n + 1)
                    for i in range(2):
                        rows = parts[i].rearrange("(b g h) r (s c) -> b s (h r) g c", b=B, h=2, s=NG // B)
                        sp.dma_start(rows[n // (NG // B), n % (NG // B)],
                                     stage[:, par, i, :, :, :].rearrange("p g t c -> p g (t c)")).then_inc(stored[par], 16)
                pipelined(sp, NG, 2, 0, body)
                for q in range(2):
                    sp.wait_ge(stored[q], 16 * NG)


def load_queries(sp, d, hh, qs, sem):
    q = d["parts_q"][hh]
    sp.dma_start(qs[0:HROWS, :], q).then_inc(sem, 16)
    sp.dma_start(qs[HROWS:HROWS + 2 * HD, :], q[0:2 * HD, :]).then_inc(sem, 16)
    sp.dma_start(qs[HROWS + 2 * HD:SROWS, :], q[0:HD, :]).then_inc(sem, 16)
    sp.dma_start(qs[SROWS:KROWS, :], d["mrow"][bass.ds(hh, 1), :]).then_inc(sem, 16)


def load_keys(sp, d, hh, ks, sem):
    k = d["parts_k"][hh]
    row = 0
    for n, copies in enumerate((3, 2, 1)):
        sp.dma_start(ks[row:row + copies * HD, :],
                     k[HD * n:HD * n + HD, :].unsqueeze(0).broadcast_to([copies, HD, T])).then_inc(sem, 16)
        row += copies * HD


def load_stacks(sp, d, hh, qs, ks, sem):
    load_queries(sp, d, hh, qs, sem)
    load_keys(sp, d, hh, ks, sem)


STACK_DMAS = 7


def score_maxima(nc, w, d):
    with Phase(nc, "mx") as ph:
        loaded, ones, s_ps, s_read, neg_ready, t_ps, row_ready, stored = [ph.sem(s) for s in (
            "loaded ones s_ps s_read neg_ready t_ps row_ready stored").split()]
        qs = ph.sb("qs", [KROWS, T], BF16)
        ks = ph.sb("ks", [KROWS, T], BF16)
        neg = ph.sb("neg", [P, KT])
        row = ph.sb("row", [KT, P], BF16)
        sps = ph.ps("sps", [P, T])
        tps = ph.ps("tps", [KT, P])
        with nc.Block() as block:
            @block.sync
            def _(sp):
                unbounded = sp.value_load(w.flag[0:1, 0:1], min_val=0, max_val=1)
                with sp.If(unbounded > 0):
                    sp.sem_inc(stored, 16)
                    with sp.Fori(0, B * H) as hh:
                        load_stacks(sp, d, hh, qs, ks, loaded)
                        sp.wait_ge(row_ready, hh + 1)
                        sp.dma_start(d["mrow"][bass.ds(hh, 1), :].rearrange("a (t p) -> (a t) p", p=P), row[:, :]).then_inc(stored, 16)
                    sp.wait_ge(stored, 16 * B * H + 16)
                    sp.nop()

            @block.gpsimd
            def _(pool):
                pool.memset(ks[SROWS:KROWS, :], 1.0).then_inc(ones, 1)

            @block.tensor
            def _(pe):
                unbounded = pe.value_load(w.flag[0:1, 0:1], min_val=0, max_val=1)
                with pe.If(unbounded > 0):
                    pe.wait_ge(ones, 1)
                    with pe.Fori(0, B * H) as hh:
                        pe.wait_ge(loaded, 16 * STACK_DMAS * (hh + 1))
                        for t in range(KT):
                            if t:
                                pe.wait_ge(s_read, KT * hh + t)
                            for c in range(4):
                                mm = pe.matmul(sps[:, 512 * c:512 * c + 512], qs[:, P * t:P * t + P],
                                               ks[:, 512 * c:512 * c + 512], start=True, stop=True)
                            mm.then_inc(s_ps, 1)
                        pe.wait_ge(neg_ready, hh + 1)
                        pe.transpose(tps[:, :], neg[:, :], w.ident[:, :]).then_inc(t_ps, 1)
                    pe.nop()

            @block.vector
            def _(dve):
                unbounded = dve.value_load(w.flag[0:1, 0:1], min_val=0, max_val=1)
                with dve.If(unbounded > 0):
                    with dve.Fori(0, B * H) as hh:
                        for t in range(KT):
                            dve.wait_ge(s_ps, KT * hh + t + 1)
                            ins = dve.tensor_reduce(neg[:, t:t + 1], sps[:, :], AX.X, ALU.max, negate=True)
                            ins.then_inc(s_read if t < KT - 1 else neg_ready, 1)
                            if t == KT - 1:
                                dve.wait_ge(neg_ready, hh + 1)
                                dve.sem_inc(s_read, 1)
                        dve.wait_ge(t_ps, hh + 1)
                        dve.wait_ge(stored, 16 * hh + 16)
                        dve.tensor_copy(row[:, :], tps[:, :]).then_inc(row_ready, 1)
                    dve.nop()


def attention_b(nc, w, d):
    with Phase(nc, "sa") as ph:
        loaded = [ph.sem("loaded0"), ph.sem("loaded1")]
        cleared, ones_ready, v_ready, s_ps, p_ready, z_ps, zt_ready, ztok_ps, rden_ready, z_ready = [ph.sem(s) for s in (
            "cleared ones_ready v_ready s_ps p_ready z_ps zt_ready ztok_ps rden_ready z_ready").split()]
        QC = 4
        W = T // QC
        UNITS = KT * QC
        SIZES = [2] * 31 + [1] * 2
        assert sum(SIZES) == UNITS
        GROUPS = len(SIZES)
        starts = [sum(SIZES[:g]) for g in range(GROUPS)]
        RING = 3
        PB = 6
        qs = [ph.sb(f"qs{i}", [KROWS, T], BF16) for i in range(2)]
        ks = [ph.sb(f"ks{i}", [KROWS, T], BF16) for i in range(2)]
        vs = ph.sb("vs", [P, 2, KT, V1])
        pr = ph.sb("pr", [P, PB, 2, W])
        zt = ph.sb("zt", [P, QC, P])
        rden = ph.sb("rden", [P, QC, 4])
        bs = [ph.ps(f"bs{i}", [P, 2, W]) for i in range(RING)]
        bz = [ph.ps("bz0", [P, 4, P]), ph.ps("bz1", [P, 4, P])]
        heads = w.mix[:, :, :, :, :].rearrange("p b h t e -> p (b h) t e")
        LAG = 3
        fours = [(starts[g - LAG] + SIZES[g - LAG]) // QC if g >= LAG else 0 for g in range(GROUPS)]
        last_four = [(starts[g] + SIZES[g] - 1) // QC for g in range(GROUPS)]
        N = B * H

        with nc.Block() as block:
            @block.sync
            def _(sp):
                def body(n, par):
                    if not isinstance(n, int):
                        sp.wait_ge(s_ps, GROUPS)
                    after(sp, s_ps, GROUPS * (n - 1))
                    load_queries(sp, d, n, qs[par], loaded[par])
                    if not isinstance(n, int) or n:
                        load_keys(sp, d, n, ks[par], loaded[par])
                pipelined(sp, N, 2, 0, body)

            @block.gpsimd
            def _(pool):
                pool.memset(vs[:, :, :, :], 1.0).then_inc(ones_ready, 1)
                pool.wait_ge(ones_ready, 1)

                def body(n, par):
                    after(pool, z_ps, KT * (n - 1))
                    pool.tensor_copy(vs[:, par, :, 0:HD], heads[:, n, :, :]).then_inc(v_ready, 1)
                pipelined(pool, N, 2, 0, body)

            @block.scalar
            def _(act):
                def body(n, par):
                    for g in range(GROUPS):
                        at = GROUPS * n + g
                        act.wait_ge(s_ps, at + 1)
                        if g >= PB:
                            act.wait_ge(z_ps, KT * n + last_four[g - PB] + 1)
                        else:
                            after(act, z_ps, KT * (n - 1) + last_four[g - PB + GROUPS] + 1)
                        s = SIZES[g]
                        act.activation(pr[:, (GROUPS * par + g) % PB, 0:s, :], bs[g % RING][:, 0:s, :], ACT.Exp).then_inc(p_ready, 1)
                load_keys(act, d, 0, ks[0], loaded[0])
                pipelined(act, N, 2, 0, body)

            @block.vector
            def _(dve):
                dve.memset(ks[0][SROWS:KROWS, :], 1.0).then_inc(cleared, 1)
                for i in range(2):
                    dve.memset(bz[i][:, :, :], 0.0).then_inc(cleared, 1)
                dve.memset(ks[1][SROWS:KROWS, :], 1.0).then_inc(cleared, 1)

                def body(n, par):
                    after(dve, z_ps, KT * (n + 1))
                    after(dve, ztok_ps, n)
                    dve.tensor_copy(zt[:, :, :], bz[par][:, :, :]).then_inc(zt_ready, 1)
                    after(dve, ztok_ps, n + 1)
                    tok = bz[par][:, :, :].rearrange("p i (j s) -> p i j s", j=QC)
                    dve.reciprocal(rden[:, :, :], tok[:, :, :, HD]).then_inc(rden_ready, 1)
                    dve.wait_ge(rden_ready, n + 1)
                    dve.tensor_tensor(heads[:, n, :, :].rearrange("p (j i) e -> p i j e", j=QC), tok[:, :, :, 0:HD],
                                      rden[:, :, :].unsqueeze(3).broadcast_to([P, QC, 4, HD]), ALU.mult).then_inc(z_ready, 1)
                pipelined(dve, N, 2, 0, body)

            @block.tensor
            def _(pe):
                pe.wait_ge(cleared, 3)

                def products(n, par, lo, hi):
                    for f in range(lo, hi):
                        for j in range(QC):
                            u = QC * f + j
                            g = max(i for i in range(GROUPS) if starts[i] <= u)
                            buf = (GROUPS * par + g) % PB
                            mm = pe.matmul(bz[par][32 * j:32 * j + V1, :, :], vs[:, par, f, :],
                                           pr[:, buf, u - starts[g], :], start=(f == 0), stop=(f == KT - 1))
                        mm.then_inc(z_ps, 1)

                def tokens(n, par):
                    after(pe, zt_ready, n + 1)
                    for i in range(4):
                        mm = pe.transpose(bz[par][:, i, :], zt[:, i, :], w.ident[:, :])
                    mm.then_inc(ztok_ps, 1)

                def body(n, par):
                    if isinstance(n, int) and n == 1:
                        pe.wait_ge(cleared, 4)
                    done = 0
                    for g in range(GROUPS):
                        if g == 0:
                            pe.wait_ge(loaded[par], 16 * STACK_DMAS * ((n - par) // 2 + 1) if isinstance(n, int)
                                       else 8 * STACK_DMAS * (n - par) + 16 * STACK_DMAS)
                        after(pe, p_ready, GROUPS * n + g - LAG + 1)
                        for u in range(starts[g], starts[g] + SIZES[g]):
                            t, j = divmod(u, QC)
                            mm = pe.matmul(bs[g % RING][:, u - starts[g], :], ks[par][:, P * t:P * t + P],
                                           qs[par][:, W * j:W * j + W], start=True, stop=True)
                        mm.then_inc(s_ps, 1)
                        if g < LAG and live(n - 1, N):
                            products(n - 1, 1 - par, tail[g], tail[g + 1])
                        if g == 4 and live(n - 1, N):
                            tokens(n - 1, 1 - par)
                        if g == LAG:
                            after(pe, v_ready, n + 1)
                            after(pe, z_ready, n - 1)
                        products(n, par, done, fours[g])
                        done = max(done, fours[g])

                tail = [fours[GROUPS - 1]] + [(starts[g] + SIZES[g]) // QC for g in range(GROUPS - LAG, GROUPS)]

                pipelined(pe, N, 2, 0, body)
                for g in range(LAG):
                    pe.wait_ge(p_ready, GROUPS * N - (LAG - 1) + g)
                    products(N - 1, (N - 1) % 2, tail[g], tail[g + 1])
                tokens(N - 1, (N - 1) % 2)


class Kept:
    pass


def build(nc, d, out):
    with ExitStack() as ctx:
        def sb(name, shape, dt=F32):
            return ctx.enter_context(nc.sbuf_tensor(name, shape, dt))

        w = Kept()
        w.mrow_out = ctx.enter_context(nc.semaphore("mrow_out"))
        w.x = sb("x", [P, NT, D])
        w.mix = sb("mix", [P, B, H, TB, HD])
        w.wa = sb("wa", [P, C, 3 * D])
        w.wb = sb("wb", [P, C, 3 * D])
        w.woa = sb("woa", [P, C, D])
        w.wob = sb("wob", [P, C, D])
        w.wf = sb("wf", [P, C, 2 * ZW])
        w.ba = sb("ba", [P, 3 * D])
        w.bb = sb("bb", [P, 3 * D])
        w.boa = sb("boa", [P, D])
        w.bob = sb("bob", [P, D])
        w.bf = sb("bf", [P, 2, ZW])
        w.wqk = sb("wqk", [P, HD])
        w.omega_a = sb("omega_a", [P, NPAIR, P], BF16)
        w.omega_b = sb("omega_b", [P, NPAIR, P], BF16)
        w.ident = sb("ident", [P, P])
        w.identb = sb("identb", [P, P], BF16)
        w.mask = sb("mask", [P, P])
        w.minushalf = sb("minushalf", [P, 2 * H])
        w.minusone = sb("minusone", [P, GT])
        w.three = sb("three", [P, 1])
        w.lneps = sb("lneps", [P, GT])
        w.one = sb("one", [P, 1])
        w.keep = sb("keep", [P, NT])
        w.fnode = sb("fnode", [P, 1])
        w.roots = sb("roots", [P, R])
        w.fweight = sb("fweight", [P, 1])
        w.flo = sb("flo", [P, 1])
        w.fhi = sb("fhi", [P, 1])
        w.fneg = sb("fneg", [P, 1])
        w.fscale = sb("fscale", [P, 1])
        w.flag = sb("flag", [1, 1], I32)
        w.zrow = sb("zrow", [B * H, T], BF16)
        setup(nc, w, d)
        attention_a(nc, w, d)
        project_and_ffn(nc, w, d, "f1", w.woa, w.boa, None)
        prepare_b(nc, w, d)
        score_maxima(nc, w, d)
        attention_b(nc, w, d)
        project_and_ffn(nc, w, d, "f2", w.wob, w.bob, out)


_NAMES = ["L0_attn_a_x", "L0_attn_a_Wqkv", "L0_attn_a_bqkv", "L0_attn_a_Wout", "L0_attn_a_bout", "L0_attn_a_omega",
          "L0_attn_a_quad_nodes", "L0_attn_a_quad_weights", "L0_attn_b_bqkv", "L0_attn_b_bo", "L0_attn_b_wq",
          "L0_attn_b_wk", "L0_ffn_gate_w", "L0_ffn_b0", "L0_ffn_b1"]
_TRANSPOSED = {"attn_b_WqkvT": "L0_attn_b_Wqkv", "attn_b_WoT": "L0_attn_b_Wo", "ffn_w0T": "L0_ffn_w0",
               "ffn_w1T": "L0_ffn_w1"}


def kernel(**inputs):
    import concourse.bacc as bacc
    from concourse.bass_utils import run_bass_kernel_spmd

    nc = bacc.Bacc("TRN2", target_bir_lowering=False, num_devices=1)
    arrays = {name: np.ascontiguousarray(inputs[name]) for name in _NAMES}
    arrays.update({name: np.ascontiguousarray(np.asarray(inputs[src]).T) for name, src in _TRANSPOSED.items()})
    d = {name: nc.dram_tensor(f"in_{name}", a.shape, mybir.dt.from_np(a.dtype), kind="ExternalInput").ap()
         for name, a in arrays.items()}
    d["parts_q"] = nc.dram_tensor("parts_q", (B * H, HROWS, T), BF16, kind="Internal").ap()
    d["parts_k"] = nc.dram_tensor("parts_k", (B * H, HROWS, T), BF16, kind="Internal").ap()
    d["mrow"] = nc.dram_tensor("mrow", (B * H, T), BF16, kind="Internal").ap()
    out = nc.dram_tensor("out", (B, T, D), F32, kind="ExternalOutput").ap()
    build(nc, d, out)
    r = run_bass_kernel_spmd(nc, [{f"in_{name}": a for name, a in arrays.items()}], core_ids=[0])
    return r.results[0]["out"]
```
